# Optimizing a Trainium2 kernel written in Bass

```python
import numpy as np
import jax
import jax.numpy as jnp

def _softmax(x, axis=-1):
    return jax.nn.softmax(x, axis=axis)

def _gelu(x):
    return jax.nn.gelu(x, approximate=True)

def _silu(x):
    return jax.nn.silu(x)

def _sigmoid(x):
    return jax.nn.sigmoid(x)

def _layernorm(x, axis=-1, eps=1e-05):
    m = jnp.mean(x, axis=axis, keepdims=True)
    v = jnp.var(x, axis=axis, keepdims=True)
    return (x - m) / jnp.sqrt(v + eps)

def _scatter_add(tgt, idx, src, axis=0):
    return tgt.at[idx].add(src)

def _segment_sum(src, seg, n):
    return jax.ops.segment_sum(src, seg, n)
kernel_name = 'mk_gnn_preln_d4_gnn_r32_89a29b'

def setup_inputs(seed: int=0):
    np.random.seed(seed)
    _w = jnp.asarray

    def _rec_inputs():
        import jax
        import jax.numpy as jnp
        _gk = jax.random.key(seed)
        x = -0.000202 + 1 * jax.random.normal(jax.random.fold_in(_gk, 1), (50000, 128), jnp.float32)
        src = jax.random.randint(jax.random.fold_in(_gk, 2), (25000,), 0, 50000, jnp.int32)
        dst = jax.random.randint(jax.random.fold_in(_gk, 3), (25000,), 0, 50000, jnp.int32)
        _o = jnp.argsort(dst, stable=True)
        src = src[_o]
        dst = dst[_o]
        edge_type_200 = jax.random.randint(jax.random.fold_in(_gk, 12), (25000,), 0, 200, jnp.int32)
        return (x, src, dst, edge_type_200)
    x, src, dst, edge_type_200 = _rec_inputs()

    def _L0_gnn_setup():
        import jax, jax.numpy as jnp
        import numpy as np
        N = 50000
        E = 18750
        D_IN = 128
        D_H = 128

        def gcn_conv(x, W, b, src, dst, n):
            xw = x @ W
            deg = jnp.ones((n,), x.dtype).at[dst].add(1.0)
            dinv = jax.lax.rsqrt(deg)
            norm = dinv[src] * dinv[dst]
            msg = xw[src] * norm[:, None]
            out = jax.ops.segment_sum(msg, dst, num_segments=n)
            out = out + xw * (dinv * dinv)[:, None]
            return out + b
        key = jax.random.key(seed)
        k1, k2, k3, k4 = jax.random.split(key, 4)
        x = jax.random.normal(k1, (N, D_IN), dtype=jnp.float32)
        edge_index = jax.random.randint(k2, (2, E), 0, N, dtype=jnp.int32)
        W1 = jax.random.normal(k3, (D_IN, D_H), dtype=jnp.float32) * (1.0 / np.sqrt(D_IN))
        b1 = jnp.zeros((D_H,), dtype=jnp.float32)
        W2 = jax.random.normal(k4, (D_H, D_H), dtype=jnp.float32) * (1.0 / np.sqrt(D_H))
        b2 = jnp.zeros((D_H,), dtype=jnp.float32)
        return {'x': x, 'edge_index': edge_index, 'W1': W1, 'b1': b1, 'W2': W2, 'b2': b2}
    _L0_gnn_all = _L0_gnn_setup()
    _L0_gnn_in = {k: v for k, v in _L0_gnn_all.items() if k in ('W1', 'b1', 'W2', 'b2')}
    del _L0_gnn_all

    def _L1_gnn_setup():
        import jax, jax.numpy as jnp
        import numpy as np
        N_NODES = 50000
        D = 128
        N_EDGES = 18750
        key = jax.random.key(seed)
        k_nodes, k_edges, k0, k1, k2 = jax.random.split(key, 5)
        nodes = jax.random.normal(k_nodes, (N_NODES, D), dtype=jnp.float32)
        edges = jax.random.randint(k_edges, (2, N_EDGES), 0, N_NODES, dtype=jnp.int64)
        scale = 1.0 / np.sqrt(D)
        W0 = jax.random.normal(k0, (D, D), dtype=jnp.float32) * scale
        W1 = jax.random.normal(k1, (D, D), dtype=jnp.float32) * scale
        W2 = jax.random.normal(k2, (D, D), dtype=jnp.float32) * scale
        return {'nodes': nodes, 'edges': edges, 'W0': W0, 'W1': W1, 'W2': W2}
    _L1_gnn_all = _L1_gnn_setup()
    _L1_gnn_in = {k: v for k, v in _L1_gnn_all.items() if k in ('W0', 'W1', 'W2')}
    del _L1_gnn_all

    def _L2_gnn_setup():
        import jax, jax.numpy as jnp
        import numpy as np
        N_NODES = 3125
        N_EDGES = 50000
        D = 128
        N_LAYERS = 3
        key = jax.random.key(seed)
        ks = jax.random.split(key, 8)
        X = jax.random.normal(ks[0], (N_NODES, D), dtype=jnp.float32)
        edge_index = jax.random.randint(ks[1], (2, N_EDGES), 0, N_NODES, dtype=jnp.int64)
        eps = jax.random.normal(ks[2], (N_LAYERS,), dtype=jnp.float32)
        W1 = jax.random.normal(ks[3], (N_LAYERS, D, D), dtype=jnp.float32) * (1.0 / np.sqrt(D))
        b1 = jnp.zeros((N_LAYERS, D), dtype=jnp.float32)
        W2 = jax.random.normal(ks[4], (N_LAYERS, D, D), dtype=jnp.float32) * (1.0 / np.sqrt(D))
        b2 = jnp.zeros((N_LAYERS, D), dtype=jnp.float32)
        return {'X': X, 'edge_index': edge_index, 'eps': eps, 'W1': W1, 'b1': b1, 'W2': W2, 'b2': b2}
    _L2_gnn_all = _L2_gnn_setup()
    _L2_gnn_in = {k: v for k, v in _L2_gnn_all.items() if k in ('eps', 'W1', 'b1', 'W2', 'b2')}
    del _L2_gnn_all

    def _L3_gnn_setup():
        import jax, jax.numpy as jnp
        import numpy as np
        N = 50000
        E = 15625
        R = 200
        DIN = 128
        DREL = 128
        DOUT = 128
        SLOPE = 0.01
        key = jax.random.key(seed)
        ks = jax.random.split(key, 6)
        x = jax.random.normal(ks[0], (N, DIN), dtype=jnp.float32)
        relation_embedding = jax.random.normal(ks[1], (R, DREL), dtype=jnp.float32)
        edge_index = jax.random.randint(ks[2], (2, E), 0, N, dtype=jnp.int32)
        edge_type = jax.random.randint(ks[3], (E,), 0, R, dtype=jnp.int32)
        W1 = jax.random.normal(ks[4], (2 * DIN + DREL, DOUT), dtype=jnp.float32) * 0.05
        b1 = jnp.zeros((DOUT,), dtype=jnp.float32)
        w2 = jax.random.normal(ks[5], (DOUT,), dtype=jnp.float32) * 0.05
        return {'x': x, 'relation_embedding': relation_embedding, 'W1': W1, 'b1': b1, 'w2': w2, 'edge_index': edge_index, 'edge_type': edge_type}
    _L3_gnn_all = _L3_gnn_setup()
    _L3_gnn_in = {k: v for k, v in _L3_gnn_all.items() if k in ('relation_embedding', 'W1', 'b1', 'w2')}
    del _L3_gnn_all
    return {'x': x, 'src': src, 'dst': dst, 'edge_type_200': edge_type_200, 'L0_gnn_W1': _L0_gnn_in['W1'], 'L0_gnn_b1': _L0_gnn_in['b1'], 'L0_gnn_W2': _L0_gnn_in['W2'], 'L0_gnn_b2': _L0_gnn_in['b2'], 'L1_gnn_W0': _L1_gnn_in['W0'], 'L1_gnn_W1': _L1_gnn_in['W1'], 'L1_gnn_W2': _L1_gnn_in['W2'], 'L2_gnn_eps': _L2_gnn_in['eps'], 'L2_gnn_W1': _L2_gnn_in['W1'], 'L2_gnn_b1': _L2_gnn_in['b1'], 'L2_gnn_W2': _L2_gnn_in['W2'], 'L2_gnn_b2': _L2_gnn_in['b2'], 'L3_gnn_relation_embedding': _L3_gnn_in['relation_embedding'], 'L3_gnn_W1': _L3_gnn_in['W1'], 'L3_gnn_b1': _L3_gnn_in['b1'], 'L3_gnn_w2': _L3_gnn_in['w2']}

def reference(x, src, dst, edge_type_200, L0_gnn_W1, L0_gnn_b1, L0_gnn_W2, L0_gnn_b2, L1_gnn_W0, L1_gnn_W1, L1_gnn_W2, L2_gnn_eps, L2_gnn_W1, L2_gnn_b1, L2_gnn_W2, L2_gnn_b2, L3_gnn_relation_embedding, L3_gnn_W1, L3_gnn_b1, L3_gnn_w2):
    import jax
    import jax.numpy as jnp

    def _L0_gnn_ref(x, edge_index, W1, b1, W2, b2):
        import jax, jax.numpy as jnp
        import numpy as np
        N = 50000
        E = 18750
        D_IN = 128
        D_H = 128

        def gcn_conv(x, W, b, src, dst, n):
            xw = x @ W
            deg = jnp.ones((n,), x.dtype).at[dst].add(1.0)
            dinv = jax.lax.rsqrt(deg)
            norm = dinv[src] * dinv[dst]
            msg = xw[src] * norm[:, None]
            out = jax.ops.segment_sum(msg, dst, num_segments=n)
            out = out + xw * (dinv * dinv)[:, None]
            return out + b
        src, dst = (edge_index[0], edge_index[1])
        n = x.shape[0]
        h = jax.nn.relu(gcn_conv(x, W1, b1, src, dst, n))
        h = jax.nn.relu(gcn_conv(h, W2, b2, src, dst, n))
        return h

    def _L1_gnn_ref(nodes, edges, W0, W1, W2):
        import jax, jax.numpy as jnp
        import numpy as np
        N_NODES = 50000
        D = 128
        N_EDGES = 18750
        n = nodes.shape[0]
        src, dst = (edges[0], edges[1])
        m_fwd = nodes[src] @ W1.T
        m_bwd = nodes[dst] @ W2.T
        msg_cat = jnp.concatenate([m_fwd, m_bwd], axis=0)
        idx = jnp.concatenate([dst, src], axis=0)
        seg_sum = jax.ops.segment_sum(msg_cat, idx, num_segments=n)
        seg_cnt = jax.ops.segment_sum(jnp.ones((idx.shape[0], 1), dtype=nodes.dtype), idx, num_segments=n)
        msg = jnp.where(seg_cnt > 0, seg_sum / jnp.maximum(seg_cnt, 1), 0.0)
        return jax.nn.relu(nodes @ W0.T + msg)

    def _L2_gnn_ref(X, edge_index, eps, W1, b1, W2, b2):
        import jax, jax.numpy as jnp
        import numpy as np
        N_NODES = 3125
        N_EDGES = 50000
        D = 128
        N_LAYERS = 3
        src = edge_index[0]
        dst = edge_index[1]
        n = X.shape[0]
        n_layers = eps.shape[0]
        for l in range(n_layers):
            S = jax.ops.segment_sum(X[src], dst, num_segments=n)
            Z = (1.0 + eps[l]) * X + S
            H = jax.nn.relu(Z @ W1[l] + b1[l])
            X = H @ W2[l] + b2[l]
        return X

    def _L3_gnn_ref(x, relation_embedding, W1, b1, w2, edge_index, edge_type):
        import jax, jax.numpy as jnp
        import numpy as np
        N = 50000
        E = 15625
        R = 200
        DIN = 128
        DREL = 128
        DOUT = 128
        SLOPE = 0.01
        src, dst = (edge_index[0], edge_index[1])
        n = x.shape[0]
        triple = jnp.concatenate([x[src], x[dst], relation_embedding[edge_type]], axis=1)
        c = triple @ W1 + b1
        b = jax.nn.leaky_relu(c @ w2, SLOPE)
        seg_max = jax.ops.segment_max(b, dst, num_segments=n)
        ex = jnp.exp(b - seg_max[dst])
        denom = jax.ops.segment_sum(ex, dst, num_segments=n)
        alpha = ex / denom[dst]
        out = jax.ops.segment_sum(c * alpha[:, None], dst, num_segments=n)
        return jax.nn.leaky_relu(out, SLOPE)
    edge_index = jnp.stack([src, dst])
    h = jnp.maximum(_layernorm(x, axis=-1), 0.0)
    x = x + _L0_gnn_ref(h, edge_index, L0_gnn_W1, L0_gnn_b1, L0_gnn_W2, L0_gnn_b2)
    h = jnp.maximum(_layernorm(x, axis=-1), 0.0)
    x = x + _L1_gnn_ref(h, edge_index, L1_gnn_W0, L1_gnn_W1, L1_gnn_W2)
    h = jnp.maximum(_layernorm(x, axis=-1), 0.0)
    x = x + _L2_gnn_ref(h, edge_index, L2_gnn_eps, L2_gnn_W1, L2_gnn_b1, L2_gnn_W2, L2_gnn_b2)
    h = jnp.maximum(_layernorm(x, axis=-1), 0.0)
    x = x + _L3_gnn_ref(h, L3_gnn_relation_embedding, L3_gnn_W1, L3_gnn_b1, L3_gnn_w2, edge_index, edge_type_200)
    return x

_drawn_inputs = setup_inputs


def setup_inputs(seed=0):
    import zlib

    import numpy as np

    out = dict(_drawn_inputs(seed))
    spreads = {'L0_gnn_b1': (0.0, 0.1),
     'L0_gnn_b2': (0.0, 0.1),
     'L2_gnn_b1': (0.0, 0.1),
     'L2_gnn_b2': (0.0, 0.1),
     'L3_gnn_b1': (0.0, 0.522)}
    factors = {'L3_gnn_w2': 8.0}
    for name, (base, spread) in spreads.items():
        noise = np.random.default_rng([zlib.crc32(name.encode()), seed]).standard_normal(out[name].shape)
        drawn = base * np.exp(spread * noise) if base else spread * noise
        out[name] = jnp.asarray(drawn.astype(out[name].dtype))
    for name, factor in factors.items():
        out[name] = (out[name] * factor).astype(out[name].dtype)
    return out
```

```python
import concourse.bass as bass
from concourse import mybir
from contextlib import ExitStack

fp32 = mybir.dt.float32
bf16 = mybir.dt.bfloat16
i32 = mybir.dt.int32
ALU = mybir.AluOpType
ACT = mybir.ActivationFunctionType

P = 128
N = 50000
E = 25000
R = 200
G = 8
BLOCK = P * G
STEPS = -(-N // BLOCK)
NP = STEPS * BLOCK
COLS = NP // P
TAIL = (N - (STEPS - 1) * BLOCK) // G
CUT = 96
TILES = -(-E // P)
LAST = E - (TILES - 1) * P
ES = 7
ROUNDS = TILES // ES
DS = 4
TURNS = (STEPS - 1) // DS
assert ROUNDS * ES == TILES and TURNS * DS == STEPS - 1 and TAIL * G == N - (STEPS - 1) * BLOCK
FAR = 1.0e5
BIG = 1.0e30
EPS = 1e-5
SLOPE = 0.01


class Chain:

    def __init__(self, sem):
        self.sem, self.base, self.per, self.count, self.round = sem, 0, 0, 0, 0

    def loop(self, turn, links):
        self.round, self.per, self.count = turn, links, 0

    def end(self, rounds):
        assert self.count == self.per, (self.count, self.per)
        self.base += self.per * rounds
        self.round, self.per, self.count = 0, 0, 0

    def link(self, engine, ins):
        self.count += 1
        ins.then_inc(self.sem, 1)
        engine.wait_ge(self.sem, self.round * self.per + (self.base + self.count))

    def settle(self):
        self.base, self.count = self.base + self.count, 0


class Signal:

    def __init__(self, sem, per=1, base=0):
        self.sem, self.per, self.base = sem, per, base

    def after(self, step):
        return self.base + self.per * (step + 1)

    def close(self, steps):
        self.base += self.per * steps


def gnn_kernel(nc, x, src, dst, edge_type, a_W1, a_b1, a_W2, a_b2, m_W0, m_W1, m_W2,
               g_eps, g_W1, g_b1, g_W2, g_b2, r_emb, r_W1, r_b1, r_w2, out):
    def scratch(name, shape):
        return nc.dram_tensor(name, shape, fp32, kind="Internal").ap()

    table_a, table_b = scratch("table_a", [NP, P]), scratch("table_b", [NP, P])
    xs = scratch("xs", [NP, P])
    agg = scratch("agg", [NP, P])
    agg_back = scratch("agg_back", [NP + P, P])
    c_rows = scratch("c_rows", [TILES * P, P])
    rows_of = {n: scratch(f"{n}_rows", [2 * P, P]) for n in ("dst", "src", "type")}

    def row_of(name, tile):
        flat = rows_of[name].rearrange("t e -> (t e)")
        return flat[bass.ds(tile * P, P)].partition_broadcast(P)

    ctx = ExitStack()
    with ctx:
        def sb(name, shape, dt=fp32):
            return ctx.enter_context(nc.sbuf_tensor(name, shape, dt))

        def sig(name, per=1, base=0):
            return Signal(ctx.enter_context(nc.semaphore(name)), per, base)

        def sigs(name, n, base=0):
            return [sig(f"{name}{k}", 16, base) for k in range(n)]

        wide = [ctx.enter_context(nc.psum_tensor(f"wide{k}", [P, BLOCK], fp32)) for k in range(4)]
        banks = [wide[k // 2][:, (k % 2) * 512:(k % 2) * 512 + 512] for k in range(8)]
        ident = sb("ident", [P, P])
        ones = sb("ones", [P, P])
        lower = sb("lower", [P, P])
        pick_last = sb("pick_last", [P, P])
        pick_first = sb("pick_first", [P, P])
        flip = sb("flip", [P, 2, TILES])
        iota_p = sb("iota_p", [P, P])
        iota_c = sb("iota_c", [P, COLS])
        part = sb("part", [P, 2])
        is_127 = sb("is_127", [P, 1])
        weights = sb("weights", [P, 16, P])
        (W_A1, W_A2, W_M0, W_M1, W_M2, W_G1, W_G2, W_RS, W_RD, W_RR) = (0, 1, 2, 3, 4, 5, 8, 11, 12, 13)
        raw = sb("raw", [P, 5, P])
        rel_rows = sb("rel_rows", [P, 2, P])
        rel_T = sb("rel_T", [P, 2, P])
        bias = sb("bias", [P, 7, P])
        gin_bias = sb("gin_bias", [P, 3])
        gin_scale = sb("gin_scale", [P, 3])
        D_, S_, T_, X_ = range(4)
        col = sb("col", [P, 4, 2 * P])
        dst_flip = sb("dst_flip", [P, TILES])
        idx = sb("idx", [P, 3, TILES], i32)
        prev_last = sb("prev_last", [P, TILES + 1])
        back_off = sb("back_off", [P, TILES])
        dump = sb("dump", [P, 1])
        node_i = sb("node_i", [P, 3, TILES], i32)
        node_at = sb("node_at", [P, 4, TILES])
        degree = sb("degree", [P, 2, COLS])
        dinv = sb("dinv", [P, COLS])
        rcount = sb("rcount", [P, COLS])
        score = sb("score", [P, TILES])
        top = sb("top", [P, 2, TILES])
        edges = sb("edges", [P, 2, TILES])
        pen = sb("pen", [P, 4, TILES])
        carry = sb("carry", [P, 2, TILES + 1])
        seg_top = sb("seg_top", [P, 2, TILES])
        d_last = sb("d_last", [P, 2, TILES])

        carrier = sig("carrier")
        s_ld, s_set, s_v, s_pe, s_act = (sig(n) for n in ("s_ld", "s_set", "s_v", "s_pe", "s_act"))
        chain = Chain(ctx.enter_context(nc.semaphore("dve_chain")))

        msg = sb("msg", [P, ES, P + 4])
        row_ids = sb("row_ids", [P, ES, P])
        same = sb("same", [P, ES, P])
        from_last = sb("from_last", [P, ES, P])
        sums = sb("sums", [P, ES, P + 4])
        norm = sb("norm", [P, ES, P])
        slot_g = sb("slot_g", [P, ES], i32)
        slot_s = sb("slot_s", [P, ES], i32)
        slot_h = sb("slot_h", [P, ES], i32)
        small = sb("small", [P, ES, 8])
        primer = sb("primer", [P, 4 * ES], i32)
        gathered = sigs("gathered", ES, 16)
        scattered = sigs("scattered", ES, 16)
        ids_in = sigs("ids_in", ES)
        c_stored = sigs("c_stored", ES, 16)
        c_loaded = sigs("c_loaded", ES)
        masks = sig("masks", 1, ES)
        index_in = sig("index_in")
        scatter_in = sig("scatter_in")
        summed = sig("summed", 1, ES)
        ends_in = sig("ends_in", 1, ES)
        top_in = sig("top_in", 1, ES)
        spread_in = sig("spread_in", 1, ES)
        ex_in = sig("ex_in", 1, ES)
        c_in = sig("c_in", 1, ES)
        kept = sig("kept", 1, 1)

        sh = [P, DS, G, P]
        in_a, in_b, in_c, in_x, node_y, node_h = (sb("t_" + n, sh) for n in ("in_a", "in_b", "in_c", "in_x", "node_y", "node_h"))
        feat = [sb(f"feat{k}", [P, BLOCK]) for k in range(6)]
        stats = sb("stats", [P, DS, G, 6])
        moments = sb("moments", [P, DS, G, 2])
        scale = sb("scale", [P, DS, 2, G])
        loaded = sigs("loaded", DS)
        stored = sigs("stored", DS, 16)
        own_in = sig("own_in")
        pre_done = sig("pre_done")
        turned = sig("turned")
        copied = sig("copied", 1, 2)
        product = sig("product", 1, 2)
        freed = sig("freed", 1, 2)
        var_in = sig("var_in")
        root_in = sig("root_in")
        scale_in = sig("scale_in")
        normed = sig("normed")

        def own_instruction(eng):
            eng.sem_inc(carrier.sem, 1)

        with ExitStack() as stage:
            def view(tile, dt, *shape):
                flat = tile[:, :, :, :].rearrange("p s g f -> p (s g f)")
                names = "abcd"[:len(shape)]
                size = 1
                for n in shape:
                    size *= n
                sizes = {n: z for n, z in zip(names, shape)}
                flat = flat[:, 0:size // (2 if dt == bf16 else 1)]
                flat = flat if dt == fp32 else flat.bitcast(dt)
                return flat.rearrange(f"p ({' '.join(names)}) -> p {' '.join(names)}", **sizes)

            oh_p = view(in_a, bf16, ES, 2, P)
            oh_c = view(in_b, bf16, ES, 2, COLS)
            edge_i = view(in_c, i32, 4, 2 * P)
            edge_f = view(node_h, fp32, 4, 2 * P)
            zeros = view(node_y, fp32, DS * G * P)
            zero_b = stage.enter_context(nc.sbuf_tensor("zero_b", [P, COLS], bf16))
            zeroed = sig("zeroed", 16)
            onehot = sig("onehot")
            counted = sig("counted", 1, ES)
            rows_out = sig("rows_out", 16)
            block = stage.enter_context(nc.Block())
            n_ld = [0]

            @block.sync
            def _(sp):
                def load(tile, source):
                    sp.dma_start(tile, source).then_inc(s_ld.sem, 16)
                    n_ld[0] += 1
                sp.wait_ge(s_set.sem, 1)
                for k, a in ((D_, dst), (S_, src), (T_, edge_type)):
                    load(edge_i[:, k, 0:P], a[0:P * P].rearrange("(t e) -> t e", e=P))
                    load(edge_i[0:TILES - 1 - P, k, P:2 * P], a[P * P:(TILES - 1) * P].rearrange("(t e) -> t e", e=P))
                    load(edge_i[TILES - 1 - P:TILES - P, k, P:P + LAST], a[(TILES - 1) * P:E].rearrange("(t e) -> t e", t=1))
                load(edge_i[:, X_, 0:P], dst[1:P * P + 1].rearrange("(t e) -> t e", e=P))
                load(edge_i[0:TILES - 1 - P, X_, P:2 * P], dst[P * P + 1:(TILES - 1) * P + 1].rearrange("(t e) -> t e", e=P))
                load(edge_i[TILES - 1 - P:TILES - P, X_, P:P + LAST - 1], dst[(TILES - 1) * P + 1:E].rearrange("(t e) -> t e", t=1))
                load(weights[:, W_A1, :], a_W1)
                load(weights[:, W_A2, :], a_W2)
                load(weights[:, W_G1:W_G1 + 3, :], g_W1.rearrange("l i o -> i l o"))
                load(weights[:, W_G2:W_G2 + 3, :], g_W2.rearrange("l i o -> i l o"))
                load(weights[:, W_RS:W_RR + 1, :], r_W1.rearrange("(k i) o -> i k o", k=3))
                for k, w in enumerate((m_W0, m_W1, m_W2)):
                    load(raw[:, k, :], w)
                load(raw[:, 3, :], r_emb[0:P, :])
                load(raw[0:R - P, 4, :], r_emb[P:R, :])
                for k, b in enumerate((a_b1, a_b2, g_b2[0, :], g_b2[1, :], g_b2[2, :], r_b1, r_w2)):
                    load(bias[:, k, :], b.partition_broadcast(P))
                with nc.allow_non_contiguous_dma(reason="384 values"):
                    load(gin_bias[:, :], g_b1.rearrange("l f -> f l"))
                load(gin_scale[:, :], g_eps.partition_broadcast(P))
                sp.wait_ge(s_v.sem, 1)
                for k, n in ((D_, "dst"), (S_, "src"), (T_, "type")):
                    sp.dma_start(rows_of[n].rearrange("(c t) e -> t c e", c=2),
                                 edge_f[:, k, :].rearrange("t (c e) -> t c e", c=2)).then_inc(rows_out.sem, 16)
                sp.wait_ge(s_set.sem, 2)
                for a, rows in ((agg, NP), (agg_back, NP + P)):
                    done = 0
                    while done < rows:
                        n = min(4096, rows - done)
                        sp.dma_start(a[done:done + n, :].rearrange("(p r) f -> p (r f)", p=P),
                                     zeros[:, 0:n]).then_inc(zeroed.sem, 16)
                        done += n
                        zeroed.base += 16
                sp.wait_ge(rows_out.sem, 48)
                sp.wait_ge(zeroed.sem, zeroed.base)

            def prime(eng, group, at):
                for k, s in enumerate(group):
                    eng.dma_start(primer[:, at + k:at + k + 1],
                                  edge_type[0:P].rearrange("(p a) -> p a", a=1)).then_inc(s.sem, 16)
                for s in group:
                    eng.wait_ge(s.sem, 16)

            @block.gpsimd
            def _(pool):
                done = [0]

                def link(ins):
                    done[0] += 1
                    ins.then_inc(s_act.sem, 1)
                    pool.wait_ge(s_act.sem, done[0])
                link(pool.memset(edge_i[:, :, :], N))
                link(pool.memset(edge_i[:, T_, :], 0))
                pool.memset(raw[:, 4, :], 0.0).then_inc(s_set.sem, 1)
                pool.memset(zeros[:, :], 0.0).then_inc(s_set.sem, 1)
                pool.memset(ones[:, :], 1.0)
                pool.memset(ident[:, :], 0.0)
                pool.memset(lower[:, :], 1.0)
                pool.memset(flip[:, :, :], 0.0)
                link(pool.memset(is_127[:, :], 0.0))
                link(pool.affine_select(out=ident[:, :], in_=ident[:, :], compare_op=ALU.not_equal, fill=1.0, base=0,
                                        pattern=[[-1, P]], channel_multiplier=1))
                link(pool.affine_select(out=is_127[:, :], in_=is_127[:, :], compare_op=ALU.not_equal, fill=1.0,
                                        base=1 - P, pattern=[[0, 1]], channel_multiplier=1))
                link(pool.affine_select(out=lower[:, :], in_=lower[:, :], compare_op=ALU.is_gt, fill=0.0, base=0,
                                        pattern=[[-1, P]], channel_multiplier=1))
                link(pool.affine_select(out=pick_first[:, :], in_=ones[:, :], compare_op=ALU.is_equal, fill=0.0, base=0,
                                        pattern=[[0, P]], channel_multiplier=1))
                link(pool.affine_select(out=pick_last[:, :], in_=ones[:, :], compare_op=ALU.is_equal, fill=0.0,
                                        base=1 - P, pattern=[[0, P]], channel_multiplier=1))
                for c in range(2):
                    link(pool.affine_select(out=flip[:, c, :], in_=flip[:, c, :], compare_op=ALU.not_equal, fill=1.0,
                                            base=c * P - (TILES - 1), pattern=[[1, TILES]], channel_multiplier=1))
                any_dt = dict(allow_small_or_imprecise_dtypes=True)
                pool.iota(iota_p[:, :], pattern=[[1, P]], base=0, channel_multiplier=0, **any_dt)
                pool.iota(iota_c[:, :], pattern=[[1, COLS]], base=0, channel_multiplier=0, **any_dt)
                pool.iota(part[:, :], pattern=[[P, 2]], base=0, channel_multiplier=1, **any_dt)
                pool.iota(dump[:, :], pattern=[[0, 1]], base=NP, channel_multiplier=1, **any_dt)
                link(pool.memset(zero_b[:, :], 0.0))
                pool.sem_inc(s_set.sem, 1)
                prime(pool, gathered + scattered + stored, 0)

            @block.tensor
            def _(pe):
                pe.sem_inc(counted.sem, ES)
                pe.sem_inc(summed.sem, ES)
                pe.sem_inc(product.sem, 2)
                pe.sem_inc(c_in.sem, ES)
                pe.wait_ge(s_set.sem, 3)
                pe.wait_ge(s_v.sem, 1)
                for k in range(4):
                    for c in range(2):
                        nc.tensor.transpose(banks[k // 2][:, (k % 2) * 256 + c * P:(k % 2) * 256 + c * P + P],
                                            edge_f[:, k, c * P:c * P + P], ident[:, :])
                for c in range(2):
                    last = nc.tensor.matmul(banks[2][:, 0:TILES], edge_f[:, D_, c * P:c * P + P], flip[:, c, :],
                                            start=c == 0, stop=c == 1)
                last.then_inc(s_pe.sem, 1)
                pe.wait_ge(s_ld.sem, 16 * n_ld[0])
                for k in range(4):
                    nc.tensor.transpose(wide[2][:, k * P:k * P + P], raw[:, k, :], ident[:, :])
                nc.tensor.transpose(wide[2][:, 512:512 + P], raw[:, 4, :], ident[:, :]).then_inc(s_pe.sem, 1)
                pe.wait_ge(s_v.sem, 3)
                for c in range(2):
                    last = nc.tensor.matmul(wide[3][:, c * P:c * P + P], rel_T[:, c, :], weights[:, W_RR, :],
                                            start=True, stop=True)
                last.then_inc(s_pe.sem, 1)
                for k in range(2):
                    nc.tensor.matmul(banks[k][:, 0:COLS], zero_b[:, 0:P], zero_b[:, :], start=True, stop=False)
                with pe.Fori(0, ROUNDS) as r:
                    for k in range(ES):
                        pe.wait_ge(onehot.sem, onehot.after(r * ES + k))
                        nc.tensor.matmul(banks[0][:, 0:COLS], oh_p[:, k, 0, :], oh_c[:, k, 0, :], start=False, stop=False)
                        nc.tensor.matmul(banks[1][:, 0:COLS], oh_p[:, k, 1, :], oh_c[:, k, 1, :], start=False, stop=False)\
                            .then_inc(counted.sem, 1)
                nc.tensor.matmul(banks[0][:, 0:COLS], zero_b[:, 0:P], zero_b[:, :], start=False, stop=True)
                nc.tensor.matmul(banks[1][:, 0:COLS], zero_b[:, 0:P], zero_b[:, :], start=False, stop=True)\
                    .then_inc(s_pe.sem, 1)

            @block.scalar
            def _(act):
                prime(act, c_stored, 3 * ES)
                act.sem_inc(copied.sem, 2)
                act.sem_inc(ends_in.sem, ES)
                act.sem_inc(ex_in.sem, ES)
                act.wait_ge(s_v.sem, 4)
                nc.scalar.activation(dinv[:, :], dinv[:, :], ACT.Sqrt).then_inc(s_v.sem, 1)

            @block.vector
            def _(dve):
                v = nc.vector

                def link(ins):
                    chain.link(dve, ins)

                v.memset(sums[:, :, :], 0.0).then_inc(kept.sem, 1)
                dve.sem_inc(masks.sem, ES)
                dve.sem_inc(freed.sem, 2)
                dve.sem_inc(top_in.sem, ES)
                dve.sem_inc(spread_in.sem, ES)
                dve.wait_ge(s_set.sem, 3)
                dve.wait_ge(s_ld.sem, 16 * 12)
                dve.wait_ge(s_ld.sem, 16 * n_ld[0])
                v.tensor_copy(edge_f[:, :, :], edge_i[:, :, :]).then_inc(s_v.sem, 1)
                link(v.tensor_scalar(gin_scale[:, :], gin_scale[:, :], 1.0, None, ALU.add))
                dve.wait_ge(s_pe.sem, 1)
                v.tensor_copy(col[:, 0:2, :], banks[0].rearrange("p (k t) -> p k t", k=2))
                v.tensor_copy(col[:, 2:4, :], banks[1].rearrange("p (k t) -> p k t", k=2))
                link(v.tensor_copy(dst_flip[:, :], banks[2][:, 0:TILES]))
                v.tensor_copy(idx[:, 0, :], col[:, S_, 0:TILES])
                v.tensor_copy(idx[:, 1, :], col[:, D_, 0:TILES])
                link(v.tensor_tensor(score[:, :], col[:, D_, 0:TILES], col[:, X_, 0:TILES], ALU.is_equal))
                v.scalar_tensor_tensor(out=idx[:, 2, :], in0=score[:, :], scalar=FAR, in1=col[:, D_, 0:TILES],
                                       op0=ALU.mult, op1=ALU.add)
                link(v.memset(prev_last[:, :], -1.0))
                v.tensor_scalar(prev_last[:, 1:TILES + 1], col[:, D_, 0:TILES], 1.0, is_127[:, 0:1], ALU.add, ALU.mult)
                link(v.tensor_scalar(back_off[:, :], col[:, S_, 0:TILES], dump[:, 0:1], None, ALU.subtract))
                link(v.tensor_scalar(prev_last[:, 1:TILES + 1], prev_last[:, 1:TILES + 1], -1.0, None, ALU.add))
                for k in range(2):
                    n_i = idx[:, 1 - k, :]
                    v.tensor_scalar(node_i[:, 0, :], n_i, 3, P - 1, ALU.logical_shift_right, ALU.bitwise_and)
                    v.tensor_scalar(node_i[:, 1, :], n_i, 10, 3, ALU.logical_shift_right, ALU.logical_shift_left)
                    link(v.tensor_scalar(node_i[:, 2, :], n_i, G - 1, None, ALU.bitwise_and))
                    v.tensor_copy(node_at[:, 2 * k, :], node_i[:, 0, :])
                    link(v.tensor_tensor(node_at[:, 2 * k + 1, :], node_i[:, 1, :], node_i[:, 2, :], ALU.add))
                dve.wait_ge(s_pe.sem, 2)
                v.tensor_copy(weights[:, W_M0:W_M2 + 1, :], wide[2][:, 0:3 * P].rearrange("p (k f) -> p k f", k=3))\
                    .then_inc(s_v.sem, 1)
                v.tensor_copy(rel_T[:, :, :], wide[2][:, 3 * P:5 * P].rearrange("p (k f) -> p k f", k=2))\
                    .then_inc(s_v.sem, 1)
                dve.wait_ge(s_pe.sem, 3)
                for c in range(2):
                    link(v.tensor_tensor(rel_rows[:, c, :], wide[3][:, c * P:c * P + P], bias[:, 5, :], ALU.add))
                chain.settle()
                with dve.Fori(0, ROUNDS) as r:
                    for k in range(ES):
                        t = r * ES + k
                        dve.wait_ge(counted.sem, counted.after(t - ES))
                        for w in range(2):
                            v.tensor_scalar(oh_p[:, k, w, :], iota_p[:, :], node_at[:, 2 * w, bass.ds(t, 1)], None,
                                            ALU.is_equal)
                            last = v.tensor_scalar(oh_c[:, k, w, :], iota_c[:, :],
                                                   node_at[:, 2 * w + 1, bass.ds(t, 1)], None, ALU.is_equal)
                        last.then_inc(onehot.sem, 1)
                dve.wait_ge(s_pe.sem, 4)
                v.tensor_copy(degree[:, 0, :], banks[0][:, 0:COLS])
                link(v.tensor_copy(degree[:, 1, :], banks[1][:, 0:COLS]))
                v.tensor_scalar(dinv[:, :], degree[:, 0, :], 1.0, None, ALU.add).then_inc(s_v.sem, 1)
                link(v.tensor_tensor(rcount[:, :], degree[:, 0, :], degree[:, 1, :], ALU.add))
                link(v.tensor_scalar(rcount[:, :], rcount[:, :], 1.0, None, ALU.max))
                link(v.reciprocal(rcount[:, :], rcount[:, :]))
                dve.wait_ge(s_v.sem, 5)
                link(v.reciprocal(dinv[:, :], dinv[:, :]))
                chain.settle()

        def edge_close():
            for group in (gathered, scattered, ids_in):
                for s in group:
                    s.close(ROUNDS)
            for s in (masks, index_in, scatter_in, summed, kept):
                s.close(TILES)

        def sum_into_dst(table):
            with nc.Block() as block:
                @block.sync
                def _(sp):
                    with sp.Fori(0, ROUNDS) as r:
                        for k in range(ES):
                            t = r * ES + k
                            sp.wait_ge(masks.sem, masks.after(t - ES))
                            sp.dma_start(row_ids[:, k, :], row_of("dst", t))\
                                .then_inc(ids_in[k].sem, 16)

                @block.vector
                def _(dve):
                    v = nc.vector
                    with dve.Fori(0, ROUNDS) as r:
                        for k in range(ES):
                            t = r * ES + k
                            dve.wait_ge(gathered[k].sem, gathered[k].base + 16 * r)
                            v.tensor_copy(slot_g[:, k:k + 1], idx[:, 0, bass.ds(t, 1)]).then_inc(index_in.sem, 1)
                            dve.wait_ge(ids_in[k].sem, ids_in[k].after(0) + 16 * r)
                            dve.wait_ge(summed.sem, summed.after(t - ES))
                            v.tensor_scalar(same[:, k, :], row_ids[:, k, :], col[:, D_, bass.ds(t, 1)], None, ALU.is_equal)
                            v.tensor_scalar(from_last[:, k, :], row_ids[:, k, :], prev_last[:, bass.ds(t, 1)], None,
                                            ALU.is_equal).then_inc(masks.sem, 1)
                            dve.wait_ge(scattered[k].sem, scattered[k].base + 16 * r)
                            v.tensor_copy(slot_s[:, k:k + 1], idx[:, 2, bass.ds(t, 1)]).then_inc(scatter_in.sem, 1)

                @block.tensor
                def _(pe):
                    with pe.Fori(0, ROUNDS) as r:
                        for k in range(ES):
                            t = r * ES + k
                            pe.wait_ge(gathered[k].sem, gathered[k].after(0) + 16 * r)
                            pe.wait_ge(masks.sem, masks.after(t))
                            nc.tensor.matmul(banks[k][:, 0:P], same[:, k, :], msg[:, k, 0:P], start=True, stop=False)
                            pe.wait_ge(kept.sem, kept.after(t - 1))
                            nc.tensor.matmul(banks[k][:, 0:P], from_last[:, k, :], sums[:, (k - 1) % ES, 0:P],
                                             start=False, stop=True).then_inc(summed.sem, 1)

                @block.scalar
                def _(act):
                    with act.Fori(0, ROUNDS) as r:
                        for k in range(ES):
                            t = r * ES + k
                            act.wait_ge(scattered[k].sem, scattered[k].base + 16 * r)
                            act.wait_ge(summed.sem, summed.after(t))
                            nc.scalar.activation(sums[:, k, 0:P], banks[k][:, 0:P], ACT.Copy).then_inc(kept.sem, 1)

                @block.gpsimd
                def _(pool):
                    def gather(r, k):
                        pool.wait_ge(index_in.sem, index_in.after(r * ES + k))
                        pool.wait_ge(summed.sem, summed.after(r * ES + k - ES))
                        own_instruction(pool)
                        pool.indirect_dma_start(out=msg[:, k, 0:P], out_offset=None, in_=table,
                                                in_offset=bass.IndirectOffsetOnAxis(ap=slot_g[:, k:k + 1], axis=0))\
                            .then_inc(gathered[k].sem, 16)

                    def scatter(r, k):
                        pool.wait_ge(kept.sem, kept.after(r * ES + k))
                        pool.wait_ge(scatter_in.sem, scatter_in.after(r * ES + k))
                        own_instruction(pool)
                        pool.indirect_dma_start(out=agg, in_=sums[:, k, 0:P], in_offset=None, bounds_check=NP - 1,
                                                oob_is_err=False,
                                                out_offset=bass.IndirectOffsetOnAxis(ap=slot_s[:, k:k + 1], axis=0))\
                            .then_inc(scattered[k].sem, 16)

                    for k in range(ES):
                        gather(0, k)
                    with pool.Fori(1, ROUNDS) as r:
                        for k in range(ES):
                            scatter(r - 1, k)
                            gather(r, k)
                    for k in range(ES):
                        scatter(ROUNDS - 1, k)
                    for k in range(ES):
                        pool.wait_ge(scattered[k].sem, scattered[k].base + 16 * ROUNDS)
            edge_close()

        def sum_into_src(table):
            with nc.Block() as block:
                @block.sync
                def _(sp):
                    with sp.Fori(0, ROUNDS) as r:
                        for k in range(ES):
                            t = r * ES + k
                            sp.wait_ge(masks.sem, masks.after(t - ES))
                            sp.dma_start(row_ids[:, k, :], row_of("src", t)).then_inc(ids_in[k].sem, 16)

                @block.vector
                def _(dve):
                    v = nc.vector
                    with dve.Fori(0, ROUNDS) as r:
                        chain.loop(r, 3 * ES)
                        for k in range(ES):
                            t = r * ES + k
                            dve.wait_ge(gathered[k].sem, gathered[k].base + 16 * r)
                            v.tensor_copy(slot_g[:, k:k + 1], idx[:, 1, bass.ds(t, 1)]).then_inc(index_in.sem, 1)
                            dve.wait_ge(ids_in[k].sem, ids_in[k].after(0) + 16 * r)
                            dve.wait_ge(summed.sem, summed.after(t - ES))
                            chain.link(dve, v.tensor_scalar(same[:, k, :], row_ids[:, k, :], col[:, S_, bass.ds(t, 1)],
                                                            None, ALU.is_equal))
                            chain.link(dve, v.tensor_tensor_reduce(out=from_last[:, k, :], in0=same[:, k, :],
                                                                   in1=lower[:, :], scale=1.0, scalar=0.0,
                                                                   op0=ALU.mult, op1=ALU.add,
                                                                   accum_out=small[:, k, 0:1]))
                            v.sem_inc(masks.sem, 1)
                            chain.link(dve, v.tensor_scalar(small[:, k, 1:2], small[:, k, 0:1], 0.0,
                                                            back_off[:, bass.ds(t, 1)], ALU.is_equal, ALU.mult))
                            dve.wait_ge(scattered[k].sem, scattered[k].base + 16 * r)
                            v.tensor_scalar(slot_s[:, k:k + 1], small[:, k, 1:2], dump[:, 0:1], None, ALU.add)\
                                .then_inc(scatter_in.sem, 1)
                    chain.end(ROUNDS)

                @block.tensor
                def _(pe):
                    with pe.Fori(0, ROUNDS) as r:
                        for k in range(ES):
                            t = r * ES + k
                            pe.wait_ge(gathered[k].sem, gathered[k].after(0) + 16 * r)
                            pe.wait_ge(masks.sem, masks.after(t))
                            pe.wait_ge(kept.sem, kept.after(t - ES))
                            nc.tensor.matmul(banks[k][:, 0:P], same[:, k, :], msg[:, k, 0:P], start=True, stop=True)\
                                .then_inc(summed.sem, 1)

                @block.scalar
                def _(act):
                    with act.Fori(0, ROUNDS) as r:
                        for k in range(ES):
                            t = r * ES + k
                            act.wait_ge(scattered[k].sem, scattered[k].base + 16 * r)
                            act.wait_ge(summed.sem, summed.after(t))
                            nc.scalar.activation(sums[:, k, 0:P], banks[k][:, 0:P], ACT.Copy).then_inc(kept.sem, 1)

                @block.gpsimd
                def _(pool):
                    def gather(r, k):
                        pool.wait_ge(index_in.sem, index_in.after(r * ES + k))
                        pool.wait_ge(summed.sem, summed.after(r * ES + k - ES))
                        own_instruction(pool)
                        pool.indirect_dma_start(out=msg[:, k, 0:P], out_offset=None, in_=table,
                                                in_offset=bass.IndirectOffsetOnAxis(ap=slot_g[:, k:k + 1], axis=0))\
                            .then_inc(gathered[k].sem, 16)

                    def scatter(r, k):
                        pool.wait_ge(kept.sem, kept.after(r * ES + k))
                        pool.wait_ge(scatter_in.sem, scatter_in.after(r * ES + k))
                        before = (k - 1) % ES
                        pool.wait_ge(scattered[before].sem, scattered[before].base + 16 * (r + (k > 0)))
                        own_instruction(pool)
                        pool.indirect_dma_start(out=agg_back, in_=sums[:, k, 0:P], in_offset=None, compute_op=ALU.add,
                                                out_offset=bass.IndirectOffsetOnAxis(ap=slot_s[:, k:k + 1], axis=0))\
                            .then_inc(scattered[k].sem, 16)

                    for k in range(ES):
                        gather(0, k)
                    with pool.Fori(1, ROUNDS) as r:
                        for k in range(ES):
                            scatter(r - 1, k)
                            gather(r, k)
                    for k in range(ES):
                        scatter(ROUNDS - 1, k)
                    for k in range(ES):
                        pool.wait_ge(scattered[k].sem, scattered[k].base + 16 * ROUNDS)
            edge_close()

        def rows(a, i):
            return a[bass.ds(i * BLOCK, BLOCK), :].rearrange("(p g) f -> p g f", g=G)

        def dense(loads, stores, ready, jobs=0, pre=None, evac=None, multiply=None, post=None, norm_scale=None, final=None,
                  turn=None):
            normalise = norm_scale is not None
            per_load = 16 * sum(1 + c for _, _, c in loads)
            per_store = 16 * sum(1 + c for _, _, c in stores)

            def move(eng, tile, a, cut, i, k, load, last, signal):
                if not cut:
                    pairs = [(tile[:, k, :, :], rows(a, i))]
                else:
                    top_ = TAIL if last else P
                    pairs = [(tile[lo:hi, k, :, :],
                              a[bass.ds(i * BLOCK + lo * G, (hi - lo) * G), :].rearrange("(p g) f -> p g f", g=G))
                             for lo, hi in ((0, CUT), (CUT, top_))]
                for t_, d_ in pairs:
                    eng.dma_start(t_ if load else d_, d_ if load else t_).then_inc(signal, 16)

            def loop(eng, body):
                with eng.Fori(0, TURNS) as j:
                    for k in range(DS):
                        body(j * DS + k, j, k, False)
                body(STEPS - 1, TURNS, 0, True)

            def skewed(eng, chain_links, first_half, second_half):
                first_half(0, 0, 0)
                with eng.Fori(0, TURNS) as j:
                    if chain_links:
                        chain.loop(j, chain_links * DS)
                    for k in range(DS):
                        first_half(j * DS + k + 1, j + (k == DS - 1), (k + 1) % DS)
                        second_half(j * DS + k, j, k)
                if chain_links:
                    chain.end(TURNS)
                second_half(STEPS - 1, TURNS, 0)
                if chain_links:
                    chain.settle()

            def wait_loaded(eng, j, k):
                eng.wait_ge(loaded[k].sem, loaded[k].base + per_load * (j + 1))

            with nc.Block() as block:
                @block.sync
                def _(sp):
                    def step(i, j, k, last):
                        sp.wait_ge(stored[k].sem, stored[k].base + per_store * j)
                        for tile, a, cut in loads:
                            move(sp, tile, a, cut, i, k, True, last, loaded[k].sem)
                    loop(sp, step)

                @block.gpsimd
                def _(pool):
                    def step(i, j, k, last):
                        pool.wait_ge(ready.sem, ready.after(i))
                        for tile, a, cut in stores:
                            move(pool, tile, a, cut, i, k, False, last, stored[k].sem)
                    loop(pool, step)
                    for k in range(DS):
                        pool.wait_ge(stored[k].sem, stored[k].base + per_store * (TURNS + (k == 0)))

                @block.tensor
                def _(pe):
                    if not jobs:
                        return
                    def first(i, j, k):
                        turn(pe, i, j, k, wait_loaded)
                    skewed(pe, 0, first, lambda i, j, k: multiply(pe, i, j, k))

                @block.scalar
                def _(act):
                    def first(i, j, k):
                        if jobs:
                            evac(act, i, j, k)

                    def second(i, j, k):
                        if final:
                            final(act, i, j, k)
                        if normalise:
                            act.wait_ge(var_in.sem, var_in.after(i))
                            nc.scalar.activation(scale[:, k, 0, :], scale[:, k, 0, :], ACT.Sqrt).then_inc(root_in.sem, 1)
                            act.wait_ge(scale_in.sem, scale_in.after(i))
                            src_ = node_y if post else in_x
                            for g in range(G):
                                last = nc.scalar.activation(node_h[:, k, g, :], src_[:, k, g, :], ACT.Relu,
                                                            bias=scale[:, k, 1, g:g + 1], scale=scale[:, k, 0, g:g + 1])
                            last.then_inc(normed.sem, 1)
                    if jobs or final or normalise:
                        skewed(act, 0, first, second)

                @block.vector
                def _(dve):
                    v = nc.vector

                    def first(i, j, k):
                        if pre:
                            wait_loaded(dve, j, k)
                            pre(dve, i, j, k)

                    def second(i, j, k):
                        links = 0
                        if post:
                            post(dve, i, j, k, wait_loaded)
                        elif normalise:
                            wait_loaded(dve, j, k)
                        if normalise:
                            src_ = node_y if post else in_x
                            for g in range(G):
                                last = v.bn_stats(stats[:, k, g, :], src_[:, k, g, :])
                            chain.link(dve, last)
                            own_instruction(dve)
                            for g in range(G):
                                last = v.bn_aggr(moments[:, k, g, :], stats[:, k, g, :])
                            chain.link(dve, last)
                            v.tensor_scalar(scale[:, k, 0, :], moments[:, k, :, 1], EPS, None, ALU.add)\
                                .then_inc(var_in.sem, 1)
                            dve.wait_ge(root_in.sem, root_in.after(i))
                            chain.link(dve, v.reciprocal(scale[:, k, 0, :], scale[:, k, 0, :]))
                            if norm_scale != 1:
                                chain.link(dve, v.tensor_tensor(scale[:, k, 0, :], scale[:, k, 0, :],
                                                                norm_scale[:, bass.ds(i * G, G)], ALU.mult))
                            v.scalar_tensor_tensor(out=scale[:, k, 1, :], in0=moments[:, k, :, 0], scalar=-1.0,
                                                   in1=scale[:, k, 0, :], op0=ALU.mult, op1=ALU.mult)\
                                .then_inc(scale_in.sem, 1)
                    links = (post.links if post else 0) + (0 if not normalise else 3 + (norm_scale != 1))
                    if pre or post or normalise:
                        skewed(dve, links, first, second)
            n_q = jobs * STEPS
            for k in range(DS):
                loaded[k].base += per_load * (TURNS + (k == 0))
                stored[k].base += per_store * (TURNS + (k == 0))
            if jobs:
                turned.close(n_q)
                copied.close(n_q)
                product.close(STEPS)
            if pre:
                pre_done.close(STEPS)
            if post:
                freed.close(STEPS)
            if normalise or final is conv1_final:
                normed.close(STEPS)
            if final is own_final:
                own_in.close(STEPS)
            if normalise:
                for s in (var_in, root_in, scale_in):
                    s.close(STEPS)

        def transpose_job(pe, tile, i, k, m, jobs):
            q = i * jobs + m
            ring = (jobs * k + m) % 2
            pe.wait_ge(copied.sem, copied.after(q - 2))
            for g in range(G):
                last = nc.tensor.transpose(wide[ring][:, g * P:g * P + P], tile[:, k, g, :], ident[:, :])
            last.then_inc(turned.sem, 1)

        def copy_job(act, i, k, m, jobs, to, func=ACT.Copy, **more):
            q = i * jobs + m
            act.wait_ge(turned.sem, turned.after(q))
            nc.scalar.activation(to[:, :], wide[(jobs * k + m) % 2][:, :], func, **more).then_inc(copied.sem, 1)

        def rows_times(ps, featT, w, start, stop):
            for g in range(G):
                last = nc.tensor.matmul(ps[:, g * P:g * P + P], featT[:, g * P:g * P + P], w, start=start, stop=stop)
            return last

        def pre_add(dve, i, j, k):
            nc.vector.tensor_tensor(in_a[:, k], in_a[:, k], in_b[:, k], ALU.add).then_inc(pre_done.sem, 1)

        def turn_one(pe, i, j, k, wait_loaded):
            pe.wait_ge(pre_done.sem, pre_done.after(i))
            transpose_job(pe, in_a, i, k, 0, 1)

        def evac_one(act, i, j, k):
            act.wait_ge(product.sem, product.after(i - 2))
            copy_job(act, i, k, 0, 1, feat[k % 2])

        def multiply_one(w):
            def multiply(pe, i, j, k):
                pe.wait_ge(copied.sem, copied.after(i))
                pe.wait_ge(freed.sem, freed.after(i - 2))
                rows_times(wide[2 + k % 2], feat[k % 2], weights[:, w, :], True, True).then_inc(product.sem, 1)
            return multiply

        def conv_rows(dve, i, k, b):
            dve.wait_ge(product.sem, product.after(i))
            for g in range(G):
                last = nc.vector.scalar_tensor_tensor(out=node_y[:, k, g, :], in0=wide[2 + k % 2][:, g * P:g * P + P],
                                                      scalar=dinv[:, bass.ds(i * G + g, 1)], in1=bias[:, b, :],
                                                      op0=ALU.mult, op1=ALU.add)
            last.then_inc(freed.sem, 1)

        def conv1_post(dve, i, j, k, wait_loaded):
            conv_rows(dve, i, k, 0)
        conv1_post.links = 0

        def conv1_final(act, i, j, k):
            act.wait_ge(freed.sem, freed.after(i))
            for g in range(G):
                last = nc.scalar.activation(node_h[:, k, g, :], node_y[:, k, g, :], ACT.Relu,
                                            scale=dinv[:, bass.ds(i * G + g, 1)])
            last.then_inc(normed.sem, 1)

        def relu_residual(dve, i, k):
            dve.wait_ge(freed.sem, freed.after(i))
            chain.link(dve, nc.vector.scalar_tensor_tensor(out=node_y[:, k], in0=node_y[:, k], scalar=0.0,
                                                           in1=in_x[:, k], op0=ALU.max, op1=ALU.add))

        def conv2_post(dve, i, j, k, wait_loaded):
            conv_rows(dve, i, k, 1)
            relu_residual(dve, i, k)
        conv2_post.links = 1

        def turn_three(pe, i, j, k, wait_loaded):
            wait_loaded(pe, j, k)
            for m, tile in enumerate((in_a, in_c, in_b)):
                transpose_job(pe, tile, i, k, m, 3)

        def evac_three(act, i, j, k):
            act.wait_ge(product.sem, product.after(i - 2))
            for m in range(3):
                copy_job(act, i, k, m, 3, feat[3 * (k % 2) + m])

        def multiply_three(pe, i, j, k):
            pe.wait_ge(copied.sem, copied.after(3 * i + 2))
            pe.wait_ge(freed.sem, freed.after(i - 1))
            f = feat[3 * (k % 2):3 * (k % 2) + 3]
            for g in range(G):
                at = slice(g * P, g * P + P)
                nc.tensor.matmul(wide[2][:, at], f[0][:, at], weights[:, W_M1, :], start=True, stop=False)
                nc.tensor.matmul(wide[2][:, at], f[1][:, at], weights[:, W_M2, :], start=False, stop=True)
            rows_times(wide[3], f[2], weights[:, W_M0, :], True, True).then_inc(product.sem, 1)

        def own_final(act, i, j, k):
            act.wait_ge(product.sem, product.after(i))
            act.wait_ge(stored[k].sem, stored[k].base + 32 * j)
            nc.scalar.activation(node_h[:, k].rearrange("p g f -> p (g f)"), wide[3][:, :], ACT.Copy)\
                .then_inc(own_in.sem, 1)

        def mean_post(dve, i, j, k, wait_loaded):
            dve.wait_ge(own_in.sem, own_in.after(i))
            for g in range(G):
                last = nc.vector.scalar_tensor_tensor(out=node_y[:, k, g, :], in0=wide[2][:, g * P:g * P + P],
                                                      scalar=rcount[:, bass.ds(i * G + g, 1)], in1=node_h[:, k, g, :],
                                                      op0=ALU.mult, op1=ALU.add)
            last.then_inc(freed.sem, 1)
            relu_residual(dve, i, k)
        mean_post.links = 1

        def gin_parts(l):
            def pre(dve, i, j, k):
                nc.vector.scalar_tensor_tensor(out=in_a[:, k], in0=in_b[:, k], scalar=gin_scale[:, l:l + 1],
                                               in1=in_a[:, k], op0=ALU.mult, op1=ALU.add).then_inc(pre_done.sem, 1)

            def turn(pe, i, j, k, wait_loaded):
                pe.wait_ge(pre_done.sem, pre_done.after(i))
                transpose_job(pe, in_a, i, k, 0, 2)
                pe.wait_ge(copied.sem, copied.after(2 * i))
                for h in range(2):
                    last = nc.tensor.matmul(wide[1][:, h * 512:h * 512 + 512], weights[:, W_G1 + l, :],
                                            feat[0][:, h * 512:h * 512 + 512], start=True, stop=True)
                last.then_inc(turned.sem, 1)

            def evac(act, i, j, k):
                copy_job(act, i, k, 0, 2, feat[0])
                act.wait_ge(product.sem, product.after(i - 2))
                copy_job(act, i, k, 1, 2, feat[1 + k % 2], ACT.Relu, bias=gin_bias[:, l:l + 1])

            def multiply(pe, i, j, k):
                pe.wait_ge(copied.sem, copied.after(2 * i + 1))
                pe.wait_ge(freed.sem, freed.after(i - 2))
                rows_times(wide[2 + k % 2], feat[1 + k % 2], weights[:, W_G2 + l, :], True, True)\
                    .then_inc(product.sem, 1)

            def post(dve, i, j, k, wait_loaded):
                dve.wait_ge(product.sem, product.after(i))
                nc.vector.tensor_tensor(node_y[:, k], wide[2 + k % 2][:, :].rearrange("p (g f) -> p g f", g=G),
                                        bias[:, 2 + l:3 + l, :].to_broadcast([P, G, P]), ALU.add).then_inc(freed.sem, 1)
                if l == 2:
                    dve.wait_ge(freed.sem, freed.after(i))
                    chain.link(dve, nc.vector.tensor_tensor(node_y[:, k], node_y[:, k], in_x[:, k], ALU.add))
            post.links = int(l == 2)
            return dict(jobs=2, pre=pre, turn=turn, evac=evac, multiply=multiply, post=post)

        def leaky_post(dve, i, j, k, wait_loaded):
            wait_loaded(dve, j, k)
            chain.link(dve, nc.vector.scalar_tensor_tensor(out=in_a[:, k], in0=in_a[:, k], scalar=SLOPE, in1=in_a[:, k],
                                                           op0=ALU.mult, op1=ALU.max))
            nc.vector.tensor_tensor(node_y[:, k], in_a[:, k], in_x[:, k], ALU.add).then_inc(freed.sem, 1)
        leaky_post.links = 1


        def tile_view(tile, n):
            return tile[:, :, :, :].rearrange("p s g f -> p (s g) f")[:, 0:n * ES, :]

        ends = tile_view(in_a, 2)
        kind = tile_view(in_b, 2)
        c_tile = tile_view(in_c, 1)
        spread = tile_view(in_x, 1)
        barrier_of = tile_view(node_y, 1)
        type_ids = tile_view(node_h, 1)
        dst_msg = norm

        def lagged(eng, links, lead, body, lag):
            def step(r, k):
                first = isinstance(r, int) and r == 0 and k == 0
                last = isinstance(r, int) and r == ROUNDS - 1 and k == ES - 1
                if not last:
                    lead(r + (k == ES - 1), (k + 1) % ES)
                body(r, k)
                if not first:
                    lag(r - (k == 0), (k - 1) % ES)
            lead(0, 0)
            for k in range(ES):
                step(0, k)
            chain.settle()
            with eng.Fori(1, ROUNDS - 1) as r:
                chain.loop(r - 1, links * ES)
                for k in range(ES):
                    step(r, k)
                if not links:
                    assert chain.count == 0
            chain.end(ROUNDS - 2)
            for k in range(ES):
                step(ROUNDS - 1, k)
            lag(ROUNDS - 1, ES - 1)
            chain.settle()

        def score_edges(table):
            with nc.Block() as block:
                @block.sync
                def _(sp):
                    with sp.Fori(0, ROUNDS) as r:
                        for k in range(ES):
                            t = r * ES + k
                            sp.wait_ge(masks.sem, masks.after(t - ES))
                            sp.dma_start(row_ids[:, k, :], row_of("dst", t)).then_inc(ids_in[k].sem, 16)
                            sp.dma_start(type_ids[:, k, :], row_of("type", t)).then_inc(ids_in[k].sem, 16)

                @block.gpsimd
                def _(pool):
                    with pool.Fori(0, ROUNDS) as r:
                        for k in range(ES):
                            pool.wait_ge(index_in.sem, index_in.after(r * ES + k))
                            pool.wait_ge(ends_in.sem, ends_in.after(r * ES + k - ES))
                            own_instruction(pool)
                            for tile, ids in ((msg, slot_g), (dst_msg, slot_h)):
                                pool.indirect_dma_start(out=tile[:, k, 0:P], out_offset=None, in_=table,
                                                        in_offset=bass.IndirectOffsetOnAxis(ap=ids[:, k:k + 1], axis=0))\
                                    .then_inc(gathered[k].sem, 16)

                @block.tensor
                def _(pe):
                    def turn(r, k):
                        pe.wait_ge(gathered[k].sem, gathered[k].base + 32 * (r + 1))
                        pe.wait_ge(top_in.sem, top_in.after(r * ES + k - ES))
                        nc.tensor.transpose(banks[k][:, 0:P], msg[:, k, 0:P], ident[:, :])
                        nc.tensor.transpose(banks[k][:, P:2 * P], dst_msg[:, k, :], ident[:, :]).then_inc(turned.sem, 1)

                    def rows_(r, k):
                        pe.wait_ge(masks.sem, masks.after(r * ES + k))
                        pe.wait_ge(ends_in.sem, ends_in.after(r * ES + k))
                        c_ps = banks[k][:, 2 * P:3 * P]
                        nc.tensor.matmul(c_ps, kind[:, 2 * k, :], rel_rows[:, 0, :], start=True, stop=False)
                        nc.tensor.matmul(c_ps, kind[:, 2 * k + 1, :], rel_rows[:, 1, :], start=False, stop=False)
                        nc.tensor.matmul(c_ps, ends[:, 2 * k, :], weights[:, W_RS, :], start=False, stop=False)
                        nc.tensor.matmul(c_ps, ends[:, 2 * k + 1, :], weights[:, W_RD, :], start=False, stop=True)\
                            .then_inc(c_in.sem, 1)

                    def broadcast(r, k):
                        pe.wait_ge(spread_in.sem, spread_in.after(r * ES + k))
                        nc.tensor.matmul(banks[k][:, 3 * P:4 * P], ones[:, :], spread[:, k, :], start=True, stop=True)\
                            .then_inc(summed.sem, 1)
                    lagged(pe, 0, turn, rows_, broadcast)

                @block.scalar
                def _(act):
                    def ends_out(r, k):
                        act.wait_ge(turned.sem, turned.after(r * ES + k))
                        nc.scalar.activation(ends[:, 2 * k:2 * k + 2, :].rearrange("p k f -> p (k f)"),
                                             banks[k][:, 0:2 * P], ACT.Copy).then_inc(ends_in.sem, 1)

                    def c_out(r, k):
                        act.wait_ge(c_in.sem, c_in.after(r * ES + k))
                        act.wait_ge(c_stored[k].sem, 16 * r + 16)
                        act.wait_ge(spread_in.sem, spread_in.after(r * ES + k - ES))
                        nc.scalar.activation(c_tile[:, k, :], banks[k][:, 2 * P:3 * P], ACT.Copy).then_inc(kept.sem, 1)
                        act.wait_ge(kept.sem, kept.after(r * ES + k))
                        act.dma_start(c_rows[bass.ds((r * ES + k) * P, P), :], c_tile[:, k, :]).then_inc(c_stored[k].sem, 16)
                    lagged(act, 0, ends_out, c_out, lambda r, k: None)
                    for k in range(ES):
                        act.wait_ge(c_stored[k].sem, 16 * ROUNDS + 16)

                @block.vector
                def _(dve):
                    v = nc.vector

                    def masks_of(r, k):
                        t = r * ES + k
                        dve.wait_ge(gathered[k].sem, gathered[k].base + 32 * r)
                        v.tensor_copy(slot_g[:, k:k + 1], idx[:, 0, bass.ds(t, 1)])
                        v.tensor_copy(slot_h[:, k:k + 1], idx[:, 1, bass.ds(t, 1)]).then_inc(index_in.sem, 1)
                        dve.wait_ge(ids_in[k].sem, ids_in[k].base + 32 * (r + 1))
                        dve.wait_ge(c_in.sem, c_in.after(t - ES))
                        v.tensor_scalar(kind[:, 2 * k, :], type_ids[:, k, :], part[:, 0:1], None, ALU.is_equal)
                        v.tensor_scalar(kind[:, 2 * k + 1, :], type_ids[:, k, :], part[:, 1:2], None, ALU.is_equal)
                        chain.link(dve, v.tensor_scalar(same[:, k, :], row_ids[:, k, :], col[:, D_, bass.ds(t, 1)],
                                                        None, ALU.is_equal))
                        v.tensor_scalar(barrier_of[:, k, :], same[:, k, :], -1.0, BIG, ALU.add, ALU.mult)\
                            .then_inc(masks.sem, 1)

                    def score_of(r, k):
                        t = r * ES + k
                        dve.wait_ge(kept.sem, kept.after(t))
                        chain.link(dve, v.tensor_tensor_reduce(out=from_last[:, k, :], in0=c_tile[:, k, :], in1=bias[:, 6, :],
                                                               scale=1.0, scalar=0.0, op0=ALU.mult, op1=ALU.add,
                                                               accum_out=small[:, k, 0:1]))
                        chain.link(dve, v.scalar_tensor_tensor(out=small[:, k, 1:2], in0=small[:, k, 0:1], scalar=SLOPE,
                                                               in1=small[:, k, 0:1], op0=ALU.mult, op1=ALU.max))
                        dve.wait_ge(summed.sem, summed.after(t - ES))
                        v.tensor_copy(score[:, bass.ds(t, 1)], small[:, k, 1:2])
                        v.tensor_scalar(spread[:, k, :], ident[:, :], small[:, k, 1:2], None, ALU.mult)\
                            .then_inc(spread_in.sem, 1)

                    def top_of(r, k):
                        t = r * ES + k
                        dve.wait_ge(summed.sem, summed.after(t))
                        own_instruction(dve)
                        chain.link(dve, v.tensor_tensor_reduce(out=from_last[:, k, :], in0=banks[k][:, 3 * P:4 * P],
                                                               in1=barrier_of[:, k, :], scale=1.0, scalar=-3.0 * BIG,
                                                               op0=ALU.add, op1=ALU.max, accum_out=small[:, k, 2:3]))
                        own_instruction(dve)
                        v.tensor_copy(top[:, 0, bass.ds(t, 1)], small[:, k, 2:3])
                        v.tensor_copy(top[:, 1, bass.ds(TILES - 1 - t, 1)], small[:, k, 2:3]).then_inc(top_in.sem, 1)
                    lagged(dve, 4, masks_of, score_of, top_of)
            for group, per in ((gathered, 32), (ids_in, 32)):
                for s in group:
                    s.base += per * ROUNDS
            for s in (masks, index_in, ends_in, top_in, turned, c_in, spread_in, summed, kept):
                s.close(TILES)

        def join_tops():
            with nc.Block() as block:
                @block.tensor
                def _(pe):
                    for at, pick, what in ((0, pick_last, top[:, 0, :]), (1, pick_first, top[:, 1, :]),
                                           (2, pick_last, col[:, D_, 0:TILES]), (3, pick_first, dst_flip[:, :])):
                        last = nc.tensor.matmul(banks[at][:, 0:TILES], pick[:, :], what, start=True, stop=True)
                    last.then_inc(turned.sem, 1)

                @block.vector
                def _(dve):
                    v = nc.vector

                    def link(ins):
                        chain.link(dve, ins)
                    dve.wait_ge(turned.sem, turned.after(0))
                    for w in range(2):
                        v.tensor_copy(edges[:, w, :], banks[w][:, 0:TILES])
                        link(v.tensor_copy(d_last[:, w, :], banks[2 + w][:, 0:TILES]))
                    for w, d in ((0, col[:, D_, 0:TILES]), (1, dst_flip[:, :])):
                        v.memset(pen[:, w, 0:1], 0.0)
                        v.memset(pen[:, 2 + w, 0:1], 0.0)
                        v.memset(carry[:, w, 0:1], -2.0 * BIG)
                        link(v.tensor_tensor(pen[:, w, 1:TILES], d_last[:, w, 1:TILES], d_last[:, w, 0:TILES - 1],
                                             ALU.is_equal))
                        link(v.tensor_tensor(pen[:, 2 + w, 1:TILES], d[:, 1:TILES], d_last[:, w, 0:TILES - 1],
                                             ALU.is_equal))
                    link(v.tensor_scalar(pen[:, :, :], pen[:, :, :], -1.0, BIG, ALU.add, ALU.mult))
                    for w in range(2):
                        link(v.tensor_tensor_scan(carry[:, w, 1:TILES + 1], pen[:, w, :], edges[:, w, :], -2.0 * BIG,
                                                  ALU.add, ALU.max))
                        link(v.tensor_tensor(seg_top[:, w, :], carry[:, w, 0:TILES], pen[:, 2 + w, :], ALU.add))
                        link(v.tensor_tensor(seg_top[:, w, :], seg_top[:, w, :], top[:, w, :], ALU.max))
                    chain.settle()
            turned.close(1)

        def attend():
            W = P + 1
            with nc.Block() as block:
                @block.sync
                def _(sp):
                    with sp.Fori(0, ROUNDS) as r:
                        for k in range(ES):
                            t = r * ES + k
                            sp.wait_ge(masks.sem, masks.after(t - ES))
                            sp.dma_start(row_ids[:, k, :], row_of("dst", t)).then_inc(ids_in[k].sem, 16)
                            sp.wait_ge(spread_in.sem, spread_in.after(t - ES))
                            sp.dma_start(c_tile[:, k, :], c_rows[bass.ds(t * P, P), :]).then_inc(c_loaded[k].sem, 16)

                @block.vector
                def _(dve):
                    v = nc.vector

                    def masks_of(r, k):
                        t = r * ES + k
                        dve.wait_ge(ex_in.sem, ex_in.after(t - ES))
                        own_instruction(dve)
                        v.scalar_tensor_tensor(out=small[:, k, 0:1], in0=seg_top[:, 1, bass.ds(TILES - 1 - t, 1)],
                                               scalar=seg_top[:, 0, bass.ds(t, 1)], in1=score[:, bass.ds(t, 1)],
                                               op0=ALU.max, op1=ALU.subtract).then_inc(index_in.sem, 1)
                        dve.wait_ge(ids_in[k].sem, ids_in[k].after(0) + 16 * r)
                        dve.wait_ge(summed.sem, summed.after(t - ES))
                        v.tensor_scalar(same[:, k, :], row_ids[:, k, :], col[:, D_, bass.ds(t, 1)], None, ALU.is_equal)
                        v.tensor_scalar(from_last[:, k, :], row_ids[:, k, :], prev_last[:, bass.ds(t, 1)], None,
                                        ALU.is_equal).then_inc(masks.sem, 1)

                    def weigh(r, k):
                        t = r * ES + k
                        dve.wait_ge(ex_in.sem, ex_in.after(t))
                        dve.wait_ge(c_loaded[k].sem, 16 * (r + 1))
                        v.tensor_scalar(msg[:, k, 0:P], c_tile[:, k, :], small[:, k, 1:2], None, ALU.mult)
                        v.tensor_copy(msg[:, k, P:W], small[:, k, 1:2]).then_inc(spread_in.sem, 1)

                    def normalise(r, k):
                        t = r * ES + k
                        dve.wait_ge(kept.sem, kept.after(t))
                        chain.link(dve, v.tensor_scalar(small[:, k, 3:4], sums[:, k, P:W], 1.0 / BIG, None, ALU.max))
                        chain.link(dve, v.reciprocal(small[:, k, 4:5], small[:, k, 3:4]))
                        dve.wait_ge(scattered[k].sem, scattered[k].base + 16 * r)
                        v.tensor_copy(slot_s[:, k:k + 1], idx[:, 2, bass.ds(t, 1)])
                        v.tensor_scalar(norm[:, k, :], sums[:, k, 0:P], small[:, k, 4:5], None, ALU.mult)\
                            .then_inc(scatter_in.sem, 1)
                    lagged(dve, 2, masks_of, weigh, normalise)

                @block.tensor
                def _(pe):
                    with pe.Fori(0, ROUNDS) as r:
                        for k in range(ES):
                            t = r * ES + k
                            pe.wait_ge(masks.sem, masks.after(t))
                            pe.wait_ge(spread_in.sem, spread_in.after(t))
                            nc.tensor.matmul(banks[k][:, 0:W], same[:, k, :], msg[:, k, 0:W], start=True, stop=False)
                            pe.wait_ge(kept.sem, kept.after(t - 1))
                            nc.tensor.matmul(banks[k][:, 0:W], from_last[:, k, :], sums[:, (k - 1) % ES, 0:W],
                                             start=False, stop=True).then_inc(summed.sem, 1)

                @block.scalar
                def _(act):
                    def exp_of(r, k):
                        t = r * ES + k
                        act.wait_ge(index_in.sem, index_in.after(t))
                        act.wait_ge(spread_in.sem, spread_in.after(t - ES))
                        nc.scalar.activation(small[:, k, 1:2], small[:, k, 0:1], ACT.Exp, scale=-1.0).then_inc(ex_in.sem, 1)

                    def keep(r, k):
                        t = r * ES + k
                        act.wait_ge(scatter_in.sem, scatter_in.after(t - ES))
                        act.wait_ge(summed.sem, summed.after(t))
                        nc.scalar.activation(sums[:, k, 0:W], banks[k][:, 0:W], ACT.Copy).then_inc(kept.sem, 1)
                    lagged(act, 0, exp_of, keep, lambda r, k: None)

                @block.gpsimd
                def _(pool):
                    with pool.Fori(0, ROUNDS) as r:
                        for k in range(ES):
                            pool.wait_ge(scatter_in.sem, scatter_in.after(r * ES + k))
                            own_instruction(pool)
                            pool.indirect_dma_start(out=agg, in_=norm[:, k, :], in_offset=None, bounds_check=NP - 1,
                                                    oob_is_err=False,
                                                    out_offset=bass.IndirectOffsetOnAxis(ap=slot_s[:, k:k + 1], axis=0))\
                                .then_inc(scattered[k].sem, 16)
                    for k in range(ES):
                        pool.wait_ge(scattered[k].sem, scattered[k].base + 16 * ROUNDS)
            for group in (scattered, ids_in):
                for s in group:
                    s.close(ROUNDS)
            for s in (masks, index_in, scatter_in, summed, kept, spread_in, ex_in):
                s.close(TILES)

        dense([(in_x, x, 1)], [(node_h, table_a, 0)], normed, norm_scale=dinv)
        sum_into_dst(table_a)
        one = dict(jobs=1, pre=pre_add, turn=turn_one, evac=evac_one)
        dense([(in_a, agg, 0), (in_b, table_a, 0)], [(node_h, table_b, 0)], normed, multiply=multiply_one(W_A1),
              post=conv1_post, final=conv1_final, **one)
        sum_into_dst(table_b)
        dense([(in_a, agg, 0), (in_b, table_b, 0), (in_x, x, 1)], [(node_y, xs, 0), (node_h, table_a, 0)], normed,
              multiply=multiply_one(W_A2), post=conv2_post, norm_scale=1, **one)
        sum_into_dst(table_a)
        sum_into_src(table_a)
        dense([(in_a, agg, 0), (in_c, agg_back, 0), (in_b, table_a, 0), (in_x, xs, 0)],
              [(node_y, xs, 0), (node_h, table_b, 0)], normed, jobs=3, turn=turn_three, evac=evac_three,
              multiply=multiply_three, post=mean_post, final=own_final, norm_scale=1)
        sum_into_dst(table_b)
        dense([(in_a, agg, 0), (in_b, table_b, 0)], [(node_y, table_a, 0)], freed, **gin_parts(0))
        sum_into_dst(table_a)
        dense([(in_a, agg, 0), (in_b, table_a, 0)], [(node_y, table_b, 0)], freed, **gin_parts(1))
        sum_into_dst(table_b)
        dense([(in_a, agg, 0), (in_b, table_b, 0), (in_x, xs, 0)], [(node_y, xs, 0), (node_h, table_a, 0)], normed,
              norm_scale=1, **gin_parts(2))
        score_edges(table_a)
        join_tops()
        attend()
        dense([(in_a, agg, 0), (in_x, xs, 0)], [(node_y, out, 1)], freed, post=leaky_post)


_INS = ["x", "src", "dst", "edge_type_200", "L0_gnn_W1", "L0_gnn_b1", "L0_gnn_W2", "L0_gnn_b2", "L1_gnn_W0",
        "L1_gnn_W1", "L1_gnn_W2", "L2_gnn_eps", "L2_gnn_W1", "L2_gnn_b1", "L2_gnn_W2", "L2_gnn_b2",
        "L3_gnn_relation_embedding", "L3_gnn_W1", "L3_gnn_b1", "L3_gnn_w2"]


def kernel(**inputs):
    import numpy as _np
    import concourse.bacc as _bacc
    from concourse import mybir as _mybir
    from concourse.bass_utils import run_bass_kernel_spmd as _run

    nc = _bacc.Bacc("TRN2", target_bir_lowering=False, num_devices=1)
    arrays, args = {}, []
    for name in _INS:
        a = _np.ascontiguousarray(inputs[name])
        arrays[f"in_{name}"] = a
        args.append(nc.dram_tensor(f"in_{name}", a.shape, _mybir.dt.from_np(a.dtype), kind="ExternalInput").ap())
    args.append(nc.dram_tensor("out_0", (N, P), _mybir.dt.float32, kind="ExternalOutput").ap())
    gnn_kernel(nc, *args)
    r = _run(nc, [arrays], core_ids=[0])
    return r.results[0]["out_0"]
```

```python
import concourse.bass as bass
from concourse import mybir
from contextlib import ExitStack

fp32 = mybir.dt.float32
bf16 = mybir.dt.bfloat16
i32 = mybir.dt.int32
ALU = mybir.AluOpType
ACT = mybir.ActivationFunctionType

P = 128
N = 50000
E = 25000
R = 200
G = 8
BLOCK = P * G
STEPS = -(-N // BLOCK)
NP = STEPS * BLOCK
COLS = NP // P
TAIL = (N - (STEPS - 1) * BLOCK) // G
CUT = 96
TILES = -(-E // P)
LAST = E - (TILES - 1) * P
ES = 8
IS = ES
DS = 4
HS = 7
PER = TILES // STEPS
HALF = BLOCK // 2
assert PER * STEPS == TILES and TILES % HS == 0 and TAIL * G == N - (STEPS - 1) * BLOCK
FAR = 1.0e5
BIG = 1.0e30
EPS = 1e-5
BESIDE = False
SLOPE = 0.01


class Chain:

    def __init__(self, sem):
        self.sem, self.base, self.per, self.count, self.round = sem, 0, 0, 0, 0

    def loop(self, turn, links):
        self.round, self.per, self.count = turn, links, 0

    def end(self, rounds):
        assert self.count == self.per, (self.count, self.per)
        self.base += self.per * rounds
        self.round, self.per, self.count = 0, 0, 0

    def link(self, engine, ins):
        self.count += 1
        ins.then_inc(self.sem, 1)
        engine.wait_ge(self.sem, self.round * self.per + (self.base + self.count))

    def settle(self):
        self.base, self.count = self.base + self.count, 0


class Signal:

    def __init__(self, sem, per=1, base=0):
        self.sem, self.per, self.base = sem, per, base

    def after(self, step):
        return self.base + self.per * (step + 1)

    def close(self, steps):
        self.base += self.per * steps


def gnn_kernel(nc, x, src, dst, edge_type, a_W1, a_b1, a_W2, a_b2, m_W0, m_W1, m_W2,
               g_eps, g_W1, g_b1, g_W2, g_b2, r_emb, r_W1, r_b1, r_w2, out):
    def scratch(name, shape):
        return nc.dram_tensor(name, shape, fp32, kind="Internal").ap()

    table_a, table_b = scratch("table_a", [NP, P]), scratch("table_b", [NP, P])
    xs = scratch("xs", [NP, P])
    agg = scratch("agg", [NP, P])
    agg_back = scratch("agg_back", [NP + P, P])
    c_rows = scratch("c_rows", [TILES * P, P])
    rows_of = {n: scratch(f"{n}_rows", [2 * P, P]) for n in ("dst", "src", "type")}

    def row_of(name, tile):
        flat = rows_of[name].rearrange("t e -> (t e)")
        return flat[bass.ds(tile * P, P)].partition_broadcast(P)

    ctx = ExitStack()
    with ctx:
        def sb(name, shape, dt=fp32):
            return ctx.enter_context(nc.sbuf_tensor(name, shape, dt))

        def sig(name, per=1, base=0):
            return Signal(ctx.enter_context(nc.semaphore(name)), per, base)

        def sigs(name, n, base=0):
            return [sig(f"{name}{k}", 16, base) for k in range(n)]

        wide = [ctx.enter_context(nc.psum_tensor(f"wide{k}", [P, BLOCK], fp32)) for k in range(4)]
        banks = [wide[k // 2][:, (k % 2) * 512:(k % 2) * 512 + 512] for k in range(8)]
        ident = sb("ident", [P, P])
        ones = sb("ones", [P, P])
        lower = sb("lower", [P, P])
        pick_last = sb("pick_last", [P, P])
        pick_first = sb("pick_first", [P, P])
        flip = sb("flip", [P, 2, TILES])
        iota_p = sb("iota_p", [P, P])
        iota_c = sb("iota_c", [P, COLS])
        part = sb("part", [P, 2])
        is_127 = sb("is_127", [P, 1])
        weights = sb("weights", [P, 16, P])
        (W_A1, W_A2, W_M0, W_M1, W_M2, W_G1, W_G2, W_RS, W_RD, W_RR) = (0, 1, 2, 3, 4, 5, 8, 11, 12, 13)
        raw = sb("raw", [P, 5, P])
        rel_rows = sb("rel_rows", [P, 2, P])
        rel_T = sb("rel_T", [P, 2, P])
        bias = sb("bias", [P, 7, P])
        gin_bias = sb("gin_bias", [P, 3])
        gin_scale = sb("gin_scale", [P, 3])
        D_, S_, T_, X_ = range(4)
        col = sb("col", [P, 4, 2 * P])
        dst_flip = sb("dst_flip", [P, TILES])
        idx = sb("idx", [P, 3, TILES], i32)
        prev_last = sb("prev_last", [P, TILES + 1])
        back_off = sb("back_off", [P, TILES])
        dump = sb("dump", [P, 1])
        node_i = sb("node_i", [P, 3, TILES], i32)
        node_at = sb("node_at", [P, 4, TILES])
        degree = sb("degree", [P, 2, COLS])
        dinv = sb("dinv", [P, COLS])
        rcount = sb("rcount", [P, COLS])
        score = sb("score", [P, TILES])
        top = sb("top", [P, 2, TILES])
        edges = sb("edges", [P, 2, TILES])
        pen = sb("pen", [P, 4, TILES])
        carry = sb("carry", [P, 2, TILES + 1])
        seg_top = sb("seg_top", [P, 2, TILES])
        d_last = sb("d_last", [P, 2, TILES])

        carrier = sig("carrier")
        s_ld, s_set, s_v, s_pe, s_act = (sig(n) for n in ("s_ld", "s_set", "s_v", "s_pe", "s_act"))
        chain = Chain(ctx.enter_context(nc.semaphore("dve_chain")))

        msg = sb("msg", [P, ES, P + 4])
        row_ids = sb("row_ids", [P, ES, P])
        same = sb("same", [P, ES, P])
        from_last = sb("from_last", [P, ES, P])
        sums = sb("sums", [P, ES, P + 4])
        norm = sb("norm", [P, ES, P])
        slot_g = sb("slot_g", [P, IS], i32)
        slot_s = sb("slot_s", [P, IS], i32)
        slot_h = sb("slot_h", [P, IS], i32)
        slot_b = sb("slot_b", [P, IS], i32)
        small = sb("small", [P, ES, 8])
        primer = sb("primer", [P, 5 * ES], i32)
        gathered = sigs("gathered", ES, 16)
        scattered = sigs("scattered", ES, 16)
        added = sigs("added", ES, 16)
        ids_in = sigs("ids_in", ES)
        c_stored = sigs("c_stored", ES, 16)
        c_loaded = sigs("c_loaded", ES)
        masks = sig("masks", 1, ES)
        index_in = sig("index_in")
        scatter_in = sig("scatter_in", 1, ES)
        summed = sig("summed", 1, ES)
        ends_in = sig("ends_in", 1, ES)
        top_in = sig("top_in", 1, ES)
        spread_in = sig("spread_in", 1, ES)
        ex_in = sig("ex_in", 1, ES)
        c_in = sig("c_in", 1, ES)
        kept = sig("kept", 1, 2)

        sh = [P, DS, G, P]
        in_a, in_b, in_c, in_x, node_y, node_h = (sb("t_" + n, sh) for n in ("in_a", "in_b", "in_c", "in_x", "node_y", "node_h"))
        feat = [sb(f"feat{k}", [P, BLOCK]) for k in range(6)]
        stats = sb("stats", [P, DS, G, 6])
        moments = sb("moments", [P, DS, G, 2])
        scale = sb("scale", [P, DS, 2, G])
        tables_in = sigs("tables_in", DS)
        x_in = sigs("x_in", DS)
        stored = sigs("stored", DS, 16)
        turned = sig("turned", 1, 24)
        copied = sig("copied", 1, 4)
        mixed = sig("mixed", 1, 4)
        relued = sig("relued", 1, 2)
        product = sig("product", 1, 4)
        own_in = sig("own_in")
        freed = sig("freed", 1, 2)
        y_in = sig("y_in", 1, 4)
        pre_done = sig("pre_done")
        var_in = sig("var_in")
        root_in = sig("root_in")
        scale_in = sig("scale_in")
        normed = sig("normed", 1, 4)

        def own_instruction(eng):
            eng.sem_inc(carrier.sem, 1)

        with ExitStack() as stage:
            def view(tile, dt, *shape):
                flat = tile[:, :, :, :].rearrange("p s g f -> p (s g f)")
                names = "abcd"[:len(shape)]
                size = 1
                for n in shape:
                    size *= n
                sizes = {n: z for n, z in zip(names, shape)}
                flat = flat[:, 0:size // (2 if dt == bf16 else 1)]
                flat = flat if dt == fp32 else flat.bitcast(dt)
                return flat.rearrange(f"p ({' '.join(names)}) -> p {' '.join(names)}", **sizes)

            oh_p = view(in_a, bf16, HS, 2, P)
            oh_c = view(in_b, bf16, HS, 2, COLS)
            edge_i = view(in_c, i32, 4, 2 * P)
            edge_f = view(node_h, fp32, 4, 2 * P)
            zeros = view(node_y, fp32, DS * G * P)
            zero_b = stage.enter_context(nc.sbuf_tensor("zero_b", [P, COLS], bf16))
            zeroed = sig("zeroed", 16)
            onehot = sig("onehot")
            counted = sig("counted", 1, HS)
            rows_out = sig("rows_out", 16)
            block = stage.enter_context(nc.Block())
            n_ld = [0]

            @block.sync
            def _(sp):
                def load(tile, source):
                    sp.dma_start(tile, source).then_inc(s_ld.sem, 16)
                    n_ld[0] += 1
                sp.wait_ge(s_set.sem, 1)
                for k, a in ((D_, dst), (S_, src), (T_, edge_type)):
                    load(edge_i[:, k, 0:P], a[0:P * P].rearrange("(t e) -> t e", e=P))
                    load(edge_i[0:TILES - 1 - P, k, P:2 * P], a[P * P:(TILES - 1) * P].rearrange("(t e) -> t e", e=P))
                    load(edge_i[TILES - 1 - P:TILES - P, k, P:P + LAST], a[(TILES - 1) * P:E].rearrange("(t e) -> t e", t=1))
                load(edge_i[:, X_, 0:P], dst[1:P * P + 1].rearrange("(t e) -> t e", e=P))
                load(edge_i[0:TILES - 1 - P, X_, P:2 * P], dst[P * P + 1:(TILES - 1) * P + 1].rearrange("(t e) -> t e", e=P))
                load(edge_i[TILES - 1 - P:TILES - P, X_, P:P + LAST - 1], dst[(TILES - 1) * P + 1:E].rearrange("(t e) -> t e", t=1))
                load(weights[:, W_A1, :], a_W1)
                load(weights[:, W_A2, :], a_W2)
                load(weights[:, W_G1:W_G1 + 3, :], g_W1.rearrange("l i o -> i l o"))
                load(weights[:, W_G2:W_G2 + 3, :], g_W2.rearrange("l i o -> i l o"))
                load(weights[:, W_RS:W_RR + 1, :], r_W1.rearrange("(k i) o -> i k o", k=3))
                for k, w in enumerate((m_W0, m_W1, m_W2)):
                    load(raw[:, k, :], w)
                load(raw[:, 3, :], r_emb[0:P, :])
                load(raw[0:R - P, 4, :], r_emb[P:R, :])
                for k, b in enumerate((a_b1, a_b2, g_b2[0, :], g_b2[1, :], g_b2[2, :], r_b1, r_w2)):
                    load(bias[:, k, :], b.partition_broadcast(P))
                with nc.allow_non_contiguous_dma(reason="384 values"):
                    load(gin_bias[:, :], g_b1.rearrange("l f -> f l"))
                load(gin_scale[:, :], g_eps.partition_broadcast(P))
                sp.wait_ge(s_v.sem, 1)
                for k, n in ((D_, "dst"), (S_, "src"), (T_, "type")):
                    sp.dma_start(rows_of[n].rearrange("(c t) e -> t c e", c=2),
                                 edge_f[:, k, :].rearrange("t (c e) -> t c e", c=2)).then_inc(rows_out.sem, 16)
                sp.wait_ge(s_set.sem, 2)
                for a, rows in ((agg, NP), (agg_back, NP + P)):
                    done = 0
                    while done < rows:
                        n = min(4096, rows - done)
                        sp.dma_start(a[done:done + n, :].rearrange("(p r) f -> p (r f)", p=P),
                                     zeros[:, 0:n]).then_inc(zeroed.sem, 16)
                        done += n
                        zeroed.base += 16
                sp.wait_ge(rows_out.sem, 48)
                sp.wait_ge(zeroed.sem, zeroed.base)

            def prime(eng, group, at):
                for k, s in enumerate(group):
                    eng.dma_start(primer[:, at + k:at + k + 1],
                                  edge_type[0:P].rearrange("(p a) -> p a", a=1)).then_inc(s.sem, 16)
                for s in group:
                    eng.wait_ge(s.sem, 16)

            @block.gpsimd
            def _(pool):
                done = [0]

                def link(ins):
                    done[0] += 1
                    ins.then_inc(s_act.sem, 1)
                    pool.wait_ge(s_act.sem, done[0])
                link(pool.memset(edge_i[:, :, :], N))
                link(pool.memset(edge_i[:, T_, :], 0))
                pool.memset(raw[:, 4, :], 0.0).then_inc(s_set.sem, 1)
                pool.memset(zeros[:, :], 0.0).then_inc(s_set.sem, 1)
                pool.memset(ones[:, :], 1.0)
                pool.memset(ident[:, :], 0.0)
                pool.memset(lower[:, :], 1.0)
                pool.memset(flip[:, :, :], 0.0)
                link(pool.memset(is_127[:, :], 0.0))
                link(pool.affine_select(out=ident[:, :], in_=ident[:, :], compare_op=ALU.not_equal, fill=1.0, base=0,
                                        pattern=[[-1, P]], channel_multiplier=1))
                link(pool.affine_select(out=is_127[:, :], in_=is_127[:, :], compare_op=ALU.not_equal, fill=1.0,
                                        base=1 - P, pattern=[[0, 1]], channel_multiplier=1))
                link(pool.affine_select(out=lower[:, :], in_=lower[:, :], compare_op=ALU.is_gt, fill=0.0, base=0,
                                        pattern=[[-1, P]], channel_multiplier=1))
                link(pool.affine_select(out=pick_first[:, :], in_=ones[:, :], compare_op=ALU.is_equal, fill=0.0, base=0,
                                        pattern=[[0, P]], channel_multiplier=1))
                link(pool.affine_select(out=pick_last[:, :], in_=ones[:, :], compare_op=ALU.is_equal, fill=0.0,
                                        base=1 - P, pattern=[[0, P]], channel_multiplier=1))
                for c in range(2):
                    link(pool.affine_select(out=flip[:, c, :], in_=flip[:, c, :], compare_op=ALU.not_equal, fill=1.0,
                                            base=c * P - (TILES - 1), pattern=[[1, TILES]], channel_multiplier=1))
                any_dt = dict(allow_small_or_imprecise_dtypes=True)
                pool.iota(iota_p[:, :], pattern=[[1, P]], base=0, channel_multiplier=0, **any_dt)
                pool.iota(iota_c[:, :], pattern=[[1, COLS]], base=0, channel_multiplier=0, **any_dt)
                pool.iota(part[:, :], pattern=[[P, 2]], base=0, channel_multiplier=1, **any_dt)
                pool.iota(dump[:, :], pattern=[[0, 1]], base=NP, channel_multiplier=1, **any_dt)
                link(pool.memset(zero_b[:, :], 0.0))
                pool.sem_inc(s_set.sem, 1)
                prime(pool, gathered + scattered + added, 0)

            @block.tensor
            def _(pe):
                pe.sem_inc(counted.sem, HS)
                for s in (summed, c_in, product, turned, mixed):
                    pe.sem_inc(s.sem, s.base)
                pe.wait_ge(s_set.sem, 3)
                pe.wait_ge(s_v.sem, 1)
                for k in range(4):
                    for c in range(2):
                        nc.tensor.transpose(banks[k // 2][:, (k % 2) * 256 + c * P:(k % 2) * 256 + c * P + P],
                                            edge_f[:, k, c * P:c * P + P], ident[:, :])
                for c in range(2):
                    last = nc.tensor.matmul(banks[2][:, 0:TILES], edge_f[:, D_, c * P:c * P + P], flip[:, c, :],
                                            start=c == 0, stop=c == 1)
                last.then_inc(s_pe.sem, 1)
                pe.wait_ge(s_ld.sem, 16 * n_ld[0])
                for k in range(4):
                    nc.tensor.transpose(wide[2][:, k * P:k * P + P], raw[:, k, :], ident[:, :])
                nc.tensor.transpose(wide[2][:, 512:512 + P], raw[:, 4, :], ident[:, :]).then_inc(s_pe.sem, 1)
                pe.wait_ge(s_v.sem, 3)
                for c in range(2):
                    last = nc.tensor.matmul(wide[3][:, c * P:c * P + P], rel_T[:, c, :], weights[:, W_RR, :],
                                            start=True, stop=True)
                last.then_inc(s_pe.sem, 1)
                for k in range(2):
                    nc.tensor.matmul(banks[k][:, 0:COLS], zero_b[:, 0:P], zero_b[:, :], start=True, stop=False)
                with pe.Fori(0, TILES // HS) as r:
                    for k in range(HS):
                        pe.wait_ge(onehot.sem, onehot.after(r * HS + k))
                        nc.tensor.matmul(banks[0][:, 0:COLS], oh_p[:, k, 0, :], oh_c[:, k, 0, :], start=False, stop=False)
                        nc.tensor.matmul(banks[1][:, 0:COLS], oh_p[:, k, 1, :], oh_c[:, k, 1, :], start=False, stop=False)\
                            .then_inc(counted.sem, 1)
                nc.tensor.matmul(banks[0][:, 0:COLS], zero_b[:, 0:P], zero_b[:, :], start=False, stop=True)
                nc.tensor.matmul(banks[1][:, 0:COLS], zero_b[:, 0:P], zero_b[:, :], start=False, stop=True)\
                    .then_inc(s_pe.sem, 1)

            @block.scalar
            def _(act):
                prime(act, c_stored + stored, 3 * ES)
                for s in (copied, relued, ends_in, ex_in, normed):
                    act.sem_inc(s.sem, s.base)
                act.wait_ge(s_v.sem, 4)
                nc.scalar.activation(dinv[:, :], dinv[:, :], ACT.Sqrt).then_inc(s_v.sem, 1)

            @block.vector
            def _(dve):
                v = nc.vector

                def link(ins):
                    chain.link(dve, ins)

                dve.sem_inc(kept.sem, kept.base - 1)
                v.memset(sums[:, :, :], 0.0).then_inc(kept.sem, 1)
                for s in (masks, freed, top_in, spread_in, scatter_in, y_in):
                    dve.sem_inc(s.sem, s.base)
                dve.wait_ge(s_set.sem, 3)
                dve.wait_ge(s_ld.sem, 16 * 12)
                dve.wait_ge(s_ld.sem, 16 * n_ld[0])
                v.tensor_copy(edge_f[:, :, :], edge_i[:, :, :]).then_inc(s_v.sem, 1)
                link(v.tensor_scalar(gin_scale[:, :], gin_scale[:, :], 1.0, None, ALU.add))
                dve.wait_ge(s_pe.sem, 1)
                v.tensor_copy(col[:, 0:2, :], banks[0].rearrange("p (k t) -> p k t", k=2))
                v.tensor_copy(col[:, 2:4, :], banks[1].rearrange("p (k t) -> p k t", k=2))
                link(v.tensor_copy(dst_flip[:, :], banks[2][:, 0:TILES]))
                v.tensor_copy(idx[:, 0, :], col[:, S_, 0:TILES])
                v.tensor_copy(idx[:, 1, :], col[:, D_, 0:TILES])
                link(v.tensor_tensor(score[:, :], col[:, D_, 0:TILES], col[:, X_, 0:TILES], ALU.is_equal))
                v.scalar_tensor_tensor(out=idx[:, 2, :], in0=score[:, :], scalar=FAR, in1=col[:, D_, 0:TILES],
                                       op0=ALU.mult, op1=ALU.add)
                link(v.memset(prev_last[:, :], -1.0))
                v.tensor_scalar(prev_last[:, 1:TILES + 1], col[:, D_, 0:TILES], 1.0, is_127[:, 0:1], ALU.add, ALU.mult)
                link(v.tensor_scalar(back_off[:, :], col[:, S_, 0:TILES], dump[:, 0:1], None, ALU.subtract))
                link(v.tensor_scalar(prev_last[:, 1:TILES + 1], prev_last[:, 1:TILES + 1], -1.0, None, ALU.add))
                for k in range(2):
                    n_i = idx[:, 1 - k, :]
                    v.tensor_scalar(node_i[:, 0, :], n_i, 3, P - 1, ALU.logical_shift_right, ALU.bitwise_and)
                    v.tensor_scalar(node_i[:, 1, :], n_i, 10, 3, ALU.logical_shift_right, ALU.logical_shift_left)
                    link(v.tensor_scalar(node_i[:, 2, :], n_i, G - 1, None, ALU.bitwise_and))
                    v.tensor_copy(node_at[:, 2 * k, :], node_i[:, 0, :])
                    link(v.tensor_tensor(node_at[:, 2 * k + 1, :], node_i[:, 1, :], node_i[:, 2, :], ALU.add))
                dve.wait_ge(s_pe.sem, 2)
                v.tensor_copy(weights[:, W_M0:W_M2 + 1, :], wide[2][:, 0:3 * P].rearrange("p (k f) -> p k f", k=3))\
                    .then_inc(s_v.sem, 1)
                v.tensor_copy(rel_T[:, :, :], wide[2][:, 3 * P:5 * P].rearrange("p (k f) -> p k f", k=2))\
                    .then_inc(s_v.sem, 1)
                dve.wait_ge(s_pe.sem, 3)
                for c in range(2):
                    link(v.tensor_tensor(rel_rows[:, c, :], wide[3][:, c * P:c * P + P], bias[:, 5, :], ALU.add))
                chain.settle()
                with dve.Fori(0, TILES // HS) as r:
                    for k in range(HS):
                        t = r * HS + k
                        dve.wait_ge(counted.sem, counted.after(t - HS))
                        for w in range(2):
                            v.tensor_scalar(oh_p[:, k, w, :], iota_p[:, :], node_at[:, 2 * w, bass.ds(t, 1)], None,
                                            ALU.is_equal)
                            last = v.tensor_scalar(oh_c[:, k, w, :], iota_c[:, :],
                                                   node_at[:, 2 * w + 1, bass.ds(t, 1)], None, ALU.is_equal)
                        last.then_inc(onehot.sem, 1)
                dve.wait_ge(s_pe.sem, 4)
                v.tensor_copy(degree[:, 0, :], banks[0][:, 0:COLS])
                link(v.tensor_copy(degree[:, 1, :], banks[1][:, 0:COLS]))
                v.tensor_scalar(dinv[:, :], degree[:, 0, :], 1.0, None, ALU.add).then_inc(s_v.sem, 1)
                link(v.tensor_tensor(rcount[:, :], degree[:, 0, :], degree[:, 1, :], ALU.add))
                link(v.tensor_scalar(rcount[:, :], rcount[:, :], 1.0, None, ALU.max))
                link(v.reciprocal(rcount[:, :], rcount[:, :]))
                dve.wait_ge(s_v.sem, 5)
                link(v.reciprocal(dinv[:, :], dinv[:, :]))
                chain.settle()

        def run(eng, groups, ticks_in_body):
            items = [(rate, rate_at + lead - rate * start, steps, slots, fn, links)
                     for parts, steps, rate, slots, start in groups
                     for rate_at in range(rate) for lead, fn, links in parts]
            if not items:
                return

            def fits(tick):
                return all(0 <= rate * tick + off < steps for rate, off, steps, _, _, _ in items)
            lo = min(-(off // rate) for rate, off, *_ in items)
            hi = max((steps - 1 - off) // rate + 1 for rate, off, steps, *_ in items)
            inner = [t for t in range(lo, hi) if fits(t)]
            turns = len(inner) // ticks_in_body
            first = inner[0] if turns > 1 else hi
            after = first + turns * ticks_in_body if turns > 1 else hi

            def straight(ticks):
                for tick in ticks:
                    for rate, off, steps, slots, fn, _ in items:
                        i = rate * tick + off
                        if 0 <= i < steps:
                            fn(i, i // slots, i % slots)
                if eng is nc.vector:
                    chain.settle()
            straight(range(lo, first))
            if turns > 1:
                with eng.Fori(0, turns) as turn:
                    if eng is nc.vector:
                        chain.loop(turn, ticks_in_body * sum(links for *_, links in items))
                    for tick in range(first, first + ticks_in_body):
                        for rate, off, steps, slots, fn, _ in items:
                            i = rate * tick + off
                            each = rate * ticks_in_body
                            fn(turn * each + i, turn * (each // slots) + i // slots, i % slots)
                if eng is nc.vector:
                    chain.end(turns)
                straight(range(after, hi))

        LAG, SLACK = 6, PER

        def run_stages(edge=None, nodes=None):
            both = edge is not None and nodes is not None

            def groups(name):
                out_ = []
                if edge:
                    out_.append((edge["parts"].get(name, []), TILES, PER if both else 1, ES, 0))
                if nodes:
                    out_.append((nodes["parts"].get(name, []), STEPS, 1, DS, LAG if both else 0))
                return out_
            body = DS if nodes else ES
            ends_ = [f for stage in (edge, nodes) if stage for f in stage["ends"]]
            with nc.Block() as block:
                @block.sync
                def _(sp):
                    run(sp, groups("sync"), body)
                    for name, wait in ends_:
                        if name == "sync":
                            wait(sp)

                @block.gpsimd
                def _(pool):
                    run(pool, groups("gpsimd"), body)
                    for name, wait in ends_:
                        if name == "gpsimd":
                            wait(pool)

                @block.tensor
                def _(pe):
                    run(pe, groups("tensor"), body)

                @block.scalar
                def _(act):
                    run(act, groups("scalar"), body)
                    for name, wait in ends_:
                        if name == "scalar":
                            wait(act)

                @block.vector
                def _(dve):
                    run(dve, groups("vector"), body)
            for stage in (edge, nodes):
                if stage:
                    for signal, n in stage["counts"]:
                        signal.base += n

        sp, pool, pe, act, dve, v = nc.sync, nc.gpsimd, nc.tensor, nc.scalar, nc.vector, nc.vector
        EACH = TILES // ES

        def uses(k):
            return -(-(TILES - k) // ES)

        def slot_counts(group, per=16):
            return [(s, per * uses(k)) for k, s in enumerate(group)]

        def all_landed(group, counts):
            def wait(eng):
                for s, n in zip(group, counts):
                    eng.wait_ge(s.sem, s.base + n)
            return wait

        def ps_dst(k):
            return banks[6 + k % 2][:, 0:P]

        def ps_src(k):
            return banks[4 + k % 2][:, 0:P]

        def tile_view(tile, n):
            return tile[:, :, :, :].rearrange("p s g f -> p (s g) f")[:, 0:n * ES, :]

        def sum_edges(table, back=False):
            back_msg, back_same, back_sums, src_ids, junk = (tile_view(a, 1) for a in (in_a, in_b, in_c, in_x, node_h))

            def ids(t, r, k):
                sp.wait_ge(masks.sem, masks.after(t - ES))
                sp.dma_start(row_ids[:, k, :], row_of("dst", t)).then_inc(ids_in[k].sem, 16)
                if back:
                    sp.dma_start(src_ids[:, k, :], row_of("src", t)).then_inc(ids_in[k].sem, 16)

            def indices(t, r, k):
                per = 32 if back else 16
                dve.wait_ge(gathered[k].sem, gathered[k].base + per * r)
                if back:
                    v.tensor_copy(slot_h[:, k:k + 1], idx[:, 1, bass.ds(t, 1)])
                v.tensor_copy(slot_g[:, k:k + 1], idx[:, 0, bass.ds(t, 1)]).then_inc(index_in.sem, 1)

            def build_masks(t, r, k):
                dve.wait_ge(ids_in[k].sem, ids_in[k].base + (32 if back else 16) * (r + 1))
                dve.wait_ge(summed.sem, summed.after(t - ES))
                v.tensor_scalar(same[:, k, :], row_ids[:, k, :], col[:, D_, bass.ds(t, 1)], None, ALU.is_equal)
                if back:
                    chain.link(dve, v.tensor_scalar(back_same[:, k, :], src_ids[:, k, :], col[:, S_, bass.ds(t, 1)], None,
                                                    ALU.is_equal))
                v.tensor_scalar(from_last[:, k, :], row_ids[:, k, :], prev_last[:, bass.ds(t, 1)], None,
                                ALU.is_equal).then_inc(masks.sem, 1)
                if back:
                    chain.link(dve, v.tensor_tensor_reduce(out=junk[:, k, :], in0=back_same[:, k, :], in1=lower[:, :],
                                                           scale=1.0, scalar=0.0, op0=ALU.mult, op1=ALU.add,
                                                           accum_out=small[:, k, 0:1]))
                    chain.link(dve, v.tensor_scalar(small[:, k, 1:2], small[:, k, 0:1], 0.0, back_off[:, bass.ds(t, 1)],
                                                    ALU.is_equal, ALU.mult))
                    dve.wait_ge(added[k].sem, added[k].base + 16 * r)
                    v.tensor_scalar(slot_b[:, k:k + 1], small[:, k, 1:2], dump[:, 0:1], None, ALU.add)
                dve.wait_ge(scattered[k].sem, scattered[k].base + 16 * r)
                v.tensor_copy(slot_s[:, k:k + 1], idx[:, 2, bass.ds(t, 1)]).then_inc(scatter_in.sem, 1)

            def sum_tile(t, r, k):
                pe.wait_ge(gathered[k].sem, gathered[k].base + (32 if back else 16) * (r + 1))
                pe.wait_ge(masks.sem, masks.after(t))
                nc.tensor.matmul(ps_dst(k), same[:, k, :], msg[:, k, 0:P], start=True, stop=False)
                if back:
                    pe.wait_ge(ends_in.sem, ends_in.after(t - 2))
                    nc.tensor.matmul(ps_src(k), back_same[:, k, :], back_msg[:, k, :], start=True, stop=True)

            def carry_on(t, r, k):
                pe.wait_ge(kept.sem, kept.after(t - 1))
                nc.tensor.matmul(ps_dst(k), from_last[:, k, :], sums[:, (k - 1) % ES, 0:P],
                                 start=False, stop=True).then_inc(summed.sem, 1)

            def keep(t, r, k):
                act.wait_ge(scattered[k].sem, scattered[k].base + 16 * r)
                act.wait_ge(summed.sem, summed.after(t))
                nc.scalar.activation(sums[:, k, 0:P], ps_dst(k), ACT.Copy).then_inc(kept.sem, 1)
                if back:
                    act.wait_ge(added[k].sem, added[k].base + 16 * r)
                    nc.scalar.activation(back_sums[:, k, :], ps_src(k), ACT.Copy).then_inc(ends_in.sem, 1)

            def gather(t, r, k):
                pool.wait_ge(index_in.sem, index_in.after(t))
                pool.wait_ge(summed.sem, summed.after(t - ES))
                own_instruction(pool)
                for tile, where in ((msg[:, k, 0:P], slot_g),) + (((back_msg[:, k, :], slot_h),) if back else ()):
                    pool.indirect_dma_start(out=tile, out_offset=None, in_=table,
                                            in_offset=bass.IndirectOffsetOnAxis(ap=where[:, k:k + 1], axis=0))\
                        .then_inc(gathered[k].sem, 16)

            def scatter(t, r, k):
                pool.wait_ge(kept.sem, kept.after(t))
                pool.wait_ge(scatter_in.sem, scatter_in.after(t))
                own_instruction(pool)
                pool.indirect_dma_start(out=agg, in_=sums[:, k, 0:P], in_offset=None, bounds_check=NP - 1, oob_is_err=False,
                                        out_offset=bass.IndirectOffsetOnAxis(ap=slot_s[:, k:k + 1], axis=0))\
                    .then_inc(scattered[k].sem, 16)
                if back:
                    before = (k - 1) % ES
                    pool.wait_ge(ends_in.sem, ends_in.after(t))
                    pool.wait_ge(added[before].sem, added[before].base + 16 * (r + (k > 0)))
                    own_instruction(pool)
                    pool.indirect_dma_start(out=agg_back, in_=back_sums[:, k, :], in_offset=None, compute_op=ALU.add,
                                            out_offset=bass.IndirectOffsetOnAxis(ap=slot_b[:, k:k + 1], axis=0))\
                        .then_inc(added[k].sem, 16)

            per = 32 if back else 16
            counts = slot_counts(gathered, per) + slot_counts(ids_in, per) + slot_counts(scattered)
            counts += [(s, TILES) for s in (masks, index_in, scatter_in, summed, kept)]
            ends_ = [("gpsimd", all_landed(scattered, [16 * uses(k) for k in range(ES)]))]
            if back:
                counts += slot_counts(added) + [(ends_in, TILES)]
                ends_ += [("gpsimd", all_landed(added, [16 * uses(k) for k in range(ES)]))]
            return dict(parts=dict(sync=[(6, ids, 0)],
                                   vector=[(5, indices, 0), (2, build_masks, 3 if back else 0)],
                                   tensor=[(0, carry_on, 0), (1, sum_tile, 0)],
                                   scalar=[(0, keep, 0)],
                                   gpsimd=[(4, gather, 0), (0, scatter, 0)]),
                        counts=counts, ends=ends_)

        def rows(a, i):
            return a[bass.ds(i * BLOCK, BLOCK), :].rearrange("(p g) f -> p g f", g=G)

        def move(eng, tile, a, i, k, load, cut, signal):
            if not cut:
                pairs = [(tile[:, k, :, :], rows(a, i))]
            else:
                top_ = TAIL if isinstance(i, int) and i == STEPS - 1 else P
                pairs = [(tile[lo:hi, k, :, :],
                          a[bass.ds(i * BLOCK + lo * G, (hi - lo) * G), :].rearrange("(p g) f -> p g f", g=G))
                         for lo, hi in ((0, CUT), (CUT, top_))]
            for t_, d_ in pairs:
                eng.dma_start(t_ if load else d_, d_ if load else t_).then_inc(signal.sem, 16)

        def half(h):
            return slice(h * HALF, h * HALF + HALF)

        def halves_of(h):
            return range(h * (G // 2), (h + 1) * (G // 2))

        def transposes(tile, i, k, m, ops, ring):
            for h in range(2):
                q = (i * ops + m) * 2 + h
                to = banks[((k * ops + m) * 2 + h) % ring]
                pe.wait_ge(copied.sem, copied.after(q - ring))
                for n, g in enumerate(halves_of(h)):
                    last = nc.tensor.transpose(to[:, n * P:n * P + P], tile[:, k, g, :], ident[:, :])
                last.then_inc(turned.sem, 1)

        def copies(to, i, k, m, ops, ring):
            for h in range(2):
                q = (i * ops + m) * 2 + h
                act.wait_ge(turned.sem, turned.after(q))
                nc.scalar.activation(to[:, half(h)], banks[((k * ops + m) * 2 + h) % ring][:, :], ACT.Copy)\
                    .then_inc(copied.sem, 1)

        def products(i, of):
            for h in range(2):
                pe.wait_ge(freed.sem, freed.after(2 * (i - 1) + h))
                for ps, terms in of:
                    for g in halves_of(h):
                        at = slice(g * P, g * P + P)
                        for n, (f, w) in enumerate(terms):
                            last = nc.tensor.matmul(ps[:, at], f[:, at], weights[:, w, :],
                                                    start=n == 0, stop=n == len(terms) - 1)
                last.then_inc(product.sem, 1)

        def dense(tables, stores, ready, x_from=None, norm_scale=None, own=(), ops=1, behind=False, ready_lag=2):
            normalise = norm_scale is not None
            per_store = 16 * sum(1 + cut for _, _, cut in stores)
            has_post = any(fn.__name__ == "post" for fn in (f for _, f, _ in own.get("vector", [])))
            src_ = node_y if has_post else in_x

            def load_tables(i, j, k):
                if ops:
                    sp.wait_ge(turned.sem, turned.after(2 * ops * (i - DS) + 2 * ops - 1))
                else:
                    sp.wait_ge(y_in.sem, y_in.after(i - DS))
                for tile, a in tables:
                    if behind and a is agg:
                        t = PER * i + PER - 1 + SLACK
                        for back_by in range(ES):
                            if isinstance(i, int):
                                u = min(t, TILES - 1) - back_by
                                if u >= 0:
                                    s_ = scattered[u % ES]
                                    sp.wait_ge(s_.sem, s_.base + 16 * (u // ES + 1))
                            else:
                                u = PER * k + PER - 1 + SLACK - back_by
                                s_ = scattered[u % ES]
                                sp.wait_ge(s_.sem, s_.base + 16 * (j * (PER * DS // ES) + u // ES + 1))
                    move(sp, tile, a, i, k, True, False, tables_in[k])

            def load_x(i, j, k):
                free = y_in if has_post else normed
                sp.wait_ge(free.sem, free.after(i - DS))
                move(sp, in_x, x_from[0], i, k, True, x_from[1], x_in[k])

            def store(i, j, k):
                sp.wait_ge(ready.sem, ready.after(i if ready is not freed else 2 * i + 1))
                for tile, a, cut in stores:
                    move(sp, tile, a, i, k, False, cut, stored[k])

            def statistics(i, j, k):
                if not has_post:
                    dve.wait_ge(x_in[k].sem, x_in[k].base + 16 * (1 + x_from[1]) * (j + 1))
                for g in range(G):
                    last = v.bn_stats(stats[:, k, g, :], src_[:, k, g, :])
                chain.link(dve, last)
                own_instruction(dve)
                for g in range(G):
                    last = v.bn_aggr(moments[:, k, g, :], stats[:, k, g, :])
                chain.link(dve, last)
                dve.wait_ge(normed.sem, normed.after(i - DS))
                v.tensor_scalar(scale[:, k, 0, :], moments[:, k, :, 1], EPS, None, ALU.add).then_inc(var_in.sem, 1)

            def factors(i, j, k):
                dve.wait_ge(root_in.sem, root_in.after(i))
                chain.link(dve, v.reciprocal(scale[:, k, 0, :], scale[:, k, 0, :]))
                if norm_scale != 1:
                    chain.link(dve, v.tensor_tensor(scale[:, k, 0, :], scale[:, k, 0, :], norm_scale[:, bass.ds(i * G, G)],
                                                    ALU.mult))
                v.scalar_tensor_tensor(out=scale[:, k, 1, :], in0=moments[:, k, :, 0], scalar=-1.0, in1=scale[:, k, 0, :],
                                       op0=ALU.mult, op1=ALU.mult).then_inc(scale_in.sem, 1)

            def roots(i, j, k):
                act.wait_ge(var_in.sem, var_in.after(i))
                nc.scalar.activation(scale[:, k, 0, :], scale[:, k, 0, :], ACT.Sqrt).then_inc(root_in.sem, 1)

            def normalised(i, j, k):
                act.wait_ge(stored[k].sem, stored[k].base + per_store * j)
                act.wait_ge(scale_in.sem, scale_in.after(i))
                for g in range(G):
                    last = nc.scalar.activation(node_h[:, k, g, :], src_[:, k, g, :], ACT.Relu,
                                                bias=scale[:, k, 1, g:g + 1], scale=scale[:, k, 0, g:g + 1])
                last.then_inc(normed.sem, 1)

            parts = {n: list(p) for n, p in own.items()} if own else {}
            lead = 3 if ops else 1
            parts["sync"] = ([(lead, load_tables, 0)] if tables else []) + ([(1, load_x, 0)] if x_from else []) + \
                [(-ready_lag, store, 0)]
            if normalise:
                parts["vector"] = parts.get("vector", [])
                parts["vector"] = [p for p in parts["vector"] if p[1].__name__ != "post"] + \
                    [(-1, factors, 1 + (norm_scale != 1))] + \
                    [p for p in parts["vector"] if p[1].__name__ == "post"] + [(0, statistics, 2)]
                parts["scalar"] = parts.get("scalar", []) + [(-1, normalised, 0), (0, roots, 0)]
            step_uses = [1 + (STEPS - 1 - k) // DS for k in range(DS)]
            counts = [(s, per_store * step_uses[k]) for k, s in enumerate(stored)]
            if tables:
                counts += [(s, 16 * len(tables) * step_uses[k]) for k, s in enumerate(tables_in)]
            if x_from:
                counts += [(s, 16 * (1 + x_from[1]) * step_uses[k]) for k, s in enumerate(x_in)]
            if ops:
                counts += [(turned, 2 * ops * STEPS), (copied, 2 * ops * STEPS), (product, 2 * STEPS), (freed, 2 * STEPS)]
            if has_post:
                counts += [(y_in, STEPS)]
            if normalise:
                counts += [(s, STEPS) for s in (var_in, root_in, scale_in)]
            if normalise or ready is normed:
                counts += [(normed, STEPS)]
            counts += own.get("counts", []) if own else []
            parts.pop("counts", None)
            return dict(parts=parts, counts=counts,
                        ends=[("sync", all_landed(stored, [per_store * n for n in step_uses]))])

        def tables_ready(eng, n, j, k):
            eng.wait_ge(tables_in[k].sem, tables_in[k].base + 16 * n * (j + 1))

        def y_free(per_store, j, k):
            dve.wait_ge(stored[k].sem, stored[k].base + per_store * j)

        def residual(i, j, k, cut, relu):
            dve.wait_ge(x_in[k].sem, x_in[k].base + 16 * (1 + cut) * (j + 1))
            dve.wait_ge(freed.sem, freed.after(2 * i + 1))
            if relu:
                last = v.scalar_tensor_tensor(out=node_y[:, k], in0=node_y[:, k], scalar=0.0, in1=in_x[:, k],
                                              op0=ALU.max, op1=ALU.add)
            else:
                last = v.tensor_tensor(node_y[:, k], node_y[:, k], in_x[:, k], ALU.add)
            last.then_inc(y_in.sem, 1)
            dve.wait_ge(y_in.sem, y_in.after(i))

        def conv(w, b, own_table, cut_x):
            per_store = 32 if cut_x else 16

            def pre(i, j, k):
                tables_ready(dve, 2, j, k)
                v.tensor_tensor(in_a[:, k], in_a[:, k], in_b[:, k], ALU.add).then_inc(pre_done.sem, 1)

            def turn(i, j, k):
                pe.wait_ge(pre_done.sem, pre_done.after(i))
                transposes(in_a, i, k, 0, 1, 4)

            def evacuate(i, j, k):
                act.wait_ge(product.sem, product.after(2 * (i - 2) + 1))
                copies(feat[k % 2], i, k, 0, 1, 4)

            def multiply(i, j, k):
                pe.wait_ge(copied.sem, copied.after(2 * i + 1))
                products(i, [(wide[2], [(feat[k % 2], w)])])

            def post(i, j, k):
                y_free(per_store, j, k)
                for h in range(2):
                    dve.wait_ge(product.sem, product.after(2 * i + h))
                    for g in halves_of(h):
                        last = v.scalar_tensor_tensor(out=node_y[:, k, g, :], in0=wide[2][:, g * P:g * P + P],
                                                      scalar=dinv[:, bass.ds(i * G + g, 1)], in1=bias[:, b, :],
                                                      op0=ALU.mult, op1=ALU.add)
                    last.then_inc(freed.sem, 1)
                if cut_x:
                    residual(i, j, k, 1, True)
                else:
                    dve.wait_ge(freed.sem, freed.after(2 * i + 1))
                    v.sem_inc(y_in.sem, 1)

            def activated(i, j, k):
                act.wait_ge(freed.sem, freed.after(2 * i + 1))
                act.wait_ge(stored[k].sem, stored[k].base + per_store * j)
                for g in range(G):
                    last = nc.scalar.activation(node_h[:, k, g, :], node_y[:, k, g, :], ACT.Relu,
                                                scale=dinv[:, bass.ds(i * G + g, 1)])
                last.then_inc(normed.sem, 1)
            own = dict(vector=[(2, pre, 0), (0, post, 0)], tensor=[(1, turn, 0), (0, multiply, 0)],
                       scalar=[(1, evacuate, 0)] + ([] if cut_x else [(0, activated, 0)]),
                       counts=[(pre_done, STEPS)])
            return own

        def mean_of_both():
            def turn(i, j, k):
                tables_ready(pe, 3, j, k)
                for m, tile in enumerate((in_a, in_c, in_b)):
                    transposes(tile, i, k, m, 3, 4)

            def evacuate(i, j, k):
                act.wait_ge(product.sem, product.after(2 * (i - 2) + 1))
                for m in range(3):
                    copies(feat[3 * (k % 2) + m], i, k, m, 3, 4)

            def multiply(i, j, k):
                f = feat[3 * (k % 2):3 * (k % 2) + 3]
                pe.wait_ge(copied.sem, copied.after(6 * i + 5))
                products(i, [(wide[2], [(f[0], W_M1), (f[1], W_M2)]), (wide[3], [(f[2], W_M0)])])

            def own_part(i, j, k):
                act.wait_ge(stored[k].sem, stored[k].base + 32 * j)
                for h in range(2):
                    act.wait_ge(product.sem, product.after(2 * i + h))
                    nc.scalar.activation(node_h[:, k].rearrange("p g f -> p (g f)")[:, half(h)], wide[3][:, half(h)],
                                         ACT.Copy).then_inc(own_in.sem, 1)

            def post(i, j, k):
                y_free(32, j, k)
                for h in range(2):
                    dve.wait_ge(own_in.sem, own_in.after(2 * i + h))
                    for g in halves_of(h):
                        last = v.scalar_tensor_tensor(out=node_y[:, k, g, :], in0=wide[2][:, g * P:g * P + P],
                                                      scalar=rcount[:, bass.ds(i * G + g, 1)], in1=node_h[:, k, g, :],
                                                      op0=ALU.mult, op1=ALU.add)
                    last.then_inc(freed.sem, 1)
                residual(i, j, k, 0, True)
            return dict(vector=[(0, post, 0)], tensor=[(1, turn, 0), (0, multiply, 0)],
                        scalar=[(1, evacuate, 0), (0, own_part, 0)], counts=[(own_in, 2 * STEPS)])

        def isomorphism(l, last_layer):
            per_store = 32 if last_layer else 16

            def pre(i, j, k):
                tables_ready(dve, 2, j, k)
                v.scalar_tensor_tensor(out=in_a[:, k], in0=in_b[:, k], scalar=gin_scale[:, l:l + 1], in1=in_a[:, k],
                                       op0=ALU.mult, op1=ALU.add).then_inc(pre_done.sem, 1)

            def turn(i, j, k):
                pe.wait_ge(pre_done.sem, pre_done.after(i))
                transposes(in_a, i, k, 0, 1, 2)

            def hidden(i, j, k):
                for h in range(2):
                    pe.wait_ge(copied.sem, copied.after(2 * i + h))
                    pe.wait_ge(relued.sem, relued.after(2 * i + h - 2))
                    nc.tensor.matmul(banks[2 + h][:, :], weights[:, W_G1 + l, :], feat[k % 2][:, half(h)],
                                     start=True, stop=True).then_inc(mixed.sem, 1)

            def evacuate(i, j, k):
                act.wait_ge(mixed.sem, mixed.after(2 * (i - 2) + 1))
                copies(feat[k % 2], i, k, 0, 1, 2)

            def hidden_relu(i, j, k):
                act.wait_ge(product.sem, product.after(2 * (i - 2) + 1))
                for h in range(2):
                    act.wait_ge(mixed.sem, mixed.after(2 * i + h))
                    nc.scalar.activation(feat[2 + k % 2][:, half(h)], banks[2 + h][:, :], ACT.Relu,
                                         bias=gin_bias[:, l:l + 1]).then_inc(relued.sem, 1)

            def multiply(i, j, k):
                pe.wait_ge(relued.sem, relued.after(2 * i + 1))
                products(i, [(wide[2], [(feat[2 + k % 2], W_G2 + l)])])

            def post(i, j, k):
                y_free(per_store, j, k)
                for h in range(2):
                    dve.wait_ge(product.sem, product.after(2 * i + h))
                    v.tensor_tensor(node_y[:, k, h * (G // 2):(h + 1) * (G // 2), :],
                                    wide[2][:, half(h)].rearrange("p (g f) -> p g f", f=P),
                                    bias[:, 2 + l:3 + l, :].to_broadcast([P, G // 2, P]), ALU.add).then_inc(freed.sem, 1)
                if last_layer:
                    residual(i, j, k, 0, False)
                else:
                    dve.wait_ge(freed.sem, freed.after(2 * i + 1))
                    v.sem_inc(y_in.sem, 1)
            return dict(vector=[(3, pre, 0), (0, post, 0)], tensor=[(2, turn, 0), (1, hidden, 0), (0, multiply, 0)],
                        scalar=[(2, evacuate, 0), (1, hidden_relu, 0)],
                        counts=[(pre_done, STEPS), (mixed, 2 * STEPS), (relued, 2 * STEPS)])

        def leaky_out():
            def post(i, j, k):
                y_free(32, j, k)
                tables_ready(dve, 1, j, k)
                chain.link(dve, v.scalar_tensor_tensor(out=in_a[:, k], in0=in_a[:, k], scalar=SLOPE, in1=in_a[:, k],
                                                       op0=ALU.mult, op1=ALU.max))
                dve.wait_ge(x_in[k].sem, x_in[k].base + 16 * (j + 1))
                v.tensor_tensor(node_y[:, k], in_a[:, k], in_x[:, k], ALU.add).then_inc(y_in.sem, 1)
            return dict(vector=[(0, post, 1)])

        ends = tile_view(in_a, 2)
        kind = tile_view(in_b, 2)
        c_tile = tile_view(in_c, 1)
        spread = tile_view(in_x, 1)
        apart = tile_view(node_y, 1)
        type_ids = tile_view(node_h, 1)
        dst_msg = norm

        def score_edges(table):
            def ids(t, r, k):
                sp.wait_ge(masks.sem, masks.after(t - ES))
                sp.dma_start(row_ids[:, k, :], row_of("dst", t)).then_inc(ids_in[k].sem, 16)
                sp.dma_start(type_ids[:, k, :], row_of("type", t)).then_inc(ids_in[k].sem, 16)

            def gather(t, r, k):
                pool.wait_ge(index_in.sem, index_in.after(t))
                pool.wait_ge(ends_in.sem, ends_in.after(t - ES))
                own_instruction(pool)
                for tile, where in ((msg, slot_g), (dst_msg, slot_h)):
                    pool.indirect_dma_start(out=tile[:, k, 0:P], out_offset=None, in_=table,
                                            in_offset=bass.IndirectOffsetOnAxis(ap=where[:, k:k + 1], axis=0))\
                        .then_inc(gathered[k].sem, 16)

            def turn(t, r, k):
                pe.wait_ge(gathered[k].sem, gathered[k].base + 32 * (r + 1))
                pe.wait_ge(top_in.sem, top_in.after(t - ES))
                nc.tensor.transpose(banks[k][:, 0:P], msg[:, k, 0:P], ident[:, :])
                nc.tensor.transpose(banks[k][:, P:2 * P], dst_msg[:, k, :], ident[:, :]).then_inc(turned.sem, 1)

            def edge_rows(t, r, k):
                pe.wait_ge(masks.sem, masks.after(t))
                pe.wait_ge(ends_in.sem, ends_in.after(t))
                c_ps = banks[k][:, 2 * P:3 * P]
                nc.tensor.matmul(c_ps, kind[:, 2 * k, :], rel_rows[:, 0, :], start=True, stop=False)
                nc.tensor.matmul(c_ps, kind[:, 2 * k + 1, :], rel_rows[:, 1, :], start=False, stop=False)
                nc.tensor.matmul(c_ps, ends[:, 2 * k, :], weights[:, W_RS, :], start=False, stop=False)
                nc.tensor.matmul(c_ps, ends[:, 2 * k + 1, :], weights[:, W_RD, :], start=False, stop=True)\
                    .then_inc(c_in.sem, 1)

            def broadcast(t, r, k):
                pe.wait_ge(spread_in.sem, spread_in.after(t))
                nc.tensor.matmul(banks[k][:, 3 * P:4 * P], ones[:, :], spread[:, k, :], start=True, stop=True)\
                    .then_inc(summed.sem, 1)

            def ends_out(t, r, k):
                act.wait_ge(turned.sem, turned.after(t))
                nc.scalar.activation(ends[:, 2 * k:2 * k + 2, :].rearrange("p k f -> p (k f)"),
                                     banks[k][:, 0:2 * P], ACT.Copy).then_inc(ends_in.sem, 1)

            def c_out(t, r, k):
                act.wait_ge(c_in.sem, c_in.after(t))
                act.wait_ge(c_stored[k].sem, c_stored[k].base + 16 * r)
                act.wait_ge(spread_in.sem, spread_in.after(t - ES))
                nc.scalar.activation(c_tile[:, k, :], banks[k][:, 2 * P:3 * P], ACT.Copy).then_inc(kept.sem, 1)

            def c_away(t, r, k):
                act.wait_ge(kept.sem, kept.after(t))
                act.dma_start(c_rows[bass.ds(t * P, P), :], c_tile[:, k, :]).then_inc(c_stored[k].sem, 16)

            def indices(t, r, k):
                dve.wait_ge(gathered[k].sem, gathered[k].base + 32 * r)
                v.tensor_copy(slot_g[:, k:k + 1], idx[:, 0, bass.ds(t, 1)])
                v.tensor_copy(slot_h[:, k:k + 1], idx[:, 1, bass.ds(t, 1)]).then_inc(index_in.sem, 1)

            def build_masks(t, r, k):
                dve.wait_ge(ids_in[k].sem, ids_in[k].base + 32 * (r + 1))
                dve.wait_ge(c_in.sem, c_in.after(t - ES))
                dve.wait_ge(top_in.sem, top_in.after(t - ES))
                v.tensor_scalar(kind[:, 2 * k, :], type_ids[:, k, :], part[:, 0:1], None, ALU.is_equal)
                v.tensor_scalar(kind[:, 2 * k + 1, :], type_ids[:, k, :], part[:, 1:2], None, ALU.is_equal)
                chain.link(dve, v.tensor_scalar(same[:, k, :], row_ids[:, k, :], col[:, D_, bass.ds(t, 1)], -1.0,
                                                ALU.is_equal, ALU.add))
                v.tensor_scalar(apart[:, k, :], same[:, k, :], BIG, None, ALU.mult).then_inc(masks.sem, 1)

            def score_of(t, r, k):
                dve.wait_ge(kept.sem, kept.after(t))
                chain.link(dve, v.tensor_tensor_reduce(out=from_last[:, k, :], in0=c_tile[:, k, :], in1=bias[:, 6, :],
                                                       scale=1.0, scalar=0.0, op0=ALU.mult, op1=ALU.add,
                                                       accum_out=small[:, k, 0:1]))
                chain.link(dve, v.scalar_tensor_tensor(out=small[:, k, 1:2], in0=small[:, k, 0:1], scalar=SLOPE,
                                                       in1=small[:, k, 0:1], op0=ALU.mult, op1=ALU.max))
                dve.wait_ge(summed.sem, summed.after(t - ES))
                v.tensor_copy(score[:, bass.ds(t, 1)], small[:, k, 1:2])
                v.tensor_scalar(spread[:, k, :], ident[:, :], small[:, k, 1:2], None, ALU.mult).then_inc(spread_in.sem, 1)

            def top_of(t, r, k):
                dve.wait_ge(summed.sem, summed.after(t))
                own_instruction(dve)
                chain.link(dve, v.tensor_tensor_reduce(out=from_last[:, k, :], in0=banks[k][:, 3 * P:4 * P],
                                                       in1=apart[:, k, :], scale=1.0, scalar=-3.0 * BIG,
                                                       op0=ALU.add, op1=ALU.max, accum_out=small[:, k, 2:3]))
                own_instruction(dve)
                v.tensor_copy(top[:, 0, bass.ds(t, 1)], small[:, k, 2:3])
                v.tensor_copy(top[:, 1, bass.ds(TILES - 1 - t, 1)], small[:, k, 2:3]).then_inc(top_in.sem, 1)

            return dict(parts=dict(sync=[(6, ids, 0)], gpsimd=[(5, gather, 0)],
                                   tensor=[(3, turn, 0), (2, edge_rows, 0), (0, broadcast, 0)],
                                   scalar=[(3, ends_out, 0), (2, c_out, 0), (1, c_away, 0)],
                                   vector=[(6, indices, 0), (4, build_masks, 1), (1, score_of, 2), (-1, top_of, 1)]),
                        counts=slot_counts(gathered, 32) + slot_counts(ids_in, 32) + slot_counts(c_stored) +
                        [(s, TILES) for s in (masks, index_in, ends_in, top_in, turned, c_in, spread_in, summed, kept)],
                        ends=[("scalar", all_landed(c_stored, [16 * uses(k) for k in range(ES)]))])

        def join_tops():
            with nc.Block() as block:
                @block.tensor
                def _(pe):
                    for at, pick, what in ((0, pick_last, top[:, 0, :]), (1, pick_first, top[:, 1, :]),
                                           (2, pick_last, col[:, D_, 0:TILES]), (3, pick_first, dst_flip[:, :])):
                        last = nc.tensor.matmul(banks[at][:, 0:TILES], pick[:, :], what, start=True, stop=True)
                    last.then_inc(turned.sem, 1)

                @block.vector
                def _(dve):
                    def link(ins):
                        chain.link(dve, ins)
                    dve.wait_ge(turned.sem, turned.after(0))
                    for w in range(2):
                        v.tensor_copy(edges[:, w, :], banks[w][:, 0:TILES])
                        link(v.tensor_copy(d_last[:, w, :], banks[2 + w][:, 0:TILES]))
                    for w, d in ((0, col[:, D_, 0:TILES]), (1, dst_flip[:, :])):
                        v.memset(pen[:, w, 0:1], 0.0)
                        v.memset(pen[:, 2 + w, 0:1], 0.0)
                        v.memset(carry[:, w, 0:1], -2.0 * BIG)
                        link(v.tensor_tensor(pen[:, w, 1:TILES], d_last[:, w, 1:TILES], d_last[:, w, 0:TILES - 1],
                                             ALU.is_equal))
                        link(v.tensor_tensor(pen[:, 2 + w, 1:TILES], d[:, 1:TILES], d_last[:, w, 0:TILES - 1],
                                             ALU.is_equal))
                    link(v.tensor_scalar(pen[:, :, :], pen[:, :, :], -1.0, BIG, ALU.add, ALU.mult))
                    for w in range(2):
                        link(v.tensor_tensor_scan(carry[:, w, 1:TILES + 1], pen[:, w, :], edges[:, w, :], -2.0 * BIG,
                                                  ALU.add, ALU.max))
                        link(v.tensor_tensor(seg_top[:, w, :], carry[:, w, 0:TILES], pen[:, 2 + w, :], ALU.add))
                        link(v.tensor_tensor(seg_top[:, w, :], seg_top[:, w, :], top[:, w, :], ALU.max))
                    chain.settle()
            turned.base += 1

        def attend():
            W = P + 1

            def ids(t, r, k):
                sp.wait_ge(masks.sem, masks.after(t - ES))
                sp.dma_start(row_ids[:, k, :], row_of("dst", t)).then_inc(ids_in[k].sem, 16)
                sp.wait_ge(spread_in.sem, spread_in.after(t - ES))
                sp.dma_start(c_tile[:, k, :], c_rows[bass.ds(t * P, P), :]).then_inc(c_loaded[k].sem, 16)

            def build_masks(t, r, k):
                dve.wait_ge(ex_in.sem, ex_in.after(t - ES))
                own_instruction(dve)
                v.scalar_tensor_tensor(out=small[:, k, 0:1], in0=seg_top[:, 1, bass.ds(TILES - 1 - t, 1)],
                                       scalar=seg_top[:, 0, bass.ds(t, 1)], in1=score[:, bass.ds(t, 1)],
                                       op0=ALU.max, op1=ALU.subtract).then_inc(index_in.sem, 1)
                dve.wait_ge(ids_in[k].sem, ids_in[k].base + 16 * (r + 1))
                dve.wait_ge(summed.sem, summed.after(t - ES))
                v.tensor_scalar(same[:, k, :], row_ids[:, k, :], col[:, D_, bass.ds(t, 1)], None, ALU.is_equal)
                v.tensor_scalar(from_last[:, k, :], row_ids[:, k, :], prev_last[:, bass.ds(t, 1)], None,
                                ALU.is_equal).then_inc(masks.sem, 1)

            def weigh(t, r, k):
                dve.wait_ge(ex_in.sem, ex_in.after(t))
                dve.wait_ge(c_loaded[k].sem, c_loaded[k].base + 16 * (r + 1))
                v.tensor_scalar(msg[:, k, 0:P], c_tile[:, k, :], small[:, k, 1:2], None, ALU.mult)
                v.tensor_copy(msg[:, k, P:W], small[:, k, 1:2]).then_inc(spread_in.sem, 1)

            def normalise(t, r, k):
                dve.wait_ge(kept.sem, kept.after(t))
                chain.link(dve, v.tensor_scalar(small[:, k, 3:4], sums[:, k, P:W], 1.0 / BIG, None, ALU.max))
                chain.link(dve, v.reciprocal(small[:, k, 4:5], small[:, k, 3:4]))
                dve.wait_ge(scattered[k].sem, scattered[k].base + 16 * r)
                v.tensor_copy(slot_s[:, k:k + 1], idx[:, 2, bass.ds(t, 1)])
                v.tensor_scalar(norm[:, k, :], sums[:, k, 0:P], small[:, k, 4:5], None, ALU.mult)\
                    .then_inc(scatter_in.sem, 1)

            def sum_tile(t, r, k):
                pe.wait_ge(masks.sem, masks.after(t))
                pe.wait_ge(spread_in.sem, spread_in.after(t))
                nc.tensor.matmul(banks[k][:, 0:W], same[:, k, :], msg[:, k, 0:W], start=True, stop=False)

            def carry_on(t, r, k):
                pe.wait_ge(kept.sem, kept.after(t - 1))
                nc.tensor.matmul(banks[k][:, 0:W], from_last[:, k, :], sums[:, (k - 1) % ES, 0:W],
                                 start=False, stop=True).then_inc(summed.sem, 1)

            def exp_of(t, r, k):
                act.wait_ge(index_in.sem, index_in.after(t))
                act.wait_ge(spread_in.sem, spread_in.after(t - ES))
                nc.scalar.activation(small[:, k, 1:2], small[:, k, 0:1], ACT.Exp, scale=-1.0).then_inc(ex_in.sem, 1)

            def keep(t, r, k):
                act.wait_ge(scatter_in.sem, scatter_in.after(t - ES))
                act.wait_ge(summed.sem, summed.after(t))
                nc.scalar.activation(sums[:, k, 0:W], banks[k][:, 0:W], ACT.Copy).then_inc(kept.sem, 1)

            def scatter(t, r, k):
                pool.wait_ge(scatter_in.sem, scatter_in.after(t))
                own_instruction(pool)
                pool.indirect_dma_start(out=agg, in_=norm[:, k, :], in_offset=None, bounds_check=NP - 1, oob_is_err=False,
                                        out_offset=bass.IndirectOffsetOnAxis(ap=slot_s[:, k:k + 1], axis=0))\
                    .then_inc(scattered[k].sem, 16)
            return dict(parts=dict(sync=[(6, ids, 0)], vector=[(4, build_masks, 0), (2, weigh, 0), (-1, normalise, 2)],
                                   tensor=[(0, carry_on, 0), (1, sum_tile, 0)],
                                   scalar=[(3, exp_of, 0), (0, keep, 0)], gpsimd=[(-1, scatter, 0)]),
                        counts=slot_counts(scattered) + slot_counts(ids_in) + slot_counts(c_loaded) +
                        [(s, TILES) for s in (masks, index_in, scatter_in, summed, kept, spread_in, ex_in)],
                        ends=[("gpsimd", all_landed(scattered, [16 * uses(k) for k in range(ES)]))])

        def layers(beside):
            def pair(edge, nodes):
                if beside:
                    run_stages(edge, nodes)
                else:
                    run_stages(edge)
                    run_stages(None, nodes)

            run_stages(None, dense([], [(node_h, table_a, 0)], normed, (x, 1), dinv, {}, ops=0))
            pair(sum_edges(table_a),
                 dense([(in_a, agg), (in_b, table_a)], [(node_h, table_b, 0)], normed, own=conv(W_A1, 0, 1, False),
                       behind=beside))
            pair(sum_edges(table_b),
                 dense([(in_a, agg), (in_b, table_b)], [(node_y, xs, 0), (node_h, table_a, 0)], normed, (x, 1), 1,
                       conv(W_A2, 1, 1, True), behind=beside))
            run_stages(sum_edges(table_a, back=True))
            run_stages(None, dense([(in_a, agg), (in_c, agg_back), (in_b, table_a)],
                                   [(node_y, xs, 0), (node_h, table_b, 0)], normed, (xs, 0), 1, mean_of_both(), ops=3))
            for l, (old, new) in enumerate(((table_b, table_a), (table_a, table_b))):
                pair(sum_edges(old), dense([(in_a, agg), (in_b, old)], [(node_y, new, 0)], y_in,
                                           own=isomorphism(l, False), behind=beside))
            pair(sum_edges(table_b),
                 dense([(in_a, agg), (in_b, table_b)], [(node_y, xs, 0), (node_h, table_a, 0)], normed, (xs, 0), 1,
                       isomorphism(2, True), behind=beside))
            run_stages(score_edges(table_a))
            join_tops()
            pair(attend(), dense([(in_a, agg)], [(node_y, out, 1)], y_in, (xs, 0), None, leaky_out(), ops=0))

        layers(BESIDE)


_INS = ["x", "src", "dst", "edge_type_200", "L0_gnn_W1", "L0_gnn_b1", "L0_gnn_W2", "L0_gnn_b2", "L1_gnn_W0",
        "L1_gnn_W1", "L1_gnn_W2", "L2_gnn_eps", "L2_gnn_W1", "L2_gnn_b1", "L2_gnn_W2", "L2_gnn_b2",
        "L3_gnn_relation_embedding", "L3_gnn_W1", "L3_gnn_b1", "L3_gnn_w2"]


def kernel(**inputs):
    import numpy as _np
    import concourse.bacc as _bacc
    from concourse import mybir as _mybir
    from concourse.bass_utils import run_bass_kernel_spmd as _run

    nc = _bacc.Bacc("TRN2", target_bir_lowering=False, num_devices=1)
    arrays, args = {}, []
    for name in _INS:
        a = _np.ascontiguousarray(inputs[name])
        arrays[f"in_{name}"] = a
        args.append(nc.dram_tensor(f"in_{name}", a.shape, _mybir.dt.from_np(a.dtype), kind="ExternalInput").ap())
    args.append(nc.dram_tensor("out_0", (N, P), _mybir.dt.float32, kind="ExternalOutput").ap())
    gnn_kernel(nc, *args)
    r = _run(nc, [arrays], core_ids=[0])
    return r.results[0]["out_0"]
```

```python
import concourse.bass as bass
from concourse import mybir
from contextlib import ExitStack

fp32 = mybir.dt.float32
bf16 = mybir.dt.bfloat16
f16 = mybir.dt.float16
i32 = mybir.dt.int32
ALU = mybir.AluOpType
ACT = mybir.ActivationFunctionType

P = 128
N = 50000
E = 25000
R = 200
G = 8
BLOCK = P * G
STEPS = -(-N // BLOCK)
NP = STEPS * BLOCK
COLS = NP // P
TAIL = (N - (STEPS - 1) * BLOCK) // G
CUT = 96
TILES = -(-E // P)
LAST = E - (TILES - 1) * P
CHUNKS = 7
CHUNK = TILES * P // CHUNKS
ES = 8
DS = 4
HS = 7
PER = TILES // STEPS
SLACK = PER
LATER = len(range(PER + SLACK, TILES, PER))
LAG = 9
HALF = BLOCK // 2
assert PER * STEPS == TILES and TILES % HS == 0 and TAIL * G == N - (STEPS - 1) * BLOCK
FAR = 1.0e5
BIG = 1.0e30
EPS = 1e-5
SLOPE = 0.01


class Chain:

    def __init__(self, sem):
        self.sem, self.base, self.per, self.count, self.round = sem, 0, 0, 0, 0

    def loop(self, turn, links):
        self.round, self.per, self.count = turn, links, 0

    def end(self, rounds):
        assert self.count == self.per, (self.count, self.per)
        self.base += self.per * rounds
        self.round, self.per, self.count = 0, 0, 0

    def link(self, engine, ins):
        self.count += 1
        ins.then_inc(self.sem, 1)
        engine.wait_ge(self.sem, self.round * self.per + (self.base + self.count))

    def settle(self):
        self.base, self.count = self.base + self.count, 0


class Signal:

    def __init__(self, sem, per=1, base=0):
        self.sem, self.per, self.base = sem, per, base

    def after(self, step):
        return self.base + self.per * (step + 1)


def gnn_kernel(nc, x, src, dst, edge_type, a_W1, a_b1, a_W2, a_b2, m_W0, m_W1, m_W2,
               g_eps, g_W1, g_b1, g_W2, g_b2, r_emb, r_W1, r_b1, r_w2, out):
    def scratch(name, shape):
        return nc.dram_tensor(name, shape, fp32, kind="Internal").ap()

    table_a, table_b = scratch("table_a", [NP, P]), scratch("table_b", [NP, P])
    xs = scratch("xs", [NP, P])
    agg = scratch("agg", [NP, P])
    agg_back = scratch("agg_back", [NP + P, P])
    c_rows = scratch("c_rows", [TILES * P, P])
    in_order = scratch("in_order", [TILES * P, 4])
    rows_of = {n: scratch(f"{n}_rows", [2 * P, P]) for n in ("dst", "src", "type")}

    def row_of(name, tile):
        flat = rows_of[name].rearrange("t e -> (t e)")
        return flat[bass.ds(tile * P, P)].partition_broadcast(P)

    ctx = ExitStack()
    with ctx:
        def sb(name, shape, dt=fp32):
            return ctx.enter_context(nc.sbuf_tensor(name, shape, dt))

        signals = []

        def sig(name, per=1, base=0):
            signals.append(Signal(ctx.enter_context(nc.semaphore(name)), per, base))
            return signals[-1]

        def sigs(name, n, base=0):
            return [sig(f"{name}{k}", 16, base) for k in range(n)]

        wide = [ctx.enter_context(nc.psum_tensor(f"wide{k}", [P, BLOCK], fp32)) for k in range(4)]
        banks = [wide[k // 2][:, (k % 2) * 512:(k % 2) * 512 + 512] for k in range(8)]
        ident = sb("ident", [P, P])
        ones = sb("ones", [P, P])
        lower = sb("lower", [P, P])
        pick_last = sb("pick_last", [P, P])
        pick_first = sb("pick_first", [P, P])
        flip = sb("flip", [P, 2, TILES])
        iota_p = sb("iota_p", [P, P], f16)
        iota_c = sb("iota_c", [P, COLS], f16)
        part = sb("part", [P, 2])
        is_127 = sb("is_127", [P, 1])
        weights = sb("weights", [P, 16, P])
        (W_A1, W_A2, W_M0, W_M1, W_M2, W_G1, W_G2, W_RS, W_RD, W_RR) = (0, 1, 2, 3, 4, 5, 8, 11, 12, 13)
        raw = sb("raw", [P, 5, P])
        rel_rows = sb("rel_rows", [P, 2, P])
        rel_T = sb("rel_T", [P, 2, P])
        bias = sb("bias", [P, 7, P])
        gin_bias = sb("gin_bias", [P, 3])
        gin_scale = sb("gin_scale", [P, 3])
        D_, S_, T_, X_ = range(4)
        col = sb("col", [P, 4, 2 * P])
        dst_flip = sb("dst_flip", [P, TILES])
        idx = sb("idx", [P, 3, TILES], i32)
        prev_last = sb("prev_last", [P, TILES + 1])
        back_off = sb("back_off", [P, TILES])
        dump = sb("dump", [P, 1])
        node_i = sb("node_i", [P, 3, TILES], i32)
        node_at = sb("node_at", [P, 4, TILES])
        degree = sb("degree", [P, 2, COLS])
        dinv = sb("dinv", [P, COLS])
        rcount = sb("rcount", [P, COLS])
        score = sb("score", [P, TILES])
        top = sb("top", [P, 2, TILES])
        edges = sb("edges", [P, 2, TILES])
        pen = sb("pen", [P, 4, TILES])
        carry = sb("carry", [P, 2, TILES + 1])
        seg_top = sb("seg_top", [P, 2, TILES])
        d_last = sb("d_last", [P, 2, TILES])

        unordered = sb("unordered", [P, 4])
        unordered_i = sb("unordered_i", [1, 1], i32)
        late = sb("late", [1, 2, STEPS])
        late_i = sb("late_i", [1, 1], i32)
        rank = sb("rank", [P, TILES])
        place = sb("place", [P, TILES])
        carrier = sig("carrier")
        zeroed, zeroed_back = sig("zeroed", 16), sig("zeroed_back", 16)
        s_ld, s_set, s_v, s_pe, s_act = (sig(n) for n in ("s_ld", "s_set", "s_v", "s_pe", "s_act"))
        chain = Chain(ctx.enter_context(nc.semaphore("dve_chain")))

        msg = sb("msg", [P, ES, P + 4])
        row_ids = sb("row_ids", [P, ES, P])
        same = sb("same", [P, ES, P])
        from_last = sb("from_last", [P, ES, P])
        sums = sb("sums", [P, ES, P + 4])
        norm = sb("norm", [P, ES, P])
        slot_g = sb("slot_g", [P, ES], i32)
        slot_s = sb("slot_s", [P, ES], i32)
        slot_h = sb("slot_h", [P, ES], i32)
        slot_b = sb("slot_b", [P, ES], i32)
        small = sb("small", [P, ES, 8])
        primer = sb("primer", [P, 5 * ES], i32)
        gathered = sigs("gathered", ES, 16)
        scattered = sigs("scattered", ES, 16)
        added = sigs("added", ES, 16)
        ids_in = sigs("ids_in", ES)
        c_stored = sigs("c_stored", ES, 16)
        c_loaded = sigs("c_loaded", ES)
        masks = sig("masks", 1, ES)
        index_in = sig("index_in")
        scatter_in = sig("scatter_in")
        summed = sig("summed", 1, ES)
        ends_in = sig("ends_in", 1, ES)
        top_in = sig("top_in", 1, ES)
        spread_in = sig("spread_in", 1, ES)
        ex_in = sig("ex_in", 1, ES)
        c_in = sig("c_in", 1, ES)
        dot_in = sig("dot_in")
        maximum_in = sig("maximum_in")
        norm_in = sig("norm_in", 1, ES)
        kept = sig("kept", 1, 2)

        sh = [P, DS, G, P]
        in_a, in_b, in_c, in_x, node_y, node_h = (sb("t_" + n, sh) for n in ("in_a", "in_b", "in_c", "in_x", "node_y", "node_h"))
        feat = [sb(f"feat{k}", [P, BLOCK]) for k in range(6)]
        stats = sb("stats", [P, DS, G, 6])
        moments = sb("moments", [P, DS, G, 2])
        scale = sb("scale", [P, DS, 2, G])
        tables_in = sigs("tables_in", DS)
        x_in = sigs("x_in", DS)
        stored = sigs("stored", DS, 16)
        turned = sig("turned", 1, 24)
        copied = sig("copied", 1, 4)
        mixed = sig("mixed", 1, 4)
        relued = sig("relued", 1, 2)
        product = sig("product", 1, 4)
        own_in = sig("own_in")
        freed = sig("freed", 1, 4)
        y_in = sig("y_in", 1, 4)
        pre_done = sig("pre_done")
        stats_in = sig("stats_in")
        moments_in = sig("moments_in")
        inverse_in = sig("inverse_in")
        var_in = sig("var_in")
        root_in = sig("root_in")
        scale_in = sig("scale_in")
        normed = sig("normed", 1, 4)

        def own_instruction(eng):
            eng.sem_inc(carrier.sem, 1)

        def zero_parts(a, rows):
            return [(a[at:at + min(4096, rows - at), :].rearrange("(p r) f -> p (r f)", p=P), min(4096, rows - at))
                    for at in range(0, rows, 4096)]

        with ExitStack() as stage:
            def view(tile, dt, *shape):
                flat = tile[:, :, :, :].rearrange("p s g f -> p (s g f)")
                names = "abcd"[:len(shape)]
                size = 1
                for n in shape:
                    size *= n
                sizes = {n: z for n, z in zip(names, shape)}
                flat = flat[:, 0:size // (2 if dt == bf16 else 1)]
                flat = flat if dt == fp32 else flat.bitcast(dt)
                return flat.rearrange(f"p ({' '.join(names)}) -> p {' '.join(names)}", **sizes)

            oh_p = view(in_a, bf16, HS, 2, P)
            oh_c = view(in_b, bf16, HS, 2, COLS)
            oh_f = view(in_b, fp32, DS * G * P)
            edge_i = view(in_c, i32, 4, 2 * P)
            edge_f = view(node_h, fp32, 4, 2 * P)
            zeros = view(node_y, fp32, DS * G * P)
            zero_b = stage.enter_context(nc.sbuf_tensor("zero_b", [P, COLS], bf16))
            onehot = sig("onehot")
            counted = sig("counted", 1, HS)
            rows_out = sig("rows_out", 16)
            n_ld = [0]

            def load(sp, tile, source):
                sp.dma_start(tile, source).then_inc(s_ld.sem, 16)
                n_ld[0] += 1

            def sort_edges():
                ids, less = view(in_a, fp32, CHUNK), view(in_b, fp32, CHUNK)
                steps_ = view(in_x, fp32, CHUNK)
                rows_, next_rows = view(in_a, fp32, 2, P, 4), view(in_b, fp32, 2, P, 4)
                s_iota, s_cols, s_chunk, s_ranked, s_row, s_done = (
                    sig("sort_" + n) for n in ("iota", "cols", "chunk", "ranked", "row", "done"))
                own_chain = Chain(ctx.enter_context(nc.semaphore("sort_chain")))
                s_landed = sig("sort_landed", 16)
                s_back = sig("sort_back", 16)
                halves = ((0, P, 0), (P, TILES, 1))
                with nc.Block() as block:
                    @block.sync
                    def _(sp):
                        sp.dma_start(rows_of["dst"].rearrange("(c t) e -> t c e", c=2),
                                     edge_f[:, D_, :].rearrange("t (c e) -> t c e", c=2)).then_inc(s_back.sem, 16)
                        sp.wait_ge(s_back.sem, 16)
                        flat = rows_of["dst"].rearrange("t e -> (t e)")
                        for c in range(CHUNKS):
                            if c:
                                sp.wait_ge(s_ranked.sem, c)
                            sp.dma_start(ids[:, :], flat[c * CHUNK:(c + 1) * CHUNK].partition_broadcast(P))\
                                .then_inc(s_back.sem, 16)
                        sp.wait_ge(s_landed.sem, 16 * TILES)
                        sp.wait_ge(s_done.sem, 1)
                        for lo, hi, c in halves:
                            sp.dma_start(rows_[0:hi - lo, c, :, :], in_order[lo * P:hi * P, :].rearrange(
                                "(t e) w -> t e w", e=P)).then_inc(s_back.sem, 16)
                        sp.dma_start(next_rows[:, 0, :, :], in_order[1:P * P + 1, :].rearrange("(t e) w -> t e w", e=P))\
                            .then_inc(s_back.sem, 16)
                        sp.dma_start(next_rows[0:TILES - 1 - P, 1, :, :], in_order[P * P + 1:(TILES - 1) * P + 1, :].rearrange(
                            "(t e) w -> t e w", e=P)).then_inc(s_back.sem, 16)
                        sp.dma_start(next_rows[TILES - 1 - P:TILES - P, 1, 0:P - 1, :],
                                     in_order[(TILES - 1) * P + 1:TILES * P, :].rearrange("(t e) w -> t e w", t=1))\
                            .then_inc(s_back.sem, 16)

                    @block.gpsimd
                    def _(pool):
                        any_dt = dict(allow_small_or_imprecise_dtypes=True)
                        pool.iota(steps_[:, :], pattern=[[1, CHUNK]], base=0, channel_multiplier=0, **any_dt)
                        pool.iota(place[:, :], pattern=[[P, TILES]], base=0, channel_multiplier=1, **any_dt)
                        pool.memset(ident[:, :], 0.0).then_inc(s_iota.sem, 1)
                        pool.wait_ge(s_iota.sem, 1)
                        pool.affine_select(out=ident[:, :], in_=ident[:, :], compare_op=ALU.not_equal, fill=1.0, base=0,
                                           pattern=[[-1, P]], channel_multiplier=1).then_inc(s_iota.sem, 1)
                        with pool.Fori(0, TILES) as t:
                            pool.wait_ge(s_row.sem, t + 1)
                            own_instruction(pool)
                            pool.indirect_dma_start(out=in_order, in_=msg[:, 0, 0:4], in_offset=None,
                                                    bounds_check=TILES * P - 1, oob_is_err=False,
                                                    out_offset=bass.IndirectOffsetOnAxis(ap=slot_s[:, 0:1], axis=0))\
                                .then_inc(s_landed.sem, 16)
                            pool.wait_ge(s_landed.sem, 16 * t + 16)
                            own_instruction(pool)

                    @block.tensor
                    def _(pe):
                        pe.wait_ge(s_iota.sem, 2)
                        for k in range(3):
                            for c in range(2):
                                last = nc.tensor.transpose(banks[k // 2][:, (k % 2) * 256 + c * P:(k % 2) * 256 + c * P + P],
                                                           edge_f[:, k, c * P:c * P + P], ident[:, :])
                        last.then_inc(s_cols.sem, 1)

                    @block.scalar
                    def _(act):
                        act.wait_ge(s_iota.sem, 2)

                    @block.vector
                    def _(dve):
                        v = nc.vector

                        def link(ins):
                            own_chain.link(dve, ins)
                        dve.wait_ge(s_iota.sem, 2)
                        dve.wait_ge(s_cols.sem, 1)
                        link(v.tensor_copy(col[:, 0:2, :], banks[0].rearrange("p (k t) -> p k t", k=2)))
                        link(v.tensor_copy(col[:, 2, :], banks[1][:, 0:2 * P]))
                        link(v.tensor_scalar(steps_[:, :], steps_[:, :], 1.0 / 65536, None, ALU.mult))
                        link(v.tensor_scalar(place[:, :], place[:, :], 1.0 / 65536, None, ALU.mult))
                        link(v.memset(rank[:, :], 0.0))
                        link(v.memset(msg[:, 0, 0:4], 0.0))
                        own_chain.settle()
                        for c in range(CHUNKS):
                            dve.wait_ge(s_back.sem, 32 + 16 * c)
                            with dve.Fori(0, TILES) as t:
                                own_chain.loop(t, 4)
                                link(v.scalar_tensor_tensor(out=less[:, :], in0=ids[:, :], scalar=col[:, D_, bass.ds(t, 1)],
                                                            in1=steps_[:, :], op0=ALU.subtract, op1=ALU.add))
                                link(v.tensor_scalar(less[:, :], less[:, :], place[:, bass.ds(t, 1)], None, ALU.is_lt))
                                own_instruction(dve)
                                link(v.tensor_reduce(unordered[:, 2:3], less[:, :], mybir.AxisListType.X, ALU.add))
                                link(v.tensor_tensor(rank[:, bass.ds(t, 1)], rank[:, bass.ds(t, 1)], unordered[:, 2:3],
                                                     ALU.add))
                            own_chain.end(TILES)
                            link(v.tensor_scalar(place[:, :], place[:, :], -CHUNK / 65536, None, ALU.add))
                            own_chain.settle()
                            v.sem_inc(s_ranked.sem, 1)
                        with dve.Fori(0, TILES) as t:
                            for k, w in enumerate((D_, S_, T_)):
                                v.tensor_copy(msg[:, 0, k:k + 1], col[:, w, bass.ds(t, 1)])
                            v.tensor_copy(slot_s[:, 0:1], rank[:, bass.ds(t, 1)]).then_inc(s_row.sem, 1)
                            dve.wait_ge(s_landed.sem, 16 * t + 16)
                            own_instruction(dve)
                        link(v.memset(rows_[:, :, :, :], 0.0))
                        link(v.memset(next_rows[:, :, :, :], float(N)))
                        v.sem_inc(s_done.sem, 1)
                        dve.wait_ge(s_back.sem, 16 * (1 + CHUNKS + 5))
                        for lo, hi, c in halves:
                            for k, w, tile in ((0, D_, rows_), (1, S_, rows_), (2, T_, rows_), (0, X_, next_rows)):
                                link(v.tensor_copy(edge_i[0:hi - lo, w, c * P:c * P + P], tile[0:hi - lo, c, :, k]))
                        own_chain.settle()

            with nc.Block() as block:
                @block.sync
                def _(sp):
                    sp.wait_ge(s_set.sem, 1)
                    for k, a in ((D_, dst), (S_, src), (T_, edge_type)):
                        load(sp, edge_i[:, k, 0:P], a[0:P * P].rearrange("(t e) -> t e", e=P))
                        load(sp, edge_i[0:TILES - 1 - P, k, P:2 * P], a[P * P:(TILES - 1) * P].rearrange("(t e) -> t e", e=P))
                        load(sp, edge_i[TILES - 1 - P:TILES - P, k, P:P + LAST], a[(TILES - 1) * P:E].rearrange("(t e) -> t e", t=1))
                    load(sp, edge_i[:, X_, 0:P], dst[1:P * P + 1].rearrange("(t e) -> t e", e=P))
                    load(sp, edge_i[0:TILES - 1 - P, X_, P:2 * P], dst[P * P + 1:(TILES - 1) * P + 1].rearrange("(t e) -> t e", e=P))
                    load(sp, edge_i[TILES - 1 - P:TILES - P, X_, P:P + LAST - 1], dst[(TILES - 1) * P + 1:E].rearrange("(t e) -> t e", t=1))
                    sp.wait_ge(s_ld.sem, 16 * n_ld[0])

                @block.gpsimd
                def _(pool):
                    pool.memset(edge_i[:, :, :], N).then_inc(s_act.sem, 1)
                    pool.wait_ge(s_act.sem, 1)
                    pool.memset(edge_i[:, T_, :], 0).then_inc(s_set.sem, 1)
                    pool.memset(ones[:, :], 1.0).then_inc(s_set.sem, 1)

                @block.tensor
                def _(pe):
                    pe.wait_ge(s_set.sem, 2)
                    pe.wait_ge(s_v.sem, 1)
                    nc.tensor.matmul(banks[7][:, 0:1], ones[:, :], unordered[:, 0:1], start=True, stop=True)\
                        .then_inc(s_pe.sem, 1)

                @block.vector
                def _(dve):
                    dve.wait_ge(s_ld.sem, 16 * n_ld[0])
                    chain.link(dve, nc.vector.tensor_copy(edge_f[:, :, :], edge_i[:, :, :]))
                    chain.link(dve, nc.vector.tensor_tensor(oh_f[:, 0:2 * P], edge_f[:, D_, :], edge_f[:, X_, :], ALU.is_gt))
                    nc.vector.tensor_reduce(unordered[:, 0:1], oh_f[:, 0:2 * P], mybir.AxisListType.X, ALU.add)\
                        .then_inc(s_v.sem, 1)
                    dve.wait_ge(s_pe.sem, 1)
                    chain.link(dve, nc.vector.tensor_copy(unordered_i[:, :], banks[7][0:1, 0:1]))
                    chain.settle()
            is_unordered = nc.values_load(unordered_i[0:1, 0:1], min_val=0, max_val=E)
            with nc.If(is_unordered > 0):
                sort_edges()

            block = stage.enter_context(nc.Block())

            @block.sync
            def _(sp):
                load(sp, weights[:, W_A1, :], a_W1)
                load(sp, weights[:, W_A2, :], a_W2)
                load(sp, weights[:, W_G1:W_G1 + 3, :], g_W1.rearrange("l i o -> i l o"))
                load(sp, weights[:, W_G2:W_G2 + 3, :], g_W2.rearrange("l i o -> i l o"))
                load(sp, weights[:, W_RS:W_RR + 1, :], r_W1.rearrange("(k i) o -> i k o", k=3))
                sp.wait_ge(s_set.sem, 3)
                for k, w in enumerate((m_W0, m_W1, m_W2)):
                    load(sp, raw[:, k, :], w)
                load(sp, raw[:, 3, :], r_emb[0:P, :])
                load(sp, raw[0:R - P, 4, :], r_emb[P:R, :])
                for k, b in enumerate((a_b1, a_b2, g_b2[0, :], g_b2[1, :], g_b2[2, :], r_b1, r_w2)):
                    load(sp, bias[:, k, :], b.partition_broadcast(P))
                with nc.allow_non_contiguous_dma(reason="384 values"):
                    load(sp, gin_bias[:, :], g_b1.rearrange("l f -> f l"))
                load(sp, gin_scale[:, :], g_eps.partition_broadcast(P))
                sp.wait_ge(s_v.sem, 2)
                for k, n in ((D_, "dst"), (S_, "src"), (T_, "type")):
                    sp.dma_start(rows_of[n].rearrange("(c t) e -> t c e", c=2),
                                 edge_f[:, k, :].rearrange("t (c e) -> t c e", c=2)).then_inc(rows_out.sem, 16)
                sp.wait_ge(s_set.sem, 4)
                for a, n in zero_parts(agg, NP):
                    sp.dma_start(a, zeros[:, 0:n]).then_inc(zeroed.sem, 16)
                sp.wait_ge(rows_out.sem, rows_out.base + 48)

            def prime(eng, group, at):
                for k, s in enumerate(group):
                    eng.dma_start(primer[:, at + k:at + k + 1],
                                  edge_type[0:P].rearrange("(p a) -> p a", a=1)).then_inc(s.sem, 16)
                for s in group:
                    eng.wait_ge(s.sem, 16)

            @block.gpsimd
            def _(pool):
                done = [1]

                def link(ins):
                    done[0] += 1
                    ins.then_inc(s_act.sem, 1)
                    pool.wait_ge(s_act.sem, done[0])
                pool.memset(raw[:, 4, :], 0.0).then_inc(s_set.sem, 1)
                pool.memset(zeros[:, :], 0.0).then_inc(s_set.sem, 1)
                pool.memset(ident[:, :], 0.0)
                pool.memset(lower[:, :], 1.0)
                pool.memset(flip[:, :, :], 0.0)
                link(pool.memset(is_127[:, :], 0.0))
                link(pool.affine_select(out=ident[:, :], in_=ident[:, :], compare_op=ALU.not_equal, fill=1.0, base=0,
                                        pattern=[[-1, P]], channel_multiplier=1))
                link(pool.affine_select(out=is_127[:, :], in_=is_127[:, :], compare_op=ALU.not_equal, fill=1.0,
                                        base=1 - P, pattern=[[0, 1]], channel_multiplier=1))
                link(pool.affine_select(out=lower[:, :], in_=lower[:, :], compare_op=ALU.is_gt, fill=0.0, base=0,
                                        pattern=[[-1, P]], channel_multiplier=1))
                link(pool.affine_select(out=pick_first[:, :], in_=ones[:, :], compare_op=ALU.is_equal, fill=0.0, base=0,
                                        pattern=[[0, P]], channel_multiplier=1))
                link(pool.affine_select(out=pick_last[:, :], in_=ones[:, :], compare_op=ALU.is_equal, fill=0.0,
                                        base=1 - P, pattern=[[0, P]], channel_multiplier=1))
                for c in range(2):
                    link(pool.affine_select(out=flip[:, c, :], in_=flip[:, c, :], compare_op=ALU.not_equal, fill=1.0,
                                            base=c * P - (TILES - 1), pattern=[[1, TILES]], channel_multiplier=1))
                any_dt = dict(allow_small_or_imprecise_dtypes=True)
                pool.iota(iota_p[:, :], pattern=[[1, P]], base=0, channel_multiplier=0, **any_dt)
                pool.iota(iota_c[:, :], pattern=[[1, COLS]], base=0, channel_multiplier=0, **any_dt)
                pool.iota(part[:, :], pattern=[[P, 2]], base=0, channel_multiplier=1, **any_dt)
                pool.iota(dump[:, :], pattern=[[0, 1]], base=NP, channel_multiplier=1, **any_dt)
                pool.iota(late[:, 0, 0:LATER], pattern=[[BLOCK, LATER]], base=BLOCK, channel_multiplier=0, **any_dt)
                link(pool.memset(zero_b[:, :], 0.0))
                pool.sem_inc(s_set.sem, 1)
                prime(pool, gathered + scattered + added, 0)

            @block.tensor
            def _(pe):
                pe.sem_inc(counted.sem, HS)
                for s in (summed, c_in, product, turned, mixed):
                    pe.sem_inc(s.sem, s.base)
                pe.wait_ge(s_set.sem, 5)
                pe.wait_ge(s_v.sem, 2)
                for k in range(4):
                    for c in range(2):
                        nc.tensor.transpose(banks[k // 2][:, (k % 2) * 256 + c * P:(k % 2) * 256 + c * P + P],
                                            edge_f[:, k, c * P:c * P + P], ident[:, :])
                for c in range(2):
                    last = nc.tensor.matmul(banks[2][:, 0:TILES], edge_f[:, D_, c * P:c * P + P], flip[:, c, :],
                                            start=c == 0, stop=c == 1)
                last.then_inc(s_pe.sem, 1)
                pe.wait_ge(s_ld.sem, 16 * n_ld[0])
                for k in range(4):
                    nc.tensor.transpose(wide[2][:, k * P:k * P + P], raw[:, k, :], ident[:, :])
                nc.tensor.transpose(wide[2][:, 512:512 + P], raw[:, 4, :], ident[:, :]).then_inc(s_pe.sem, 1)
                pe.wait_ge(s_v.sem, 4)
                for c in range(2):
                    last = nc.tensor.matmul(wide[3][:, c * P:c * P + P], rel_T[:, c, :], weights[:, W_RR, :],
                                            start=True, stop=True)
                last.then_inc(s_pe.sem, 1)
                for k in range(2):
                    nc.tensor.matmul(banks[k][:, 0:COLS], zero_b[:, 0:P], zero_b[:, :], start=True, stop=False)
                with pe.Fori(0, TILES // HS) as r:
                    for k in range(HS):
                        pe.wait_ge(onehot.sem, onehot.after(r * HS + k))
                        nc.tensor.matmul(banks[0][:, 0:COLS], oh_p[:, k, 0, :], oh_c[:, k, 0, :], start=False, stop=False)
                        nc.tensor.matmul(banks[1][:, 0:COLS], oh_p[:, k, 1, :], oh_c[:, k, 1, :], start=False, stop=False)\
                            .then_inc(counted.sem, 1)
                nc.tensor.matmul(banks[0][:, 0:COLS], zero_b[:, 0:P], zero_b[:, :], start=False, stop=True)
                nc.tensor.matmul(banks[1][:, 0:COLS], zero_b[:, 0:P], zero_b[:, :], start=False, stop=True)\
                    .then_inc(s_pe.sem, 1)

            @block.scalar
            def _(act):
                prime(act, c_stored + stored, 3 * ES)
                for s in (copied, relued, ends_in, ex_in, normed):
                    act.sem_inc(s.sem, s.base)
                act.wait_ge(s_v.sem, 5)
                nc.scalar.activation(dinv[:, :], dinv[:, :], ACT.Sqrt).then_inc(s_v.sem, 1)

            @block.vector
            def _(dve):
                v = nc.vector

                def link(ins):
                    chain.link(dve, ins)

                dve.sem_inc(kept.sem, kept.base - 1)
                v.memset(sums[:, :, :], 0.0).then_inc(kept.sem, 1)
                for s in (masks, freed, top_in, spread_in, norm_in, y_in):
                    dve.sem_inc(s.sem, s.base)
                v.tensor_copy(edge_f[:, :, :], edge_i[:, :, :]).then_inc(s_v.sem, 1)
                dve.wait_ge(s_set.sem, 5)
                dve.wait_ge(s_ld.sem, 16 * n_ld[0])
                link(v.tensor_scalar(gin_scale[:, :], gin_scale[:, :], 1.0, None, ALU.add))
                dve.wait_ge(s_pe.sem, 2)
                v.tensor_copy(col[:, 0:2, :], banks[0].rearrange("p (k t) -> p k t", k=2))
                v.tensor_copy(col[:, 2:4, :], banks[1].rearrange("p (k t) -> p k t", k=2))
                link(v.tensor_copy(dst_flip[:, :], banks[2][:, 0:TILES]))
                v.tensor_copy(idx[:, 0, :], col[:, S_, 0:TILES])
                v.tensor_copy(idx[:, 1, :], col[:, D_, 0:TILES])
                link(v.tensor_tensor(score[:, :], col[:, D_, 0:TILES], col[:, X_, 0:TILES], ALU.is_equal))
                v.scalar_tensor_tensor(out=idx[:, 2, :], in0=score[:, :], scalar=FAR, in1=col[:, D_, 0:TILES],
                                       op0=ALU.mult, op1=ALU.add)
                link(v.memset(prev_last[:, :], -1.0))
                v.tensor_scalar(prev_last[:, 1:TILES + 1], col[:, D_, 0:TILES], 1.0, is_127[:, 0:1], ALU.add, ALU.mult)
                link(v.tensor_scalar(back_off[:, :], col[:, S_, 0:TILES], dump[:, 0:1], None, ALU.subtract))
                link(v.tensor_scalar(prev_last[:, 1:TILES + 1], prev_last[:, 1:TILES + 1], -1.0, None, ALU.add))
                firsts = slice(PER + SLACK, TILES, PER)
                link(v.tensor_tensor(late[:, 1, 0:LATER], col[0:1, D_, firsts], late[:, 0, 0:LATER], ALU.is_lt))
                link(v.tensor_reduce(late[:, 0, 0:1], late[:, 1, 0:LATER], mybir.AxisListType.X, ALU.add))
                link(v.tensor_copy(late_i[:, :], late[:, 0, 0:1]))
                for k in range(2):
                    n_i = idx[:, 1 - k, :]
                    v.tensor_scalar(node_i[:, 0, :], n_i, 3, P - 1, ALU.logical_shift_right, ALU.bitwise_and)
                    v.tensor_scalar(node_i[:, 1, :], n_i, 10, 3, ALU.logical_shift_right, ALU.logical_shift_left)
                    link(v.tensor_scalar(node_i[:, 2, :], n_i, G - 1, None, ALU.bitwise_and))
                    v.tensor_copy(node_at[:, 2 * k, :], node_i[:, 0, :])
                    link(v.tensor_tensor(node_at[:, 2 * k + 1, :], node_i[:, 1, :], node_i[:, 2, :], ALU.add))
                dve.wait_ge(s_pe.sem, 3)
                v.tensor_copy(weights[:, W_M0:W_M2 + 1, :], wide[2][:, 0:3 * P].rearrange("p (k f) -> p k f", k=3))\
                    .then_inc(s_v.sem, 1)
                v.tensor_copy(rel_T[:, :, :], wide[2][:, 3 * P:5 * P].rearrange("p (k f) -> p k f", k=2))\
                    .then_inc(s_v.sem, 1)
                dve.wait_ge(s_pe.sem, 4)
                for c in range(2):
                    link(v.tensor_tensor(rel_rows[:, c, :], wide[3][:, c * P:c * P + P], bias[:, 5, :], ALU.add))
                chain.settle()
                with dve.Fori(0, TILES // HS) as r:
                    for k in range(HS):
                        t = r * HS + k
                        dve.wait_ge(counted.sem, counted.after(t - HS))
                        for w in range(2):
                            v.tensor_scalar(oh_p[:, k, w, :], iota_p[:, :], node_at[:, 2 * w, bass.ds(t, 1)], None,
                                            ALU.is_equal)
                            last = v.tensor_scalar(oh_c[:, k, w, :], iota_c[:, :],
                                                   node_at[:, 2 * w + 1, bass.ds(t, 1)], None, ALU.is_equal)
                        last.then_inc(onehot.sem, 1)
                dve.wait_ge(s_pe.sem, 5)
                v.tensor_copy(degree[:, 0, :], banks[0][:, 0:COLS])
                link(v.tensor_copy(degree[:, 1, :], banks[1][:, 0:COLS]))
                v.tensor_scalar(dinv[:, :], degree[:, 0, :], 1.0, None, ALU.add).then_inc(s_v.sem, 1)
                link(v.tensor_tensor(rcount[:, :], degree[:, 0, :], degree[:, 1, :], ALU.add))
                link(v.tensor_scalar(rcount[:, :], rcount[:, :], 1.0, None, ALU.max))
                link(v.reciprocal(rcount[:, :], rcount[:, :]))
                dve.wait_ge(s_v.sem, 6)
                link(v.reciprocal(dinv[:, :], dinv[:, :]))
                chain.settle()

        def run(eng, groups, ticks_in_body):
            items = []
            for parts, steps, rate, slots, start in groups:
                own = [(rate, rate_at + lead - rate * start, steps, slots, fn, links)
                       for rate_at in range(rate) for lead, fn, links in parts]
                items += [((n + 1) / (len(own) + 1), item) for n, item in enumerate(own)]
            items = [item for _, item in sorted(items, key=lambda placed: placed[0])]
            if not items:
                return

            def fits(tick):
                return all(0 <= rate * tick + off < steps - (steps == STEPS) for rate, off, steps, _, _, _ in items)
            lo = min(-(off // rate) for rate, off, *_ in items)
            hi = max((steps - 1 - off) // rate + 1 for rate, off, steps, *_ in items)
            inner = [t for t in range(lo, hi) if fits(t)]
            turns = len(inner) // ticks_in_body
            first = inner[0] if turns > 1 else hi
            after = first + turns * ticks_in_body if turns > 1 else hi

            def straight(ticks):
                for tick in ticks:
                    for rate, off, steps, slots, fn, _ in items:
                        i = rate * tick + off
                        if 0 <= i < steps:
                            fn(i, i // slots, i % slots)
                if eng is nc.vector:
                    chain.settle()
            straight(range(lo, first))
            if turns > 1:
                with eng.Fori(0, turns) as turn:
                    if eng is nc.vector:
                        chain.loop(turn, ticks_in_body * sum(links for *_, links in items))
                    for tick in range(first, first + ticks_in_body):
                        for rate, off, steps, slots, fn, _ in items:
                            i = rate * tick + off
                            each = rate * ticks_in_body
                            fn(turn * each + i, turn * (each // slots) + i // slots, i % slots)
                if eng is nc.vector:
                    chain.end(turns)
                straight(range(after, hi))

        def run_stages(edge=None, nodes=None):
            both = edge is not None and nodes is not None

            def groups(name):
                out_ = []
                if edge:
                    out_.append((edge["parts"].get(name, []), TILES, PER if both else 1, ES, 0))
                if nodes:
                    out_.append((nodes["parts"].get(name, []), STEPS, 1, DS, LAG if both else 0))
                return out_
            body = DS if nodes else ES
            ends_ = [f for stage in (edge, nodes) if stage for f in stage["ends"]]
            with nc.Block() as block:
                @block.sync
                def _(sp):
                    run(sp, groups("sync"), body)
                    for name, wait in ends_:
                        if name == "sync":
                            wait(sp)

                @block.gpsimd
                def _(pool):
                    run(pool, groups("gpsimd"), body)
                    for name, wait in ends_:
                        if name == "gpsimd":
                            wait(pool)

                @block.tensor
                def _(pe):
                    run(pe, groups("tensor"), body)

                @block.scalar
                def _(act):
                    run(act, groups("scalar"), body)
                    for name, wait in ends_:
                        if name == "scalar":
                            wait(act)

                @block.vector
                def _(dve):
                    run(dve, groups("vector"), body)
            for stage in (edge, nodes):
                if stage:
                    for signal, n in stage["counts"]:
                        signal.base += n

        sp, pool, pe, act, dve, v = nc.sync, nc.gpsimd, nc.tensor, nc.scalar, nc.vector, nc.vector

        def uses(k):
            return -(-(TILES - k) // ES)

        def slot_counts(group, per=16):
            return [(s, per * uses(k)) for k, s in enumerate(group)]

        def all_landed(group, counts):
            def wait(eng):
                for s, n in zip(group, counts):
                    eng.wait_ge(s.sem, s.base + n)
            return wait

        GROUP = 4

        def grouped_indices(which, landed, per, signal):
            def fill(t, r, k):
                if k % GROUP:
                    return
                for at in range(k, k + GROUP):
                    dve.wait_ge(landed[at].sem, landed[at].base + per * r)
                for slots, row in which:
                    last = v.tensor_copy(slots[:, k:k + GROUP], idx[:, row, bass.ds(t, GROUP)])
                last.then_inc(signal.sem, GROUP)
            return fill

        def ps_dst(k):
            return banks[6 + k % 2][:, 0:P]

        def ps_src(k):
            return banks[4 + k % 2][:, 0:P]

        def tile_view(tile, n):
            return tile[:, :, :, :].rearrange("p s g f -> p (s g) f")[:, 0:n * ES, :]

        def sum_edges(table, back=False):
            back_msg, back_same, back_sums, src_ids, junk = (tile_view(a, 1) for a in (in_a, in_b, in_c, in_x, node_h))

            def ids(t, r, k):
                sp.wait_ge(masks.sem, masks.after(t - ES))
                sp.dma_start(row_ids[:, k, :], row_of("dst", t)).then_inc(ids_in[k].sem, 16)
                if back:
                    sp.dma_start(src_ids[:, k, :], row_of("src", t)).then_inc(ids_in[k].sem, 16)

            indices = grouped_indices(((slot_h, 1), (slot_g, 0)) if back else ((slot_g, 0),), gathered,
                                      32 if back else 16, index_in)
            scatter_indices = grouped_indices(((slot_s, 2),), scattered, 16, scatter_in)

            def build_masks(t, r, k):
                dve.wait_ge(ids_in[k].sem, ids_in[k].base + (32 if back else 16) * (r + 1))
                dve.wait_ge(summed.sem, summed.after(t - ES))
                v.tensor_scalar(same[:, k, :], row_ids[:, k, :], col[:, D_, bass.ds(t, 1)], None, ALU.is_equal)
                if back:
                    chain.link(dve, v.tensor_scalar(back_same[:, k, :], src_ids[:, k, :], col[:, S_, bass.ds(t, 1)], None,
                                                    ALU.is_equal))
                v.tensor_scalar(from_last[:, k, :], row_ids[:, k, :], prev_last[:, bass.ds(t, 1)], None,
                                ALU.is_equal).then_inc(masks.sem, 1)
                if back:
                    chain.link(dve, v.tensor_tensor_reduce(out=junk[:, k, :], in0=back_same[:, k, :], in1=lower[:, :],
                                                           scale=1.0, scalar=0.0, op0=ALU.mult, op1=ALU.add,
                                                           accum_out=small[:, k, 0:1]))
                    chain.link(dve, v.tensor_scalar(small[:, k, 1:2], small[:, k, 0:1], 0.0, back_off[:, bass.ds(t, 1)],
                                                    ALU.is_equal, ALU.mult))
                    dve.wait_ge(added[k].sem, added[k].base + 16 * r)
                    v.tensor_scalar(slot_b[:, k:k + 1], small[:, k, 1:2], dump[:, 0:1], None, ALU.add)\
                        .then_inc(dot_in.sem, 1)

            def sum_tile(t, r, k):
                pe.wait_ge(gathered[k].sem, gathered[k].base + (32 if back else 16) * (r + 1))
                pe.wait_ge(masks.sem, masks.after(t))
                nc.tensor.matmul(ps_dst(k), same[:, k, :], msg[:, k, 0:P], start=True, stop=False)
                if back:
                    pe.wait_ge(ends_in.sem, ends_in.after(t - 2))
                    nc.tensor.matmul(ps_src(k), back_same[:, k, :], back_msg[:, k, :], start=True, stop=True)

            def carry_on(t, r, k):
                pe.wait_ge(kept.sem, kept.after(t - 1))
                nc.tensor.matmul(ps_dst(k), from_last[:, k, :], sums[:, (k - 1) % ES, 0:P],
                                 start=False, stop=True).then_inc(summed.sem, 1)

            def keep(t, r, k):
                act.wait_ge(scattered[k].sem, scattered[k].base + 16 * r)
                act.wait_ge(summed.sem, summed.after(t))
                nc.scalar.activation(sums[:, k, 0:P], ps_dst(k), ACT.Copy).then_inc(kept.sem, 1)
                if back:
                    act.wait_ge(added[k].sem, added[k].base + 16 * r)
                    nc.scalar.activation(back_sums[:, k, :], ps_src(k), ACT.Copy).then_inc(ends_in.sem, 1)

            def gather(t, r, k):
                pool.wait_ge(index_in.sem, index_in.after(t))
                pool.wait_ge(summed.sem, summed.after(t - ES))
                own_instruction(pool)
                for tile, where in ((msg[:, k, 0:P], slot_g),) + (((back_msg[:, k, :], slot_h),) if back else ()):
                    pool.indirect_dma_start(out=tile, out_offset=None, in_=table,
                                            in_offset=bass.IndirectOffsetOnAxis(ap=where[:, k:k + 1], axis=0))\
                        .then_inc(gathered[k].sem, 16)

            def scatter(t, r, k):
                pool.wait_ge(kept.sem, kept.after(t))
                pool.wait_ge(scatter_in.sem, scatter_in.after(t))
                own_instruction(pool)
                pool.indirect_dma_start(out=agg, in_=sums[:, k, 0:P], in_offset=None, bounds_check=NP - 1, oob_is_err=False,
                                        out_offset=bass.IndirectOffsetOnAxis(ap=slot_s[:, k:k + 1], axis=0))\
                    .then_inc(scattered[k].sem, 16)
                if back:
                    before = (k - 1) % ES
                    pool.wait_ge(ends_in.sem, ends_in.after(t))
                    pool.wait_ge(dot_in.sem, dot_in.after(t))
                    pool.wait_ge(added[before].sem, added[before].base + 16 * (r + (k > 0)))
                    own_instruction(pool)
                    pool.indirect_dma_start(out=agg_back, in_=back_sums[:, k, :], in_offset=None, compute_op=ALU.add,
                                            out_offset=bass.IndirectOffsetOnAxis(ap=slot_b[:, k:k + 1], axis=0))\
                        .then_inc(added[k].sem, 16)

            per = 32 if back else 16
            counts = slot_counts(gathered, per) + slot_counts(ids_in, per) + slot_counts(scattered)
            counts += [(s, TILES) for s in (masks, index_in, scatter_in, summed, kept)]
            ends_ = [("gpsimd", all_landed(scattered, [16 * uses(k) for k in range(ES)]))]
            if back:
                counts += slot_counts(added) + [(ends_in, TILES), (dot_in, TILES)]
                ends_ += [("gpsimd", all_landed(added, [16 * uses(k) for k in range(ES)]))]
            return dict(parts=dict(sync=[(6, ids, 0)],
                                   vector=[(5, indices, 0), (2, build_masks, 3 if back else 0), (1, scatter_indices, 0)],
                                   tensor=[(0, carry_on, 0), (1, sum_tile, 0)],
                                   scalar=[(0, keep, 0)],
                                   gpsimd=[(4, gather, 0), (0, scatter, 0)]),
                        counts=counts, ends=ends_)

        def rows(a, i):
            return a[bass.ds(i * BLOCK, BLOCK), :].rearrange("(p g) f -> p g f", g=G)

        def move(eng, tile, a, i, k, load, cut, signal):
            if not cut:
                pairs = [(tile[:, k, :, :], rows(a, i))]
            else:
                top_ = TAIL if isinstance(i, int) and i == STEPS - 1 else P
                pairs = [(tile[lo:hi, k, :, :],
                          a[bass.ds(i * BLOCK + lo * G, (hi - lo) * G), :].rearrange("(p g) f -> p g f", g=G))
                         for lo, hi in ((0, CUT), (CUT, top_))]
            for t_, d_ in pairs:
                eng.dma_start(t_ if load else d_, d_ if load else t_).then_inc(signal.sem, 16)

        def half(h):
            return slice(h * HALF, h * HALF + HALF)

        def halves_of(h):
            return range(h * (G // 2), (h + 1) * (G // 2))

        def by_half(fn):
            def first_half(i, j, k):
                fn(i, j, k, (0,))

            def second_half(i, j, k):
                fn(i, j, k, (1,))
            return first_half, second_half

        def split(lead, fn):
            return [(lead, part_, 0) for part_ in by_half(fn)]

        def transposes(tile, i, k, m, ops, ring, halves=(0, 1)):
            for h in halves:
                q = (i * ops + m) * 2 + h
                to = banks[((k * ops + m) * 2 + h) % ring]
                pe.wait_ge(copied.sem, copied.after(q - ring))
                for n, g in enumerate(halves_of(h)):
                    last = nc.tensor.transpose(to[:, n * P:n * P + P], tile[:, k, g, :], ident[:, :])
                last.then_inc(turned.sem, 1)

        def copies(to, i, k, m, ops, ring, halves=(0, 1)):
            for h in halves:
                q = (i * ops + m) * 2 + h
                act.wait_ge(turned.sem, turned.after(q))
                nc.scalar.activation(to[:, half(h)], banks[((k * ops + m) * 2 + h) % ring][:, :], ACT.Copy)\
                    .then_inc(copied.sem, 1)

        def products(i, of, buffers=1, halves=(0, 1)):
            for h in halves:
                pe.wait_ge(freed.sem, freed.after(2 * (i - buffers) + h))
                for ps, terms in of:
                    for g in halves_of(h):
                        at = slice(g * P, g * P + P)
                        for n, (f, w) in enumerate(terms):
                            last = nc.tensor.matmul(ps[:, at], f[:, at], weights[:, w, :],
                                                    start=n == 0, stop=n == len(terms) - 1)
                last.then_inc(product.sem, 1)

        def dense(tables, stores, ready, x_from=None, norm_scale=None, own=(), ops=1, behind=False):
            normalise = norm_scale is not None
            per_store = 16 * sum(1 + cut for _, _, cut in stores)
            has_post = any(fn.__name__ == "post" for fn in (f for _, f, _ in own.get("vector", [])))
            src_ = node_y if has_post else in_x

            def load_tables(i, j, k):
                if ops:
                    sp.wait_ge(turned.sem, turned.after(2 * ops * (i - DS) + 2 * ops - 1))
                else:
                    sp.wait_ge(y_in.sem, y_in.after(i - DS))
                for tile, a in tables:
                    if behind and a is agg:
                        t = PER * i + PER - 1 + SLACK
                        own_instruction(sp)
                        for back_by in range(ES):
                            if isinstance(i, int):
                                u = min(t, TILES - 1) - back_by
                                if u >= 0:
                                    s_ = scattered[u % ES]
                                    sp.wait_ge(s_.sem, s_.base + 16 * (u // ES + 1))
                            else:
                                u = PER * k + PER - 1 + SLACK - back_by
                                s_ = scattered[u % ES]
                                sp.wait_ge(s_.sem, s_.base + 16 * (j * (PER * DS // ES) + u // ES + 1))
                                own_instruction(sp)
                    move(sp, tile, a, i, k, True, False, tables_in[k])

            def load_x(i, j, k):
                free = y_in if has_post else normed
                sp.wait_ge(free.sem, free.after(i - DS))
                move(sp, in_x, x_from[0], i, k, True, x_from[1], x_in[k])

            def store(i, j, k):
                sp.wait_ge(ready.sem, ready.after(i if ready is not freed else 2 * i + 1))
                for tile, a, cut in stores:
                    move(sp, tile, a, i, k, False, cut, stored[k])

            def statistics(i, j, k):
                if has_post:
                    dve.wait_ge(y_in.sem, y_in.after(i))
                else:
                    dve.wait_ge(x_in[k].sem, x_in[k].base + 16 * (1 + x_from[1]) * (j + 1))
                for g in range(G):
                    last = v.bn_stats(stats[:, k, g, :], src_[:, k, g, :])
                last.then_inc(stats_in.sem, 1)

            def aggregate(i, j, k):
                dve.wait_ge(stats_in.sem, stats_in.after(i))
                own_instruction(dve)
                for g in range(G):
                    last = v.bn_aggr(moments[:, k, g, :], stats[:, k, g, :])
                last.then_inc(moments_in.sem, 1)

            def variance(i, j, k):
                dve.wait_ge(moments_in.sem, moments_in.after(i))
                dve.wait_ge(normed.sem, normed.after(i - DS))
                v.tensor_scalar(scale[:, k, 0, :], moments[:, k, :, 1], EPS, None, ALU.add).then_inc(var_in.sem, 1)

            def invert(i, j, k):
                dve.wait_ge(root_in.sem, root_in.after(i))
                v.reciprocal(scale[:, k, 0, :], scale[:, k, 0, :]).then_inc(inverse_in.sem, 1)

            def by_degree(i, j, k):
                dve.wait_ge(inverse_in.sem, inverse_in.after(2 * i))
                v.tensor_tensor(scale[:, k, 0, :], scale[:, k, 0, :], norm_scale[:, bass.ds(i * G, G)], ALU.mult)\
                    .then_inc(inverse_in.sem, 1)

            inverse_steps = 1 if norm_scale is None or isinstance(norm_scale, int) else 2

            def shift(i, j, k):
                dve.wait_ge(inverse_in.sem, inverse_in.after(inverse_steps * (i + 1) - 1))
                v.scalar_tensor_tensor(out=scale[:, k, 1, :], in0=moments[:, k, :, 0], scalar=-1.0, in1=scale[:, k, 0, :],
                                       op0=ALU.mult, op1=ALU.mult).then_inc(scale_in.sem, 1)

            def roots(i, j, k):
                act.wait_ge(var_in.sem, var_in.after(i))
                nc.scalar.activation(scale[:, k, 0, :], scale[:, k, 0, :], ACT.Sqrt).then_inc(root_in.sem, 1)

            def normalised(i, j, k, halves):
                if 0 in halves:
                    act.wait_ge(stored[k].sem, stored[k].base + per_store * j)
                    act.wait_ge(scale_in.sem, scale_in.after(i))
                for g in halves_of(halves[0]):
                    last = nc.scalar.activation(node_h[:, k, g, :], src_[:, k, g, :], ACT.Relu,
                                                bias=scale[:, k, 1, g:g + 1], scale=scale[:, k, 0, g:g + 1])
                if 1 in halves:
                    last.then_inc(normed.sem, 1)

            parts = {n: list(p) for n, p in own.items() if n != "counts"} if own else {}
            at = next((lead for lead, fn, _ in own["vector"] if fn.__name__ == "post"), 0) if own else 0
            first = max([lead for p in parts.values() for lead, _, _ in p], default=0)
            parts["sync"] = parts.get("sync", []) + [(at - (3 if normalise else 2), store, 0)] + ([(at + 3, load_x, 0)] if x_from else []) + \
                ([(first + 1, load_tables, 0)] if tables else [])
            apart_by = 2
            if normalise:
                given = {fn.__name__: (lead, fn, links) for lead, fn, links in parts.get("vector", [])}
                order = [(at - apart_by, invert, 0), given.get("post"), (at - apart_by, by_degree, 0) if inverse_steps == 2 else None,
                         given.get("residual"), (at - apart_by, shift, 0), (at, statistics, 0), given.get("pre"),
                         (at, aggregate, 0), (at, variance, 0)]
                parts["vector"] = [p for p in order if p]
                parts["scalar"] = [(at - apart_by + 1, roots, 0)] + parts.get("scalar", []) + \
                    split(at - apart_by, normalised)
            step_uses = [1 + (STEPS - 1 - k) // DS for k in range(DS)]
            counts = [(s, per_store * step_uses[k]) for k, s in enumerate(stored)]
            if tables:
                counts += [(s, 16 * len(tables) * step_uses[k]) for k, s in enumerate(tables_in)]
            if x_from:
                counts += [(s, 16 * (1 + x_from[1]) * step_uses[k]) for k, s in enumerate(x_in)]
            if ops:
                counts += [(turned, 2 * ops * STEPS), (copied, 2 * ops * STEPS), (product, 2 * STEPS), (freed, 2 * STEPS)]
            if has_post:
                counts += [(y_in, STEPS)]
            if normalise:
                counts += [(s, STEPS) for s in (var_in, root_in, scale_in, stats_in, moments_in)]
                counts += [(inverse_in, inverse_steps * STEPS)]
            if normalise or ready is normed:
                counts += [(normed, STEPS)]
            counts += own.get("counts", []) if own else []
            return dict(parts=parts, counts=counts,
                        ends=[("sync", all_landed(stored, [per_store * n for n in step_uses]))])

        def tables_ready(eng, n, j, k):
            eng.wait_ge(tables_in[k].sem, tables_in[k].base + 16 * n * (j + 1))

        def y_free(per_store, j, k):
            dve.wait_ge(stored[k].sem, stored[k].base + per_store * j)

        def add_stream(cut, relu):
            def residual(i, j, k):
                dve.wait_ge(x_in[k].sem, x_in[k].base + 16 * (1 + cut) * (j + 1))
                dve.wait_ge(freed.sem, freed.after(2 * i + 1))
                if relu:
                    last = v.scalar_tensor_tensor(out=node_y[:, k], in0=node_y[:, k], scalar=0.0, in1=in_x[:, k],
                                                  op0=ALU.max, op1=ALU.add)
                else:
                    last = v.tensor_tensor(node_y[:, k], node_y[:, k], in_x[:, k], ALU.add)
                last.then_inc(y_in.sem, 1)
            return residual

        def written(i, j, k):
            dve.wait_ge(freed.sem, freed.after(2 * i + 1))
            v.sem_inc(y_in.sem, 1)

        def conv(w, b, cut_x):
            per_store = 32 if cut_x else 16

            def pre(i, j, k):
                tables_ready(dve, 2, j, k)
                v.tensor_tensor(in_a[:, k], in_a[:, k], in_b[:, k], ALU.add).then_inc(pre_done.sem, 1)

            def turn(i, j, k, halves):
                pe.wait_ge(pre_done.sem, pre_done.after(i))
                transposes(in_a, i, k, 0, 1, 2, halves)

            def evacuate(i, j, k, halves):
                act.wait_ge(product.sem, product.after(2 * (i - 2) + 1))
                copies(feat[k % 2], i, k, 0, 1, 2, halves)

            def multiply(i, j, k, halves):
                pe.wait_ge(copied.sem, copied.after(2 * i + halves[0]))
                products(i, [(wide[1 + k % 2], [(feat[k % 2], w)])], buffers=2, halves=halves)

            def post(i, j, k):
                y_free(per_store, j, k)
                for h in range(2):
                    dve.wait_ge(product.sem, product.after(2 * i + h))
                    for g in halves_of(h):
                        last = v.scalar_tensor_tensor(out=node_y[:, k, g, :], in0=wide[1 + k % 2][:, g * P:g * P + P],
                                                      scalar=dinv[:, bass.ds(i * G + g, 1)], in1=bias[:, b, :],
                                                      op0=ALU.mult, op1=ALU.add)
                    last.then_inc(freed.sem, 1)

            def activated(i, j, k):
                act.wait_ge(freed.sem, freed.after(2 * i + 1))
                act.wait_ge(stored[k].sem, stored[k].base + per_store * j)
                for g in range(G):
                    last = nc.scalar.activation(node_h[:, k, g, :], node_y[:, k, g, :], ACT.Relu,
                                                scale=dinv[:, bass.ds(i * G + g, 1)])
                last.then_inc(normed.sem, 1)
            own = dict(vector=[(-1, post, 0), (3, pre, 0), (-1, add_stream(1, True) if cut_x else written, 0)], tensor=split(0, multiply) + split(2, turn),
                       scalar=split(1, evacuate) + ([] if cut_x else [(-2, activated, 0)]),
                       counts=[(pre_done, STEPS)])
            return own

        def mean_of_both():
            def turn(i, j, k):
                tables_ready(pe, 3, j, k)
                for m, tile in enumerate((in_a, in_c, in_b)):
                    transposes(tile, i, k, m, 3, 4)

            def evacuate(i, j, k):
                act.wait_ge(product.sem, product.after(2 * (i - 2) + 1))
                for m in range(3):
                    copies(feat[3 * (k % 2) + m], i, k, m, 3, 4)

            def multiply(i, j, k):
                f = feat[3 * (k % 2):3 * (k % 2) + 3]
                pe.wait_ge(copied.sem, copied.after(6 * i + 5))
                products(i, [(wide[2], [(f[0], W_M1), (f[1], W_M2)]), (wide[3], [(f[2], W_M0)])])

            def own_part(i, j, k):
                act.wait_ge(stored[k].sem, stored[k].base + 32 * j)
                for h in range(2):
                    act.wait_ge(product.sem, product.after(2 * i + h))
                    nc.scalar.activation(node_h[:, k].rearrange("p g f -> p (g f)")[:, half(h)], wide[3][:, half(h)],
                                         ACT.Copy).then_inc(own_in.sem, 1)

            def post(i, j, k):
                y_free(32, j, k)
                for h in range(2):
                    dve.wait_ge(own_in.sem, own_in.after(2 * i + h))
                    for g in halves_of(h):
                        last = v.scalar_tensor_tensor(out=node_y[:, k, g, :], in0=wide[2][:, g * P:g * P + P],
                                                      scalar=rcount[:, bass.ds(i * G + g, 1)], in1=node_h[:, k, g, :],
                                                      op0=ALU.mult, op1=ALU.add)
                    last.then_inc(freed.sem, 1)
            return dict(vector=[(-1, post, 0), (-1, add_stream(0, True), 0)], tensor=[(1, turn, 0), (0, multiply, 0)],
                        scalar=[(-1, own_part, 0), (1, evacuate, 0)], counts=[(own_in, 2 * STEPS)])

        def isomorphism(l, last_layer):
            per_store = 32 if last_layer else 16

            def pre(i, j, k):
                tables_ready(dve, 2, j, k)
                v.scalar_tensor_tensor(out=in_a[:, k], in0=in_b[:, k], scalar=gin_scale[:, l:l + 1], in1=in_a[:, k],
                                       op0=ALU.mult, op1=ALU.add).then_inc(pre_done.sem, 1)

            def turn(i, j, k, halves):
                pe.wait_ge(pre_done.sem, pre_done.after(i))
                transposes(in_a, i, k, 0, 1, 2, halves)

            def hidden(i, j, k, halves):
                for h in halves:
                    pe.wait_ge(copied.sem, copied.after(2 * i + h))
                    pe.wait_ge(relued.sem, relued.after(2 * i + h - 2))
                    nc.tensor.matmul(banks[2 + h][:, :], weights[:, W_G1 + l, :], feat[k % 2][:, half(h)],
                                     start=True, stop=True).then_inc(mixed.sem, 1)

            def evacuate(i, j, k, halves):
                act.wait_ge(mixed.sem, mixed.after(2 * (i - 2) + 1))
                copies(feat[k % 2], i, k, 0, 1, 2, halves)

            def hidden_relu(i, j, k, halves):
                act.wait_ge(product.sem, product.after(2 * (i - 2) + 1))
                for h in halves:
                    act.wait_ge(mixed.sem, mixed.after(2 * i + h))
                    nc.scalar.activation(feat[2 + k % 2][:, half(h)], banks[2 + h][:, :], ACT.Relu,
                                         bias=gin_bias[:, l:l + 1]).then_inc(relued.sem, 1)

            def multiply(i, j, k, halves):
                pe.wait_ge(relued.sem, relued.after(2 * i + halves[0]))
                products(i, [(wide[2], [(feat[2 + k % 2], W_G2 + l)])], halves=halves)

            def post(i, j, k):
                y_free(per_store, j, k)
                for h in range(2):
                    dve.wait_ge(product.sem, product.after(2 * i + h))
                    v.tensor_tensor(node_y[:, k, h * (G // 2):(h + 1) * (G // 2), :],
                                    wide[2][:, half(h)].rearrange("p (g f) -> p g f", f=P),
                                    bias[:, 2 + l:3 + l, :].to_broadcast([P, G // 2, P]), ALU.add).then_inc(freed.sem, 1)
            return dict(vector=[(-2, post, 0), (4, pre, 0), (-2, add_stream(0, False) if last_layer else written, 0)], tensor=split(-1, multiply) + split(1, hidden) + split(3, turn),
                        scalar=split(0, hidden_relu) + split(2, evacuate),
                        counts=[(pre_done, STEPS), (mixed, 2 * STEPS), (relued, 2 * STEPS)])

        def leaky_out():
            def pre(i, j, k):
                tables_ready(dve, 1, j, k)
                v.scalar_tensor_tensor(out=in_a[:, k], in0=in_a[:, k], scalar=SLOPE, in1=in_a[:, k], op0=ALU.mult,
                                       op1=ALU.max).then_inc(pre_done.sem, 1)

            def post(i, j, k):
                y_free(32, j, k)
                dve.wait_ge(x_in[k].sem, x_in[k].base + 16 * (j + 1))
                dve.wait_ge(pre_done.sem, pre_done.after(i))
                v.tensor_tensor(node_y[:, k], in_a[:, k], in_x[:, k], ALU.add).then_inc(y_in.sem, 1)
            return dict(vector=[(0, post, 0), (1, pre, 0)], counts=[(pre_done, STEPS)])

        ends = tile_view(in_a, 2)
        kind = tile_view(in_b, 2)
        c_tile = tile_view(in_c, 1)
        spread = tile_view(in_x, 1)
        apart = tile_view(node_y, 1)
        type_ids = tile_view(node_h, 1)
        dst_msg = norm

        def score_edges(table):
            def ids(t, r, k):
                sp.wait_ge(masks.sem, masks.after(t - ES))
                sp.dma_start(row_ids[:, k, :], row_of("dst", t)).then_inc(ids_in[k].sem, 16)
                sp.dma_start(type_ids[:, k, :], row_of("type", t)).then_inc(ids_in[k].sem, 16)

            def gather(t, r, k):
                pool.wait_ge(index_in.sem, index_in.after(t))
                pool.wait_ge(ends_in.sem, ends_in.after(t - ES))
                own_instruction(pool)
                for tile, where in ((msg, slot_g), (dst_msg, slot_h)):
                    pool.indirect_dma_start(out=tile[:, k, 0:P], out_offset=None, in_=table,
                                            in_offset=bass.IndirectOffsetOnAxis(ap=where[:, k:k + 1], axis=0))\
                        .then_inc(gathered[k].sem, 16)

            def turn(t, r, k):
                pe.wait_ge(gathered[k].sem, gathered[k].base + 32 * (r + 1))
                pe.wait_ge(top_in.sem, top_in.after(t - ES))
                nc.tensor.transpose(banks[k][:, 0:P], msg[:, k, 0:P], ident[:, :])
                nc.tensor.transpose(banks[k][:, P:2 * P], dst_msg[:, k, :], ident[:, :]).then_inc(turned.sem, 1)

            def edge_rows(t, r, k):
                pe.wait_ge(masks.sem, masks.after(t))
                pe.wait_ge(ends_in.sem, ends_in.after(t))
                c_ps = banks[k][:, 2 * P:3 * P]
                nc.tensor.matmul(c_ps, kind[:, 2 * k, :], rel_rows[:, 0, :], start=True, stop=False)
                nc.tensor.matmul(c_ps, kind[:, 2 * k + 1, :], rel_rows[:, 1, :], start=False, stop=False)
                nc.tensor.matmul(c_ps, ends[:, 2 * k, :], weights[:, W_RS, :], start=False, stop=False)
                nc.tensor.matmul(c_ps, ends[:, 2 * k + 1, :], weights[:, W_RD, :], start=False, stop=True)\
                    .then_inc(c_in.sem, 1)

            def broadcast(t, r, k):
                pe.wait_ge(spread_in.sem, spread_in.after(t))
                nc.tensor.matmul(banks[k][:, 3 * P:4 * P], ones[:, :], spread[:, k, :], start=True, stop=True)\
                    .then_inc(summed.sem, 1)

            def ends_out(t, r, k):
                act.wait_ge(turned.sem, turned.after(t))
                nc.scalar.activation(ends[:, 2 * k:2 * k + 2, :].rearrange("p k f -> p (k f)"),
                                     banks[k][:, 0:2 * P], ACT.Copy).then_inc(ends_in.sem, 1)

            def c_out(t, r, k):
                act.wait_ge(c_in.sem, c_in.after(t))
                act.wait_ge(c_stored[k].sem, c_stored[k].base + 16 * r)
                act.wait_ge(spread_in.sem, spread_in.after(t - ES))
                nc.scalar.activation(c_tile[:, k, :], banks[k][:, 2 * P:3 * P], ACT.Copy).then_inc(kept.sem, 1)

            def c_away(t, r, k):
                act.wait_ge(kept.sem, kept.after(t))
                act.dma_start(c_rows[bass.ds(t * P, P), :], c_tile[:, k, :]).then_inc(c_stored[k].sem, 16)

            indices = grouped_indices(((slot_g, 0), (slot_h, 1)), gathered, 32, index_in)

            def build_masks(t, r, k):
                dve.wait_ge(ids_in[k].sem, ids_in[k].base + 32 * (r + 1))
                dve.wait_ge(c_in.sem, c_in.after(t - ES))
                dve.wait_ge(top_in.sem, top_in.after(t - ES))
                v.tensor_scalar(kind[:, 2 * k, :], type_ids[:, k, :], part[:, 0:1], None, ALU.is_equal)
                v.tensor_scalar(kind[:, 2 * k + 1, :], type_ids[:, k, :], part[:, 1:2], None, ALU.is_equal)
                v.tensor_scalar(apart[:, k, :], row_ids[:, k, :], col[:, D_, bass.ds(t, 1)], -BIG,
                                ALU.not_equal, ALU.mult).then_inc(masks.sem, 1)

            def dot(t, r, k):
                dve.wait_ge(kept.sem, kept.after(t))
                own_instruction(dve)
                v.tensor_tensor_reduce(out=from_last[:, k, :], in0=c_tile[:, k, :], in1=bias[:, 6, :], scale=1.0,
                                       scalar=0.0, op0=ALU.mult, op1=ALU.add, accum_out=small[:, k, 0:1])\
                    .then_inc(dot_in.sem, 1)

            def leaky(t, r, k):
                dve.wait_ge(dot_in.sem, dot_in.after(2 * t))
                v.scalar_tensor_tensor(out=score[:, bass.ds(t, 1)], in0=small[:, k, 0:1], scalar=SLOPE,
                                       in1=small[:, k, 0:1], op0=ALU.mult, op1=ALU.max).then_inc(dot_in.sem, 1)

            def diagonal(t, r, k):
                dve.wait_ge(dot_in.sem, dot_in.after(2 * t + 1))
                dve.wait_ge(summed.sem, summed.after(t - ES))
                v.tensor_scalar(spread[:, k, :], ident[:, :], score[:, bass.ds(t, 1)], None, ALU.mult).then_inc(spread_in.sem, 1)

            def top_of(t, r, k):
                dve.wait_ge(summed.sem, summed.after(t))
                own_instruction(dve)
                v.tensor_tensor_reduce(out=from_last[:, k, :], in0=banks[k][:, 3 * P:4 * P], in1=apart[:, k, :],
                                       scale=1.0, scalar=-3.0 * BIG, op0=ALU.add, op1=ALU.max,
                                       accum_out=small[:, k, 2:3]).then_inc(maximum_in.sem, 1)

            def keep_top(t, r, k):
                dve.wait_ge(maximum_in.sem, maximum_in.after(t))
                own_instruction(dve)
                v.tensor_copy(top[:, 0, bass.ds(t, 1)], small[:, k, 2:3])
                v.tensor_copy(top[:, 1, bass.ds(TILES - 1 - t, 1)], small[:, k, 2:3]).then_inc(top_in.sem, 1)

            return dict(parts=dict(sync=[(6, ids, 0)], gpsimd=[(6, gather, 0)],
                                   tensor=[(3, turn, 0), (2, edge_rows, 0), (0, broadcast, 0)],
                                   scalar=[(3, ends_out, 0), (2, c_out, 0), (1, c_away, 0)],
                                   vector=[(7, indices, 0), (1, dot, 0), (4, build_masks, 0), (1, leaky, 0), (-1, top_of, 0),
                                           (1, diagonal, 0), (-1, keep_top, 0)]),
                        counts=slot_counts(gathered, 32) + slot_counts(ids_in, 32) + slot_counts(c_stored) +
                        [(s, TILES) for s in (masks, index_in, ends_in, top_in, turned, c_in, spread_in, summed, kept, maximum_in)] +
                        [(dot_in, 2 * TILES)],
                        ends=[("scalar", all_landed(c_stored, [16 * uses(k) for k in range(ES)]))])

        def join_tops():
            with nc.Block() as block:
                @block.tensor
                def _(pe):
                    for at, pick, what in ((0, pick_last, top[:, 0, :]), (1, pick_first, top[:, 1, :]),
                                           (2, pick_last, col[:, D_, 0:TILES]), (3, pick_first, dst_flip[:, :])):
                        last = nc.tensor.matmul(banks[at][:, 0:TILES], pick[:, :], what, start=True, stop=True)
                    last.then_inc(turned.sem, 1)

                @block.vector
                def _(dve):
                    def link(ins):
                        chain.link(dve, ins)
                    dve.wait_ge(turned.sem, turned.after(0))
                    for w in range(2):
                        v.tensor_copy(edges[:, w, :], banks[w][:, 0:TILES])
                        link(v.tensor_copy(d_last[:, w, :], banks[2 + w][:, 0:TILES]))
                    for w, d in ((0, col[:, D_, 0:TILES]), (1, dst_flip[:, :])):
                        v.memset(pen[:, w, 0:1], 0.0)
                        v.memset(pen[:, 2 + w, 0:1], 0.0)
                        v.memset(carry[:, w, 0:1], -2.0 * BIG)
                        link(v.tensor_tensor(pen[:, w, 1:TILES], d_last[:, w, 1:TILES], d_last[:, w, 0:TILES - 1],
                                             ALU.is_equal))
                        link(v.tensor_tensor(pen[:, 2 + w, 1:TILES], d[:, 1:TILES], d_last[:, w, 0:TILES - 1],
                                             ALU.is_equal))
                    link(v.tensor_scalar(pen[:, :, :], pen[:, :, :], -1.0, BIG, ALU.add, ALU.mult))
                    for w in range(2):
                        link(v.tensor_tensor_scan(carry[:, w, 1:TILES + 1], pen[:, w, :], edges[:, w, :], -2.0 * BIG,
                                                  ALU.add, ALU.max))
                        link(v.tensor_tensor(seg_top[:, w, :], carry[:, w, 0:TILES], pen[:, 2 + w, :], ALU.add))
                        link(v.tensor_tensor(seg_top[:, w, :], seg_top[:, w, :], top[:, w, :], ALU.max))
                    chain.settle()
            turned.base += 1

        def attend():
            W = P + 1

            def ids(t, r, k):
                sp.wait_ge(masks.sem, masks.after(t - ES))
                sp.dma_start(row_ids[:, k, :], row_of("dst", t)).then_inc(ids_in[k].sem, 16)
                sp.wait_ge(spread_in.sem, spread_in.after(t - ES))
                sp.dma_start(c_tile[:, k, :], c_rows[bass.ds(t * P, P), :]).then_inc(c_loaded[k].sem, 16)

            def below_top(t, r, k):
                dve.wait_ge(ex_in.sem, ex_in.after(t - ES))
                own_instruction(dve)
                v.scalar_tensor_tensor(out=small[:, k, 0:1], in0=seg_top[:, 1, bass.ds(TILES - 1 - t, 1)],
                                       scalar=seg_top[:, 0, bass.ds(t, 1)], in1=score[:, bass.ds(t, 1)],
                                       op0=ALU.max, op1=ALU.subtract).then_inc(index_in.sem, 1)

            def build_masks(t, r, k):
                dve.wait_ge(ids_in[k].sem, ids_in[k].base + 16 * (r + 1))
                dve.wait_ge(summed.sem, summed.after(t - ES))
                v.tensor_scalar(same[:, k, :], row_ids[:, k, :], col[:, D_, bass.ds(t, 1)], None, ALU.is_equal)
                v.tensor_scalar(from_last[:, k, :], row_ids[:, k, :], prev_last[:, bass.ds(t, 1)], None,
                                ALU.is_equal).then_inc(masks.sem, 1)

            def weigh(t, r, k):
                dve.wait_ge(ex_in.sem, ex_in.after(t))
                dve.wait_ge(c_loaded[k].sem, c_loaded[k].base + 16 * (r + 1))
                v.tensor_scalar(msg[:, k, 0:P], c_tile[:, k, :], msg[:, k, P:W], None, ALU.mult).then_inc(spread_in.sem, 1)

            def clamp(t, r, k):
                dve.wait_ge(kept.sem, kept.after(t))
                v.tensor_scalar(small[:, k, 3:4], sums[:, k, P:W], 1.0 / BIG, None, ALU.max).then_inc(dot_in.sem, 1)

            def invert(t, r, k):
                dve.wait_ge(dot_in.sem, dot_in.after(2 * t))
                v.reciprocal(small[:, k, 4:5], small[:, k, 3:4]).then_inc(dot_in.sem, 1)

            def normalise(t, r, k):
                dve.wait_ge(scattered[k].sem, scattered[k].base + 16 * r)
                dve.wait_ge(dot_in.sem, dot_in.after(2 * t + 1))
                v.tensor_scalar(norm[:, k, :], sums[:, k, 0:P], small[:, k, 4:5], None, ALU.mult)\
                    .then_inc(norm_in.sem, 1)

            scatter_indices = grouped_indices(((slot_s, 2),), scattered, 16, scatter_in)

            def sum_tile(t, r, k):
                pe.wait_ge(masks.sem, masks.after(t))
                pe.wait_ge(spread_in.sem, spread_in.after(t))
                nc.tensor.matmul(banks[k][:, 0:W], same[:, k, :], msg[:, k, 0:W], start=True, stop=False)

            def carry_on(t, r, k):
                pe.wait_ge(kept.sem, kept.after(t - 1))
                nc.tensor.matmul(banks[k][:, 0:W], from_last[:, k, :], sums[:, (k - 1) % ES, 0:W],
                                 start=False, stop=True).then_inc(summed.sem, 1)

            def exp_of(t, r, k):
                act.wait_ge(index_in.sem, index_in.after(t))
                act.wait_ge(summed.sem, summed.after(t - ES))
                nc.scalar.activation(msg[:, k, P:W], small[:, k, 0:1], ACT.Exp, scale=-1.0).then_inc(ex_in.sem, 1)

            def keep(t, r, k):
                act.wait_ge(norm_in.sem, norm_in.after(t - ES))
                act.wait_ge(summed.sem, summed.after(t))
                nc.scalar.activation(sums[:, k, 0:W], banks[k][:, 0:W], ACT.Copy).then_inc(kept.sem, 1)

            def scatter(t, r, k):
                pool.wait_ge(scatter_in.sem, scatter_in.after(t))
                pool.wait_ge(norm_in.sem, norm_in.after(t))
                own_instruction(pool)
                pool.indirect_dma_start(out=agg, in_=norm[:, k, :], in_offset=None, bounds_check=NP - 1, oob_is_err=False,
                                        out_offset=bass.IndirectOffsetOnAxis(ap=slot_s[:, k:k + 1], axis=0))\
                    .then_inc(scattered[k].sem, 16)
            return dict(parts=dict(sync=[(6, ids, 0)], vector=[(-1, clamp, 0), (5, below_top, 0), (3, weigh, 0), (-1, invert, 0),
                                           (3, build_masks, 0), (0, scatter_indices, 0), (-1, normalise, 0)],
                                   tensor=[(0, carry_on, 0), (1, sum_tile, 0)],
                                   scalar=[(0, keep, 0), (4, exp_of, 0)], gpsimd=[(-1, scatter, 0)]),
                        counts=slot_counts(scattered) + slot_counts(ids_in) + slot_counts(c_loaded) +
                        [(s, TILES) for s in (masks, index_in, scatter_in, summed, kept, spread_in, ex_in, norm_in)] + [(dot_in, 2 * TILES)],
                        ends=[("gpsimd", all_landed(scattered, [16 * uses(k) for k in range(ES)]))])

        how_many_late = nc.values_load(late_i[0:1, 0:1], min_val=0, max_val=LATER)

        def pair(edge, nodes):
            before = [s.base for s in signals]
            with nc.If(how_many_late > 0):
                run_stages(edge)
                run_stages(None, nodes(False))
            after = [s.base for s in signals]
            for s, base in zip(signals, before):
                s.base = base
            with nc.Else():
                run_stages(edge, nodes(True))
            assert after == [s.base for s in signals]

        start = dense([], [(node_h, table_a, 0)], normed, (x, 1), dinv, {}, ops=0)
        zeros = in_c[:, 0]

        def prepare_zeros(pool):
            pool.memset(zeros[:, :, :], 0.0)
            pool.wait_ge(zeroed.sem, zeroed.base + 16 * len(zero_parts(agg, NP)))

        def zero_back(i, j, k):
            sp.dma_start(rows(agg_back, i), zeros).then_inc(zeroed_back.sem, 16)

        def zero_dumps(eng):
            eng.dma_start(agg_back[NP:NP + P, :], zeros[:, 0, :]).then_inc(zeroed_back.sem, 16)
            eng.wait_ge(zeroed_back.sem, 16 * (STEPS + 1))

        def first_conv(beside):
            own = conv(W_A1, 0, False)
            own["sync"] = [(0, zero_back, 0)]
            stage_ = dense([(in_a, agg), (in_b, table_a)], [(node_h, table_b, 0)], normed, own=own, behind=beside)
            stage_["ends"].append(("sync", zero_dumps))
            return stage_

        def second_conv(beside):
            return dense([(in_a, agg), (in_b, table_b)], [(node_y, xs, 0), (node_h, table_a, 0)], normed, (x, 1), 1,
                         conv(W_A2, 1, True), behind=beside)
        start["ends"].append(("gpsimd", prepare_zeros))
        run_stages(None, start)
        pair(sum_edges(table_a), first_conv)
        pair(sum_edges(table_b), second_conv)

        run_stages(sum_edges(table_a, back=True))
        run_stages(None, dense([(in_a, agg), (in_c, agg_back), (in_b, table_a)],
                               [(node_y, xs, 0), (node_h, table_b, 0)], normed, (xs, 0), 1, mean_of_both(), ops=3))

        def inner(l, old, new):
            return lambda beside: dense([(in_a, agg), (in_b, old)], [(node_y, new, 0)], y_in, own=isomorphism(l, False),
                                        behind=beside)

        def last_isomorphism(beside):
            return dense([(in_a, agg), (in_b, table_b)], [(node_y, xs, 0), (node_h, table_a, 0)], normed, (xs, 0), 1,
                         isomorphism(2, True), behind=beside)
        pair(sum_edges(table_b), inner(0, table_b, table_a))
        pair(sum_edges(table_a), inner(1, table_a, table_b))
        pair(sum_edges(table_b), last_isomorphism)

        def output(beside):
            return dense([(in_a, agg)], [(node_y, out, 1)], y_in, (xs, 0), None, leaky_out(), ops=0, behind=beside)
        run_stages(score_edges(table_a))
        join_tops()
        pair(attend(), output)


_INS = ["x", "src", "dst", "edge_type_200", "L0_gnn_W1", "L0_gnn_b1", "L0_gnn_W2", "L0_gnn_b2", "L1_gnn_W0",
        "L1_gnn_W1", "L1_gnn_W2", "L2_gnn_eps", "L2_gnn_W1", "L2_gnn_b1", "L2_gnn_W2", "L2_gnn_b2",
        "L3_gnn_relation_embedding", "L3_gnn_W1", "L3_gnn_b1", "L3_gnn_w2"]


def kernel(**inputs):
    import numpy as _np
    import concourse.bacc as _bacc
    from concourse import mybir as _mybir
    from concourse.bass_utils import run_bass_kernel_spmd as _run

    nc = _bacc.Bacc("TRN2", target_bir_lowering=False, num_devices=1)
    arrays, args = {}, []
    for name in _INS:
        a = _np.ascontiguousarray(inputs[name])
        arrays[f"in_{name}"] = a
        args.append(nc.dram_tensor(f"in_{name}", a.shape, _mybir.dt.from_np(a.dtype), kind="ExternalInput").ap())
    args.append(nc.dram_tensor("out_0", (N, P), _mybir.dt.float32, kind="ExternalOutput").ap())
    gnn_kernel(nc, *args)
    r = _run(nc, [arrays], core_ids=[0])
    return r.results[0]["out_0"]
```
